# Optimizing a Trainium2 kernel written in Bass

```python
import numpy as np
import jax
import jax.numpy as jnp

def _softmax(x, axis=-1):
    return jax.nn.softmax(x, axis=axis)

def _gelu(x):
    return jax.nn.gelu(x, approximate=True)

def _silu(x):
    return jax.nn.silu(x)

def _sigmoid(x):
    return jax.nn.sigmoid(x)

def _layernorm(x, axis=-1, eps=1e-05):
    m = jnp.mean(x, axis=axis, keepdims=True)
    v = jnp.var(x, axis=axis, keepdims=True)
    return (x - m) / jnp.sqrt(v + eps)

def _scatter_add(tgt, idx, src, axis=0):
    return tgt.at[idx].add(src)

def _segment_sum(src, seg, n):
    return jax.ops.segment_sum(src, seg, n)
kernel_name = 'mk_gnn_preln_d4_gnn_r8_093fca'

def setup_inputs(seed: int=0):
    np.random.seed(seed)
    _w = jnp.asarray

    def _rec_inputs():
        import jax
        import jax.numpy as jnp
        _gk = jax.random.key(seed)
        x = -0.0003713 + 1 * jax.random.normal(jax.random.fold_in(_gk, 1), (6250, 128), jnp.float32)
        src = jax.random.randint(jax.random.fold_in(_gk, 2), (100000,), 0, 6250, jnp.int32)
        dst = jnp.minimum((6250 * jax.random.uniform(jax.random.fold_in(_gk, 3), (100000,)) ** 2.0).astype(jnp.int32), 49999)
        _o = jnp.argsort(dst, stable=True)
        src = src[_o]
        dst = dst[_o]
        edge_attr_128 = -8.513e-05 + 0.999844 * jax.random.normal(jax.random.fold_in(_gk, 12), (100000, 128), jnp.float32)
        edge_type_8 = jax.random.randint(jax.random.fold_in(_gk, 14), (100000,), 0, 8, jnp.int32)
        return (x, src, dst, edge_attr_128, edge_type_8)
    x, src, dst, edge_attr_128, edge_type_8 = _rec_inputs()

    def _L0_gnn_setup():
        import jax, jax.numpy as jnp
        import numpy as np
        N_NODES = 12500
        N_EDGES = 80000
        D_IN = 128
        D_OUT = 128
        key = jax.random.key(seed)
        k1, k2, k3, k4, k5, k6 = jax.random.split(key, 6)
        nfeat = jax.random.normal(k1, (N_NODES, D_IN), dtype=jnp.float32)
        efeat = jax.random.normal(k2, (N_EDGES, D_IN), dtype=jnp.float32)
        src = jax.random.randint(k3, (N_EDGES,), 0, N_NODES, dtype=jnp.int64)
        dst = jax.random.randint(k4, (N_EDGES,), 0, N_NODES, dtype=jnp.int64)
        W = jax.random.normal(k5, (D_IN, D_OUT), dtype=jnp.float32) * (1.0 / np.sqrt(D_IN))
        b = jnp.zeros((D_OUT,), dtype=jnp.float32)
        We = jax.random.normal(k6, (D_IN, D_OUT), dtype=jnp.float32) * (1.0 / np.sqrt(D_IN))
        be = jnp.zeros((D_OUT,), dtype=jnp.float32)
        return {'nfeat': nfeat, 'efeat': efeat, 'src': src, 'dst': dst, 'W': W, 'b': b, 'We': We, 'be': be}
    _L0_gnn_all = _L0_gnn_setup()
    _L0_gnn_in = {k: v for k, v in _L0_gnn_all.items() if k in ('W', 'b', 'We', 'be')}
    del _L0_gnn_all

    def _L1_gnn_setup():
        import jax, jax.numpy as jnp
        import numpy as np
        N, D, H, F = (6250, 128, 8, 512)
        HD = D // H
        EPS_BN = 1e-05

        def _batchnorm(x, gamma, beta):
            m = x.mean(axis=0)
            v = x.var(axis=0)
            return (x - m) * jax.lax.rsqrt(v + EPS_BN) * gamma + beta
        key = jax.random.key(seed)
        ks = jax.random.split(key, 12)
        s = 0.05
        return {'src': jax.random.normal(ks[0], (N, D), jnp.float32), 'edge_index': jax.random.randint(ks[1], (2, 100000), 0, N, jnp.int64), 'q_w': jax.random.normal(ks[2], (D, D), jnp.float32) * s, 'q_b': jnp.zeros((D,), jnp.float32), 'k_w': jax.random.normal(ks[3], (D, D), jnp.float32) * s, 'v_w': jax.random.normal(ks[4], (D, D), jnp.float32) * s, 'out_w': jax.random.normal(ks[5], (D, D), jnp.float32) * s, 'out_b': jnp.zeros((D,), jnp.float32), 'g1': jnp.ones((D,), jnp.float32), 'b1': jnp.zeros((D,), jnp.float32), 'lin1_w': jax.random.normal(ks[6], (F, D), jnp.float32) * s, 'lin1_b': jnp.zeros((F,), jnp.float32), 'lin2_w': jax.random.normal(ks[7], (D, F), jnp.float32) * s, 'lin2_b': jnp.zeros((D,), jnp.float32), 'g2': jnp.ones((D,), jnp.float32), 'b2': jnp.zeros((D,), jnp.float32)}
    _L1_gnn_all = _L1_gnn_setup()
    _L1_gnn_in = {k: v for k, v in _L1_gnn_all.items() if k in ('q_w', 'q_b', 'k_w', 'v_w', 'out_w', 'out_b', 'g1', 'b1', 'lin1_w', 'lin1_b', 'lin2_w', 'lin2_b', 'g2', 'b2')}
    del _L1_gnn_all

    def _L2_gnn_setup():
        import jax, jax.numpy as jnp
        import numpy as np
        NUM_RELS = 8

        def rgcn_layer(x, src, dst, etype, W, W_root, b, num_rels):
            N = x.shape[0]
            do = W.shape[-1]
            h = jnp.einsum('ni,rio->rno', x, W)
            msg = h[etype, src]
            seg = dst * num_rels + etype
            sums = jax.ops.segment_sum(msg, seg, num_segments=N * num_rels)
            cnt = jax.ops.segment_sum(jnp.ones(msg.shape[0], x.dtype), seg, num_segments=N * num_rels)
            mean = sums / jnp.maximum(cnt, 1.0)[:, None]
            agg = mean.reshape(N, num_rels, do).sum(axis=1)
            return agg + x @ W_root + b
        key = jax.random.key(seed)
        ks = jax.random.split(key, 10)
        N, E = (6250, 75000)
        di, dh, do, R = (128, 256, 128, NUM_RELS)
        x = jax.random.normal(ks[0], (N, di), dtype=jnp.float32)
        edge_index = jax.random.randint(ks[1], (2, E), 0, N, dtype=jnp.int64)
        edge_type = jax.random.randint(ks[2], (E,), 0, R, dtype=jnp.int64)
        s1 = 1.0 / np.sqrt(di)
        s2 = 1.0 / np.sqrt(dh)
        W1 = jax.random.normal(ks[3], (R, di, dh), dtype=jnp.float32) * s1
        root1 = jax.random.normal(ks[4], (di, dh), dtype=jnp.float32) * s1
        b1 = jnp.zeros((dh,), jnp.float32)
        W2 = jax.random.normal(ks[5], (R, dh, do), dtype=jnp.float32) * s2
        root2 = jax.random.normal(ks[6], (dh, do), dtype=jnp.float32) * s2
        b2 = jnp.zeros((do,), jnp.float32)
        return {'x': x, 'edge_index': edge_index, 'edge_type': edge_type, 'W1': W1, 'root1': root1, 'b1': b1, 'W2': W2, 'root2': root2, 'b2': b2}
    _L2_gnn_all = _L2_gnn_setup()
    _L2_gnn_in = {k: v for k, v in _L2_gnn_all.items() if k in ('W1', 'root1', 'b1', 'W2', 'root2', 'b2')}
    del _L2_gnn_all

    def _L3_gnn_setup():
        import jax, jax.numpy as jnp
        import numpy as np
        N, F, H = (12500, 128, 2)
        DH = F // H
        E = 200000

        def transformer_conv(nodes, src, dst, Wq, bq, Wk, bk, Wv, bv, Wskip, bskip):
            n = nodes.shape[0]
            q = (nodes @ Wq + bq).reshape(n, H, DH)
            k = (nodes @ Wk + bk).reshape(n, H, DH)
            v = (nodes @ Wv + bv).reshape(n, H, DH)
            alpha = jnp.einsum('ehd,ehd->eh', q[dst], k[src]) / jnp.sqrt(jnp.float32(DH))
            amax = jax.ops.segment_max(alpha, dst, num_segments=n)
            ex = jnp.exp(alpha - amax[dst])
            denom = jax.ops.segment_sum(ex, dst, num_segments=n)
            w = ex / denom[dst]
            msg = v[src] * w[:, :, None]
            agg = jax.ops.segment_sum(msg, dst, num_segments=n).reshape(n, F)
            return agg + nodes @ Wskip + bskip
        key = jax.random.key(seed)
        ks = jax.random.split(key, 10)
        s = 0.05
        return {'nodes': jax.random.normal(ks[0], (N, F), jnp.float32), 'edge_index': jax.random.randint(ks[1], (2, E), 0, N, jnp.int64), 'Wq': jax.random.normal(ks[2], (F, F), jnp.float32) * s, 'bq': jnp.zeros((F,), jnp.float32), 'Wk': jax.random.normal(ks[3], (F, F), jnp.float32) * s, 'bk': jnp.zeros((F,), jnp.float32), 'Wv': jax.random.normal(ks[4], (F, F), jnp.float32) * s, 'bv': jnp.zeros((F,), jnp.float32), 'Wskip': jax.random.normal(ks[5], (F, F), jnp.float32) * s, 'bskip': jnp.zeros((F,), jnp.float32), 'Wgate': jax.random.normal(ks[6], (2 * F, F), jnp.float32) * s, 'Wfuse': jax.random.normal(ks[7], (F, F), jnp.float32) * s}
    _L3_gnn_all = _L3_gnn_setup()
    _L3_gnn_in = {k: v for k, v in _L3_gnn_all.items() if k in ('Wq', 'bq', 'Wk', 'bk', 'Wv', 'bv', 'Wskip', 'bskip', 'Wgate', 'Wfuse')}
    del _L3_gnn_all
    return {'x': x, 'src': src, 'dst': dst, 'edge_attr_128': edge_attr_128, 'edge_type_8': edge_type_8, 'L0_gnn_W': _L0_gnn_in['W'], 'L0_gnn_b': _L0_gnn_in['b'], 'L0_gnn_We': _L0_gnn_in['We'], 'L0_gnn_be': _L0_gnn_in['be'], 'L1_gnn_q_w': _L1_gnn_in['q_w'], 'L1_gnn_q_b': _L1_gnn_in['q_b'], 'L1_gnn_k_w': _L1_gnn_in['k_w'], 'L1_gnn_v_w': _L1_gnn_in['v_w'], 'L1_gnn_out_w': _L1_gnn_in['out_w'], 'L1_gnn_out_b': _L1_gnn_in['out_b'], 'L1_gnn_g1': _L1_gnn_in['g1'], 'L1_gnn_b1': _L1_gnn_in['b1'], 'L1_gnn_lin1_w': _L1_gnn_in['lin1_w'], 'L1_gnn_lin1_b': _L1_gnn_in['lin1_b'], 'L1_gnn_lin2_w': _L1_gnn_in['lin2_w'], 'L1_gnn_lin2_b': _L1_gnn_in['lin2_b'], 'L1_gnn_g2': _L1_gnn_in['g2'], 'L1_gnn_b2': _L1_gnn_in['b2'], 'L2_gnn_W1': _L2_gnn_in['W1'], 'L2_gnn_root1': _L2_gnn_in['root1'], 'L2_gnn_b1': _L2_gnn_in['b1'], 'L2_gnn_W2': _L2_gnn_in['W2'], 'L2_gnn_root2': _L2_gnn_in['root2'], 'L2_gnn_b2': _L2_gnn_in['b2'], 'L3_gnn_Wq': _L3_gnn_in['Wq'], 'L3_gnn_bq': _L3_gnn_in['bq'], 'L3_gnn_Wk': _L3_gnn_in['Wk'], 'L3_gnn_bk': _L3_gnn_in['bk'], 'L3_gnn_Wv': _L3_gnn_in['Wv'], 'L3_gnn_bv': _L3_gnn_in['bv'], 'L3_gnn_Wskip': _L3_gnn_in['Wskip'], 'L3_gnn_bskip': _L3_gnn_in['bskip'], 'L3_gnn_Wgate': _L3_gnn_in['Wgate'], 'L3_gnn_Wfuse': _L3_gnn_in['Wfuse']}

def reference(x, src, dst, edge_attr_128, edge_type_8, L0_gnn_W, L0_gnn_b, L0_gnn_We, L0_gnn_be, L1_gnn_q_w, L1_gnn_q_b, L1_gnn_k_w, L1_gnn_v_w, L1_gnn_out_w, L1_gnn_out_b, L1_gnn_g1, L1_gnn_b1, L1_gnn_lin1_w, L1_gnn_lin1_b, L1_gnn_lin2_w, L1_gnn_lin2_b, L1_gnn_g2, L1_gnn_b2, L2_gnn_W1, L2_gnn_root1, L2_gnn_b1, L2_gnn_W2, L2_gnn_root2, L2_gnn_b2, L3_gnn_Wq, L3_gnn_bq, L3_gnn_Wk, L3_gnn_bk, L3_gnn_Wv, L3_gnn_bv, L3_gnn_Wskip, L3_gnn_bskip, L3_gnn_Wgate, L3_gnn_Wfuse):
    import jax
    import jax.numpy as jnp

    def _L0_gnn_ref(nfeat, efeat, src, dst, W, b, We, be):
        import jax, jax.numpy as jnp
        import numpy as np
        N_NODES = 12500
        N_EDGES = 80000
        D_IN = 128
        D_OUT = 128
        N = nfeat.shape[0]
        ones_e = jnp.ones(src.shape, dtype=nfeat.dtype)
        in_deg = jax.ops.segment_sum(ones_e, dst, num_segments=N)
        out_deg = jax.ops.segment_sum(ones_e, src, num_segments=N)
        norm_src = jnp.clip(out_deg, 1.0, None) ** (-0.5)
        norm_dst = jnp.clip(in_deg, 1.0, None) ** (-0.5)
        h = nfeat * norm_src[:, None]
        agg = jax.ops.segment_sum(h[src], dst, num_segments=N)
        conv = agg @ W * norm_dst[:, None] + b
        sfeat = (nfeat @ W + b) / (in_deg + 1.0)[:, None]
        out = conv + sfeat
        e = efeat @ We + be
        esum = jax.ops.segment_sum(e, dst, num_segments=N)
        h_e = esum / jnp.clip(in_deg, 1.0, None)[:, None]
        return out + h_e

    def _L1_gnn_ref(src, edge_index, q_w, q_b, k_w, v_w, out_w, out_b, g1, b1, lin1_w, lin1_b, lin2_w, lin2_b, g2, b2):
        import jax, jax.numpy as jnp
        import numpy as np
        N, D, H, F = (6250, 128, 8, 512)
        HD = D // H
        EPS_BN = 1e-05

        def _batchnorm(x, gamma, beta):
            m = x.mean(axis=0)
            v = x.var(axis=0)
            return (x - m) * jax.lax.rsqrt(v + EPS_BN) * gamma + beta
        n = src.shape[0]
        loops = jnp.arange(n, dtype=edge_index.dtype)
        ei = jnp.concatenate([edge_index, jnp.stack([loops, loops])], axis=1)
        e_src, e_dst = (ei[0], ei[1])
        scaling = float(HD) ** (-0.5)
        q = ((src @ q_w.T + q_b) * scaling).reshape(n, H, HD)
        k = (src @ k_w.T).reshape(n, H, HD)
        v = (src @ v_w.T).reshape(n, H, HD)
        w = jnp.einsum('ehd,ehd->eh', q[e_dst], k[e_src])
        mx = jax.ops.segment_max(w, e_dst, num_segments=n)
        ex = jnp.exp(w - mx[e_dst])
        den = jax.ops.segment_sum(ex, e_dst, num_segments=n)
        attn_w = ex / (den[e_dst] + 1e-16)
        msgs = attn_w[:, :, None] * v[e_src]
        agg = jax.ops.segment_sum(msgs, e_dst, num_segments=n)
        attn_out = agg.reshape(n, D) @ out_w.T + out_b
        x = _batchnorm(src + attn_out, g1, b1)
        ff = jax.nn.leaky_relu(x @ lin1_w.T + lin1_b, negative_slope=0.01)
        ff = ff @ lin2_w.T + lin2_b
        x = _batchnorm(x + ff, g2, b2)
        return x

    def _L2_gnn_ref(x, edge_index, edge_type, W1, root1, b1, W2, root2, b2):
        import jax, jax.numpy as jnp
        import numpy as np
        NUM_RELS = 8

        def rgcn_layer(x, src, dst, etype, W, W_root, b, num_rels):
            N = x.shape[0]
            do = W.shape[-1]
            h = jnp.einsum('ni,rio->rno', x, W)
            msg = h[etype, src]
            seg = dst * num_rels + etype
            sums = jax.ops.segment_sum(msg, seg, num_segments=N * num_rels)
            cnt = jax.ops.segment_sum(jnp.ones(msg.shape[0], x.dtype), seg, num_segments=N * num_rels)
            mean = sums / jnp.maximum(cnt, 1.0)[:, None]
            agg = mean.reshape(N, num_rels, do).sum(axis=1)
            return agg + x @ W_root + b
        src, dst = (edge_index[0], edge_index[1])
        h = rgcn_layer(x, src, dst, edge_type, W1, root1, b1, NUM_RELS)
        h = jax.nn.relu(h)
        return rgcn_layer(h, src, dst, edge_type, W2, root2, b2, NUM_RELS)

    def _L3_gnn_ref(nodes, edge_index, Wq, bq, Wk, bk, Wv, bv, Wskip, bskip, Wgate, Wfuse):
        import jax, jax.numpy as jnp
        import numpy as np
        N, F, H = (12500, 128, 2)
        DH = F // H
        E = 200000

        def transformer_conv(nodes, src, dst, Wq, bq, Wk, bk, Wv, bv, Wskip, bskip):
            n = nodes.shape[0]
            q = (nodes @ Wq + bq).reshape(n, H, DH)
            k = (nodes @ Wk + bk).reshape(n, H, DH)
            v = (nodes @ Wv + bv).reshape(n, H, DH)
            alpha = jnp.einsum('ehd,ehd->eh', q[dst], k[src]) / jnp.sqrt(jnp.float32(DH))
            amax = jax.ops.segment_max(alpha, dst, num_segments=n)
            ex = jnp.exp(alpha - amax[dst])
            denom = jax.ops.segment_sum(ex, dst, num_segments=n)
            w = ex / denom[dst]
            msg = v[src] * w[:, :, None]
            agg = jax.ops.segment_sum(msg, dst, num_segments=n).reshape(n, F)
            return agg + nodes @ Wskip + bskip
        src, dst = (edge_index[0], edge_index[1])
        x = transformer_conv(nodes, src, dst, Wq, bq, Wk, bk, Wv, bv, Wskip, bskip)
        h = jnp.concatenate([nodes, x], axis=-1)
        gate = jax.nn.sigmoid(h @ Wgate)
        fuse = jnp.tanh(x @ Wfuse)
        return gate * fuse + (1.0 - gate) * nodes
    edge_index = jnp.stack([src, dst])
    h = jnp.maximum(_layernorm(x, axis=-1), 0.0)
    x = x + _L0_gnn_ref(h, edge_attr_128, src, dst, L0_gnn_W, L0_gnn_b, L0_gnn_We, L0_gnn_be)
    h = jnp.maximum(_layernorm(x, axis=-1), 0.0)
    x = x + _L1_gnn_ref(h, edge_index, L1_gnn_q_w, L1_gnn_q_b, L1_gnn_k_w, L1_gnn_v_w, L1_gnn_out_w, L1_gnn_out_b, L1_gnn_g1, L1_gnn_b1, L1_gnn_lin1_w, L1_gnn_lin1_b, L1_gnn_lin2_w, L1_gnn_lin2_b, L1_gnn_g2, L1_gnn_b2)
    h = jnp.maximum(_layernorm(x, axis=-1), 0.0)
    x = x + _L2_gnn_ref(h, edge_index, edge_type_8, L2_gnn_W1, L2_gnn_root1, L2_gnn_b1, L2_gnn_W2, L2_gnn_root2, L2_gnn_b2)
    h = jnp.maximum(_layernorm(x, axis=-1), 0.0)
    x = x + _L3_gnn_ref(h, edge_index, L3_gnn_Wq, L3_gnn_bq, L3_gnn_Wk, L3_gnn_bk, L3_gnn_Wv, L3_gnn_bv, L3_gnn_Wskip, L3_gnn_bskip, L3_gnn_Wgate, L3_gnn_Wfuse)
    return x

_drawn_inputs = setup_inputs


def setup_inputs(seed=0):
    import zlib

    import numpy as np

    out = dict(_drawn_inputs(seed))
    spreads = {'L0_gnn_b': (0.0, 0.1),
     'L0_gnn_be': (0.0, 0.1),
     'L1_gnn_q_b': (0.0, 0.8),
     'L1_gnn_out_b': (0.0, 0.8),
     'L1_gnn_g1': (1.0, 0.2),
     'L1_gnn_b1': (0.0, 0.704),
     'L1_gnn_lin1_b': (0.0, 0.389),
     'L1_gnn_lin2_b': (0.0, 0.8),
     'L1_gnn_g2': (1.0, 0.2),
     'L1_gnn_b2': (0.0, 0.1),
     'L2_gnn_b1': (0.0, 0.1),
     'L2_gnn_b2': (0.0, 0.333),
     'L3_gnn_bq': (0.0, 0.8),
     'L3_gnn_bk': (0.0, 0.8),
     'L3_gnn_bv': (0.0, 0.8),
     'L3_gnn_bskip': (0.0, 0.8)}
    factors = {'L1_gnn_q_w': 8.0, 'L1_gnn_k_w': 8.0, 'L3_gnn_Wq': 8.0, 'L3_gnn_Wk': 8.0}
    for name, (base, spread) in spreads.items():
        noise = np.random.default_rng([zlib.crc32(name.encode()), seed]).standard_normal(out[name].shape)
        drawn = base * np.exp(spread * noise) if base else spread * noise
        out[name] = jnp.asarray(drawn.astype(out[name].dtype))
    for name, factor in factors.items():
        out[name] = (out[name] * factor).astype(out[name].dtype)
    return out
```

```python
from contextlib import ExitStack

import concourse.bass as bass
from concourse import mybir

P = 128
D = 128
N = 6250
E = 100000
NW = 50
NP = NW * P
REST = N - (N // P) * P
LASTW = N // P
T = 832
TB = 7
TA = TB * P
EP, EC = 125, E // 125
RELS = 8
HID = 256
FF = 512
FAR = -1.0e30
EPS = 1e-5

F32 = mybir.dt.float32
BF16 = mybir.dt.bfloat16
I32 = mybir.dt.int32
ALU = mybir.AluOpType
ACT = mybir.ActivationFunctionType
X = mybir.AxisListType.X


class Chain:

    def __init__(self, eng, sem):
        self.eng, self.sem, self.n = eng, sem, 0

    def step(self, ins):
        ins.then_inc(self.sem, 1)
        self.n = self.n + 1
        self.eng.wait_ge(self.sem, self.n)


class Semaphores:

    def __init__(self, nc):
        self.nc, self.out = nc, []

    def __call__(self, name):
        self.out.append(self.nc.alloc_semaphore(name=name))
        return self.out[-1]

    def give_back(self):
        nc, out = self.nc, self.out
        with nc.Block() as block:
            @block.gpsimd
            def _(pool):
                nc.clear_and_free_semaphores(out)
        self.out = []


def view(tensor, offset, pattern):
    return bass.AP(tensor, offset, pattern)


class Stage:

    def __init__(self, nc, name):
        self.nc, self.name, self.ctx = nc, name, ExitStack()

    def __enter__(self):
        return self

    def __exit__(self, *a):
        self.ctx.close()

    def sb(self, name, shape, dt=F32):
        return self.ctx.enter_context(self.nc.sbuf_tensor(f"{self.name}_{name}", shape, dt))

    def ps(self, name, shape=(P, 512)):
        return self.ctx.enter_context(self.nc.psum_tensor(f"{self.name}_{name}", list(shape), F32))


def constants(nc, g, sem):
    made, dve_s = sem("const_made"), sem("const_dve")
    with nc.Block() as block:
        @block.gpsimd
        def _(pool):
            nc.gpsimd.iota(g.iota_i[:, :], [[1, P]], base=0, channel_multiplier=0).then_inc(made, 1)
            nc.gpsimd.iota(g.tile_i[:, :], [[P, TB]], base=0, channel_multiplier=1).then_inc(made, 1)
            nc.gpsimd.memset(g.ident[:, :], 0.0).then_inc(made, 1)
            pool.wait_ge(made, 3)
            nc.gpsimd.affine_select(out=g.ident[:, :], in_=g.ident[:, :], compare_op=ALU.not_equal, fill=1.0,
                                    base=0, pattern=[[-1, P]], channel_multiplier=1).then_inc(made, 1)

        @block.vector
        def _(dve):
            nc.vector.memset(g.ones[:, :], 1.0)
            dve.wait_ge(made, 2)
            nc.vector.tensor_copy(g.iota[:, :], g.iota_i[:, :])
            nc.vector.tensor_copy(g.tile_f[:, :], g.tile_i[:, :])


def tile_tables(nc, g, sem, src, dst, etype):
    with Stage(nc, "tt") as st:
        dsti = st.sb("dsti", [EP, EC], I32)
        dstf = st.sb("dstf", [EP, EC])
        junk = st.sb("junk", [EP, EC])
        below = st.sb("below", [EP, NW + 1])
        first = st.sb("first", [P, NW + 1])
        cnti = st.sb("cnti", [P, NW], I32)
        ntile = st.sb("ntile", [P, NW])
        upto = st.sb("upto", [P, NW])
        tmp = st.sb("tmp", [P, NW])
        base = st.sb("base", [P, NW])
        win = st.sb("win", [P, TB])
        start = st.sb("start", [P, TB])
        cut = st.sb("cut", [P, TB])
        off = st.sb("off", [P, TB])
        cuti = st.sb("cuti", [P, TB], I32)
        starti = st.sb("starti", [P, TB], I32)
        padi = st.sb("padi", [1, 3, P], I32)
        wini = st.sb("wini", [P, TB], I32)
        raw = st.sb("raw", [P, 2 * TB, 3, P], I32)
        rawf = st.sb("rawf", [P, 2 * TB, 3, P])
        ok = st.sb("ok", [P, P])
        key = st.sb("key", [P, TB, P])
        pads = st.sb("pads", [1, P])
        ps = st.ps("ps")
        pt = [st.ps("pt0"), st.ps("pt1")]
        padded, padf = sem("tt_padded"), sem("tt_padf")
        ld, dv, mm = sem("tt_ld"), sem("tt_dv"), sem("tt_mm")
        counted, cut_ready, got, laid, turned, copied, out = (
            sem("tt_counted"), sem("tt_cut"), sem("tt_got"), sem("tt_laid"), sem("tt_turned"),
            sem("tt_copied"), sem("tt_out"))
        with nc.Block() as block:
            @block.sync
            def _(sp):
                sp.dma_start(dsti[:, :], dst.rearrange("(p c) -> p c", p=EP)).then_inc(ld, 16)
                for k, one in enumerate((src, dst, etype)):
                    sp.dma_start(g.edges_d[k, 0:E].rearrange("(p c) -> p c", p=EP),
                                 one.rearrange("(p c) -> p c", p=EP)).then_inc(padded, 16)
                sp.wait_ge(padf, 3)
                sp.dma_start(g.edges_d[:, E:E + P].unsqueeze(0), padi[:, :, :]).then_inc(padded, 16)
                sp.wait_ge(cut_ready, 1)
                sp.dma_start(view(g.rows_d.tensor, 0, [[1, P], [P, TB]]), cuti[:, :],
                             allow_slow_non_contiguous=True).then_inc(out, 16)
                sp.dma_start(view(g.rows_d.tensor, TA, [[1, P], [P, TB]]), wini[:, :],
                             allow_slow_non_contiguous=True).then_inc(out, 16)
                sp.wait_ge(out, 32)
                sp.dma_start(g.rows[:, :], g.rows_d).then_inc(out, 16)
                for b in range(TB):
                    sp.wait_ge(laid, TB + b + 1)
                    n = P if (b + 1) * P <= T else T - b * P
                    sp.dma_start(view(g.keys_d.tensor, P + b * P * P, [[P, n], [1, P]]),
                                 key[0:n, b, :]).then_inc(out, 16)
                sp.dma_start(view(g.keys_d.tensor, 0, [[P, 1], [1, P]]), pads[:, :]).then_inc(out, 16)
                sp.dma_start(view(g.keys_d.tensor, P + T * P, [[P, 1], [1, P]]), pads[:, :]).then_inc(out, 16)
                sp.wait_ge(out, 16 * (3 + TB + 2))

            @block.gpsimd
            def _(pool):
                pool.wait_ge(padded, 64)
                pool.wait_ge(cut_ready, 1)
                for b in range(2 * TB):
                    at = (cuti if b < TB else starti)[:, b % TB:b % TB + 1]
                    for k in range(3):
                        pool.indirect_dma_start(raw[:, b, k, :], None,
                                                g.edges_d.rearrange("k (e one) -> (k e) one", one=1),
                                                bass.IndirectOffsetOnAxis(at, 0),
                                                element_offset=k * (E + P)).then_inc(got, 16)

            @block.tensor
            def _(pe):
                pe.wait_ge(counted, 1)
                nc.tensor.matmul(ps[:, 0:NW + 1], g.ones[0:EP, :], below[:, :],
                                 start=True, stop=True).then_inc(mm, 1)
                for b in range(2 * TB):
                    pe.wait_ge(laid, b + 1)
                    if b >= 2:
                        pe.wait_ge(copied, b - 1)
                    for k in range(3):
                        t = nc.tensor.transpose(pt[b % 2][:, k * P:(k + 1) * P], rawf[:, b, k, :], g.ident[:, :])
                    t.then_inc(turned, 1)

            @block.vector
            def _(dve):
                c = Chain(dve, dv)
                nc.vector.memset(pads[:, :], -5.0)
                for k in range(3):
                    nc.vector.memset(padi[:, k, :], -1 if k == 1 else 0).then_inc(padf, 1)
                dve.wait_ge(ld, 16)
                c.step(nc.vector.tensor_copy(dstf[:, :], dsti[:, :]))
                for w in range(NW + 1):
                    ins = nc.vector.tensor_scalar(junk[:, :], dstf[:, :], float(P * w), None, ALU.is_lt, ALU.add,
                                                  accum_out=below[:, w:w + 1])
                    c.step(ins)
                nc.vector.engine_nop().then_inc(counted, 1)
                dve.wait_ge(mm, 1)
                c.step(nc.vector.tensor_copy(first[:, :], ps[:, 0:NW + 1]))
                c.step(nc.vector.tensor_tensor(tmp[:, :], first[:, 1:NW + 1], first[:, 0:NW], ALU.subtract))
                c.step(nc.vector.tensor_scalar(cnti[:, :], tmp[:, :], 127.0, None, ALU.add))
                c.step(nc.vector.tensor_scalar(cnti[:, :], cnti[:, :], 7, None, ALU.arith_shift_right))
                c.step(nc.vector.tensor_copy(ntile[:, :], cnti[:, :]))
                c.step(nc.vector.tensor_tensor_scan(upto[:, :], g.ones[:, 0:NW], ntile[:, :], 0.0,
                                                    ALU.mult, ALU.add))
                c.step(nc.vector.tensor_tensor(tmp[:, :], upto[:, :], ntile[:, :], ALU.subtract))
                c.step(nc.vector.scalar_tensor_tensor(base[:, :], tmp[:, :], -128.0, first[:, 0:NW],
                                                      ALU.mult, ALU.add))
                for b in range(TB):
                    t = g.tile_f[:, b:b + 1]
                    c.step(nc.vector.tensor_scalar(tmp[:, :], upto[:, :], t, None, ALU.is_le, ALU.add,
                                                   accum_out=win[:, b:b + 1]))
                    c.step(nc.vector.tensor_scalar(tmp[:, :], g.iota[:, 0:NW], win[:, b:b + 1], None, ALU.is_equal))
                    c.step(nc.vector.tensor_tensor(tmp[:, :], tmp[:, :], base[:, :], ALU.mult))
                    c.step(nc.vector.tensor_reduce(start[:, b:b + 1], tmp[:, :], X, ALU.add))
                c.step(nc.vector.scalar_tensor_tensor(start[:, :], g.tile_f[:, :], 128.0, start[:, :],
                                                      ALU.mult, ALU.add))
                c.step(nc.vector.tensor_scalar(cut[:, :], start[:, :], float(E - P), None, ALU.min))
                c.step(nc.vector.tensor_tensor(off[:, :], start[:, :], cut[:, :], ALU.subtract))
                c.step(nc.vector.tensor_scalar(win[:, :], win[:, :], float(NW - 1), None, ALU.min))
                c.step(nc.vector.tensor_scalar(start[:, :], start[:, :], float(E), None, ALU.min))
                c.step(nc.vector.tensor_copy(starti[:, :], start[:, :]))
                c.step(nc.vector.tensor_copy(cuti[:, :], cut[:, :]))
                c.step(nc.vector.tensor_scalar(tmp[:, 0:TB], win[:, :], -float(P), None, ALU.mult))
                nc.vector.tensor_copy(wini[:, :], win[:, :]).then_inc(cut_ready, 1)
                for b in range(2 * TB):
                    if b == 0:
                        dve.wait_ge(got, 16 * 6 * TB)
                    c.step(nc.vector.tensor_copy(rawf[:, b, :, :], raw[:, b, :, :]))
                    dl, key_b, u = rawf[:, b, 1, :], key[:, b % TB, :], b % TB
                    c.step(nc.vector.tensor_scalar(key_b, dl, 1.0, None, ALU.add))
                    c.step(nc.vector.tensor_scalar(dl, dl, tmp[:, u:u + 1], None, ALU.add))
                    if b < TB:
                        c.step(nc.vector.tensor_scalar(ok[:, :], g.iota[:, :], off[:, u:u + 1], None, ALU.is_ge))
                    else:
                        c.step(nc.vector.tensor_copy(ok[:, :], g.ones[:, :]))
                    c.step(nc.vector.scalar_tensor_tensor(ok[:, :], dl, 0.0, ok[:, :], ALU.is_ge, ALU.mult))
                    c.step(nc.vector.scalar_tensor_tensor(ok[:, :], dl, float(P), ok[:, :], ALU.is_lt, ALU.mult))
                    c.step(nc.vector.scalar_tensor_tensor(dl, dl, 1.0, ok[:, :], ALU.add, ALU.mult))
                    c.step(nc.vector.tensor_tensor(key_b, key_b, ok[:, :], ALU.mult))
                    c.step(nc.vector.tensor_scalar(dl, dl, -1.0, None, ALU.add))
                    nc.vector.tensor_scalar(key_b, key_b, -1.0, None, ALU.add).then_inc(laid, 1)
                for b in range(2 * TB):
                    bs = slice((b % TB) * P, (b % TB + 1) * P)
                    bank = pt[b % 2]
                    dve.wait_ge(turned, b + 1)
                    if b < TB:
                        c.step(nc.vector.tensor_copy(g.cut_src_i[:, bs], bank[:, 0:P]))
                        c.step(nc.vector.tensor_copy(g.cut_dloc[:, bs], bank[:, P:2 * P]))
                        nc.vector.tensor_copy(g.cut_rel[:, bs], bank[:, 2 * P:3 * P]).then_inc(copied, 1)
                    else:
                        c.step(nc.vector.tensor_copy(g.src_i[:, bs], bank[:, 0:P]))
                        c.step(nc.vector.tensor_copy(g.dloc[:, bs], bank[:, P:2 * P]))
                        c.step(nc.vector.tensor_copy(g.rel[:, bs], bank[:, 2 * P:3 * P]))
                        nc.vector.scalar_tensor_tensor(g.msg_i[:, bs], g.src_i[:, bs], float(RELS), g.rel[:, bs],
                                                       ALU.mult, ALU.add).then_inc(copied, 1)


def out_degrees(nc, g, sem, src):
    W = 8
    with Stage(nc, "od") as st:
        si = st.sb("si", [EP, EC], I32)
        part = st.sb("part", [EP, EC], I32)
        lo = st.sb("lo", [EP, EC])
        hi = st.sb("hi", [EP, EC])
        low = st.sb("low", [EP, 2, W, P], BF16)
        high = st.sb("high", [EP, 2, W, NW], BF16)
        zero = st.sb("zero", [EP, P], BF16)
        ps = st.ps("ps")
        ld, dv, built, counted = sem("od_ld"), sem("od_dv"), sem("od_built"), sem("od_counted")
        groups = EC // W
        with nc.Block() as block:
            @block.sync
            def _(sp):
                sp.dma_start(si[:, :], src.rearrange("(p c) -> p c", p=EP)).then_inc(ld, 16)

            @block.vector
            def _(dve):
                c = Chain(dve, dv)
                nc.vector.memset(zero[:, :], 0.0)
                dve.wait_ge(ld, 16)
                c.step(nc.vector.tensor_scalar(part[:, :], si[:, :], 127, None, ALU.bitwise_and))
                c.step(nc.vector.tensor_copy(lo[:, :], part[:, :]))
                c.step(nc.vector.tensor_scalar(part[:, :], si[:, :], 7, None, ALU.arith_shift_right))
                c.step(nc.vector.tensor_copy(hi[:, :], part[:, :]))
                with dve.Fori(0, groups // 2) as i:
                    for s in range(2):
                        dve.wait_ge(counted, 2 * i + s + 1)
                        cols = bass.ds((2 * i + s) * W, W)
                        nc.vector.tensor_tensor(low[:, s, :, :], lo[:, cols].unsqueeze(2).broadcast_to([EP, W, P]),
                                                g.iota[0:EP, :].unsqueeze(1).broadcast_to([EP, W, P]),
                                                ALU.is_equal).then_inc(built, 1)
                        nc.vector.tensor_tensor(high[:, s, :, :], hi[:, cols].unsqueeze(2).broadcast_to([EP, W, NW]),
                                                g.iota[0:EP, 0:NW].unsqueeze(1).broadcast_to([EP, W, NW]),
                                                ALU.is_equal).then_inc(built, 1)
                dve.wait_ge(counted, groups + 3)
                nc.vector.tensor_copy(g.outdeg[:, :], ps[:, 0:NW])

            @block.tensor
            def _(pe):
                pe.sem_inc(counted, 2)
                pe.wait_ge(built, 2)
                nc.tensor.matmul(ps[:, 0:NW], zero[:, :], zero[:, 0:NW], start=True, stop=False)
                with pe.Fori(0, groups // 2) as i:
                    for s in range(2):
                        pe.wait_ge(built, 4 * i + 2 * s + 2)
                        for k in range(W):
                            mm = nc.tensor.matmul(ps[:, 0:NW], low[:, s, k, :], high[:, s, k, :],
                                                  start=False, stop=False)
                        mm.then_inc(counted, 1)
                nc.tensor.matmul(ps[:, 0:NW], zero[:, :], zero[:, 0:NW], start=False, stop=True).then_inc(counted, 1)


def layer_norm(nc, g, sem, name):
    x3 = g.x[:, :].rearrange("p (w f) -> p w f", f=D)
    h3 = g.h[:, :].rearrange("p (w f) -> p w f", f=D)
    with Stage(nc, name) as st:
        sq = st.sb("sq", [P, NW, D])
        mean = st.sb("mean", [P, NW])
        var = st.sb("var", [P, NW])
        rstd = st.sb("rstd", [P, NW])
        dv, centred, squared, rooted = sem(name + "_dv"), sem(name + "_cen"), sem(name + "_sq"), sem(name + "_rt")
        with nc.Block() as block:
            @block.vector
            def _(dve):
                c = Chain(dve, dv)
                c.step(nc.vector.tensor_reduce(mean[:, :], x3, X, ALU.add))
                c.step(nc.vector.tensor_scalar(mean[:, :], mean[:, :], 1.0 / D, None, ALU.mult))
                nc.vector.tensor_tensor(h3, x3, mean[:, :].unsqueeze(2).broadcast_to([P, NW, D]),
                                        ALU.subtract).then_inc(centred, 1)
                dve.wait_ge(squared, 1)
                c.step(nc.vector.tensor_reduce(var[:, :], sq[:, :, :], X, ALU.add))
                nc.vector.tensor_scalar(var[:, :], var[:, :], 1.0 / D, EPS, ALU.mult, ALU.add).then_inc(centred, 1)
                dve.wait_ge(rooted, 1)
                c.step(nc.vector.reciprocal(rstd[:, :], var[:, :]))
                nc.vector.scalar_tensor_tensor(h3, h3, 0.0, rstd[:, :].unsqueeze(2).broadcast_to([P, NW, D]),
                                               ALU.max, ALU.mult)

            @block.scalar
            def _(act):
                act.wait_ge(centred, 1)
                nc.scalar.activation(sq[:, :, :], h3, ACT.Square).then_inc(squared, 1)
                act.wait_ge(centred, 2)
                nc.scalar.activation(var[:, :], var[:, :], ACT.Sqrt).then_inc(rooted, 1)


def gather_sum(nc, g, sem, name, table, index, width, acc, acc_width, attr=None, coef=None):
    B, R = 8, 8
    GROUP = 4
    full = 2 * D if attr is not None else width
    dloc = g.cut_dloc if attr is not None else g.dloc
    with Stage(nc, name) as st:
        rows = st.sb("rows", [P, R, full])
        idx = st.sb("idx", [P, B], I32)
        sel = st.sb("sel", [P, GROUP, P])
        of_rel = st.sb("of_rel", [P, GROUP, RELS])
        ps = [st.ps(f"ps{s}") for s in range(GROUP)]
        gathered = [sem(f"{name}_g{r}") for r in range(R)]
        loaded = [sem(f"{name}_a{r}") for r in range(R)] if attr is not None else None
        staged, sel_made, summed, added = (
            sem(name + "_staged"), sem(name + "_sel"), sem(name + "_summed"), sem(name + "_added"))
        with nc.Block() as block:
            @block.gpsimd
            def _(pool):
                with pool.Fori(0, T // B) as i:
                    pool.wait_ge(summed, B * i + R)
                    pool.nop(nofuse=True)
                    nc.gpsimd.tensor_copy(idx[:, :], index[:, bass.ds(B * i, B)]).then_inc(staged, 1)
                    pool.wait_ge(staged, i + 1)
                    pool.nop(nofuse=True)
                    for r in range(B):
                        pool.indirect_dma_start(rows[:, r, 0:width], None, table,
                                                bass.IndirectOffsetOnAxis(idx[:, r:r + 1], 0)).then_inc(gathered[r], 16)

            if attr is not None:
                @block.sync
                def _(sp):
                    with sp.Fori(0, T // B) as i:
                        for r in range(B):
                            e0 = sp.value_load(g.rows[0:1, bass.ds(B * i + r, 1)], min_val=0, max_val=E - P)
                            sp.wait_ge(summed, B * i + r + 1)
                            sp.dma_start(rows[:, r, D:2 * D], attr[bass.ds(e0, P), :]).then_inc(loaded[r], 16)

            @block.tensor
            def _(pe):
                pe.sem_inc(summed, R)
                with pe.Fori(0, T // B) as i:
                    for r in range(B):
                        s = r % GROUP
                        pe.wait_ge(gathered[r], 16 * (i + 1))
                        if attr is not None:
                            pe.wait_ge(loaded[r], 16 * (i + 1))
                        pe.wait_ge(sel_made, (B // GROUP) * i + r // GROUP + 1)
                        mm = nc.tensor.matmul(ps[s][:, 0:full], sel[:, s, :], rows[:, r, :], start=True, stop=True)
                        if attr is not None:
                            mm = nc.tensor.matmul(ps[s][:, full:full + RELS], sel[:, s, :], of_rel[:, s, :],
                                                  start=True, stop=True)
                        mm.then_inc(summed, 1)

            @block.vector
            def _(dve):
                with dve.Fori(0, T // B) as i:
                    for q in range(B // GROUP):
                        t0 = B * i + q * GROUP
                        dve.wait_ge(summed, t0 + R)
                        if attr is not None:
                            nc.vector.tensor_tensor(
                                of_rel[:, :, :], g.cut_rel[:, bass.ds(t0, GROUP)].unsqueeze(2).broadcast_to([P, GROUP, RELS]),
                                g.iota[:, 0:RELS].unsqueeze(1).broadcast_to([P, GROUP, RELS]), ALU.is_equal)
                        for s in range(GROUP):
                            if coef is None:
                                ins = nc.vector.tensor_scalar(sel[:, s, :], g.iota[:, :], dloc[:, bass.ds(t0 + s, 1)],
                                                              None, ALU.is_equal)
                            else:
                                ins = nc.vector.tensor_scalar(sel[:, s, :], g.iota[:, :], dloc[:, bass.ds(t0 + s, 1)],
                                                              coef[:, bass.ds(t0 + s, 1)], ALU.is_equal, ALU.mult)
                        ins.then_inc(sel_made, 1)
                        for s in range(GROUP):
                            w = dve.value_load(g.rows[0:1, bass.ds(TA + t0 + s, 1)], min_val=0, max_val=NW - 1)
                            dve.wait_ge(summed, t0 + s + R + 1)
                            dve.wait_ge(added, t0 + s + 1)
                            part = acc[:, bass.ds(w * acc_width, acc_width)]
                            nc.vector.tensor_tensor(part, part, ps[s][:, 0:acc_width], ALU.add).then_inc(added, 1)

            @block.scalar
            def _(act):
                act.sem_inc(added, 1)


def layer0(nc, g, sem, a):
    W0 = 2 * D + RELS
    with Stage(nc, "l0") as st:
        acc = st.sb("acc", [P, NW * W0])
        nsrc = st.sb("nsrc", [P, NW])
        ndst = st.sb("ndst", [P, NW])
        deg = g.deg
        rself = st.sb("rself", [P, NW])
        redge = st.sb("redge", [P, NW])
        has = st.sb("has", [P, NW])
        acc3 = acc[:, :].rearrange("p (w f) -> p w f", f=W0)
        h3 = g.h[:, :].rearrange("p (w f) -> p w f", f=D)
        with Stage(nc, "l0a") as sa:
            hn = sa.sb("hn", [P, NW, D])
            dv, rt, ready, out = sem("l0a_dv"), sem("l0a_rt"), sem("l0a_ready"), sem("l0a_out")
            with nc.Block() as block:
                @block.vector
                def _(dve):
                    c = Chain(dve, dv)
                    nc.vector.memset(acc[:, :], 0.0)
                    c.step(nc.vector.tensor_scalar(nsrc[:, :], g.outdeg[:, :], 1.0, None, ALU.max))
                    nc.vector.engine_nop().then_inc(ready, 1)
                    dve.wait_ge(rt, 1)
                    c.step(nc.vector.reciprocal(nsrc[:, :], nsrc[:, :]))
                    nc.vector.tensor_tensor(hn[:, :, :], h3, nsrc[:, :].unsqueeze(2).broadcast_to([P, NW, D]),
                                            ALU.mult).then_inc(ready, 1)

                @block.scalar
                def _(act):
                    act.wait_ge(ready, 1)
                    nc.scalar.activation(nsrc[:, :], nsrc[:, :], ACT.Sqrt).then_inc(rt, 1)

                @block.sync
                def _(sp):
                    sp.wait_ge(ready, 2)
                    sp.dma_start(g.node_d.rearrange("(w p) f -> p w f", p=P), hn[:, :, :]).then_inc(out, 16)
                    sp.wait_ge(out, 16)
        gather_sum(nc, g, sem, "l0e", g.node_d, g.cut_src_i, D, acc, W0, attr=a["edge_attr_128"])
        with Stage(nc, "l0b") as sb_:
            w = sb_.sb("w", [P, 2, D])
            bb = sb_.sb("bb", [P, 2, D])
            z = sb_.sb("z", [P, 2, 2, D])
            zt = sb_.sb("zt", [P, 2, 2, D])
            pt = [sb_.ps("pt0"), sb_.ps("pt1")]
            po = [sb_.ps("po0"), sb_.ps("po1")]
            dv, rt, ready, ld = sem("l0b_dv"), sem("l0b_rt"), sem("l0b_ready"), sem("l0b_ld")
            mixed, turned, copied, multiplied, lp = (
                sem("l0b_mixed"), sem("l0b_turned"), sem("l0b_copied"), sem("l0b_mult"), sem("l0b_lp"))
            with nc.Block() as block:
                @block.sync
                def _(sp):
                    sp.dma_start(w[:, 0, :], a["L0_gnn_W"]).then_inc(ld, 16)
                    sp.dma_start(w[:, 1, :], a["L0_gnn_We"]).then_inc(ld, 16)
                    sp.dma_start(bb[:, 0, :], a["L0_gnn_b"].partition_broadcast(P)).then_inc(ld, 16)
                    sp.dma_start(bb[:, 1, :], a["L0_gnn_be"].partition_broadcast(P)).then_inc(ld, 16)

                @block.scalar
                def _(act):
                    act.wait_ge(ready, 1)
                    nc.scalar.activation(ndst[:, :], ndst[:, :], ACT.Sqrt).then_inc(rt, 1)
                    with act.Fori(0, NW // 2) as i:
                        for j in range(2):
                            act.wait_ge(turned, 2 * i + j + 1)
                            act.wait_ge(multiplied, 2 * i + j + 1)
                            act.nop(nofuse=True)
                            nc.scalar.copy(zt[:, j, :, :], pt[j][:, 0:2 * D]).then_inc(copied, 1)

                @block.tensor
                def _(pe):
                    pe.sem_inc(multiplied, 2)
                    pe.wait_ge(ld, 64)
                    with pe.Fori(0, NW // 2) as i:
                        for j in range(2):
                            pe.wait_ge(mixed, 2 * i + j + 1)
                            for k in range(2):
                                mm = nc.tensor.transpose(pt[j][:, k * D:(k + 1) * D], z[:, j, k, :], g.ident[:, :])
                            mm.then_inc(turned, 1)
                        for j in range(2):
                            pe.wait_ge(copied, 2 * i + j + 1)
                            for k in range(2):
                                mm = nc.tensor.matmul(po[j][:, 0:D], zt[:, j, k, :], w[:, k, :],
                                                      start=(k == 0), stop=(k == 1))
                            mm.then_inc(multiplied, 1)

                @block.vector
                def _(dve):
                    c = Chain(dve, dv)
                    c.step(nc.vector.tensor_reduce(deg[:, :], acc3[:, :, 2 * D:], X, ALU.add))
                    c.step(nc.vector.tensor_copy(g.count[:, :].rearrange("p (w f) -> p w f", f=RELS), acc3[:, :, 2 * D:]))
                    c.step(nc.vector.tensor_scalar(redge[:, :], deg[:, :], 1.0, None, ALU.max))
                    c.step(nc.vector.tensor_copy(ndst[:, :], redge[:, :]))
                    nc.vector.engine_nop().then_inc(ready, 1)
                    c.step(nc.vector.reciprocal(redge[:, :], redge[:, :]))
                    c.step(nc.vector.tensor_scalar(rself[:, :], deg[:, :], 1.0, None, ALU.add))
                    c.step(nc.vector.reciprocal(rself[:, :], rself[:, :]))
                    c.step(nc.vector.tensor_tensor(has[:, :], deg[:, :], redge[:, :], ALU.mult))
                    dve.wait_ge(rt, 1)
                    c.step(nc.vector.reciprocal(ndst[:, :], ndst[:, :]))
                    dve.wait_ge(ld, 64)
                    base = c.n
                    with dve.Fori(0, NW // 2) as i:
                        for j in range(2):
                            v = 2 * i + j
                            wd = bass.ds(v * D, D)
                            c.n = base + i * 12 + 2 * j
                            c.step(nc.vector.tensor_scalar(z[:, j, 0, :], acc[:, bass.ds(v * W0, D)],
                                                           ndst[:, bass.ds(v, 1)], None, ALU.mult))
                            c.step(nc.vector.scalar_tensor_tensor(z[:, j, 0, :], g.h[:, wd], rself[:, bass.ds(v, 1)],
                                                                  z[:, j, 0, :], ALU.mult, ALU.add))
                            nc.vector.tensor_scalar(z[:, j, 1, :], acc[:, bass.ds(v * W0 + D, D)],
                                                    redge[:, bass.ds(v, 1)], None, ALU.mult).then_inc(mixed, 1)
                        for j in range(2):
                            v = 2 * i + j
                            xw = g.x[:, bass.ds(v * D, D)]
                            dve.wait_ge(multiplied, v + 3)
                            c.n = base + i * 12 + 4 + 4 * j
                            c.step(nc.vector.tensor_tensor(xw, xw, po[j][:, 0:D], ALU.add))
                            c.step(nc.vector.tensor_tensor(xw, xw, bb[:, 0, :], ALU.add))
                            c.step(nc.vector.scalar_tensor_tensor(xw, bb[:, 0, :], rself[:, bass.ds(v, 1)], xw,
                                                                  ALU.mult, ALU.add))
                            c.step(nc.vector.scalar_tensor_tensor(xw, bb[:, 1, :], has[:, bass.ds(v, 1)], xw,
                                                                  ALU.mult, ALU.add))


def window_copies(nc, pool, src, dst_of, freed, copied, width=D, stride=None, offset=0):
    stride = width if stride is None else stride
    with pool.Fori(0, NW // 2) as i:
        for j in range(2):
            v = 2 * i + j
            pool.wait_ge(freed, v + 1)
            pool.nop(nofuse=True)
            nc.gpsimd.tensor_copy(dst_of(j), src[:, bass.ds(v * stride + offset, width)]).then_inc(copied, 1)


def attention_nodes(nc, g, sem, name, weights, biases, transposed, scale, heads, qwin, qw, self_score=None):
    HD = D // heads
    with Stage(nc, name) as st:
        w = st.sb("w", [P, 3 * D])
        wraw = st.sb("wraw", [P, 3 * D])
        bias = st.sb("bias", [P, 3 * D])
        hc = st.sb("hc", [P, 2, D])
        ht = st.sb("ht", [P, 2, D])
        vkq = st.sb("vkq", [P, 2, 3 * D])
        prod = st.sb("prod", [P, 2, D])
        pw = st.ps("pw")
        pt = [st.ps("pt0"), st.ps("pt1")]
        po = [st.ps("po0"), st.ps("po1")]
        ld, wt, wc, dv, copied, turned, moved, projected, ready, stored = (
            sem(name + k) for k in ("_ld", "_wt", "_wc", "_dv", "_copied", "_turned", "_moved", "_proj", "_ready", "_st"))
        nld = 3 + sum(b is not None for b in biases)
        with nc.Block() as block:
            @block.sync
            def _(sp):
                for k in range(3):
                    sp.dma_start((wraw if transposed else w)[:, k * D:(k + 1) * D], weights[k]).then_inc(ld, 16)
                    if biases[k] is not None:
                        sp.dma_start(bias[:, k * D:(k + 1) * D], biases[k].partition_broadcast(P)).then_inc(ld, 16)
                sp.sem_inc(stored, 16)
                with sp.Fori(0, NW // 2) as i:
                    sp.wait_ge(ready, 2 * i + 4)
                    sp.dma_start(g.pair_d[bass.ds(2 * i * P, 2 * P), :].rearrange("(j p) f -> p j f", p=P),
                                 vkq[:, :, 0:2 * D]).then_inc(stored, 16)
                sp.wait_ge(stored, 16 * (NW // 2 + 1))

            @block.gpsimd
            def _(pool):
                window_copies(nc, pool, g.h, lambda j: hc[:, j, :], turned, copied)

            @block.scalar
            def _(act):
                act.sem_inc(ready, 2)
                with act.Fori(0, NW // 2) as i:
                    for j in range(2):
                        act.wait_ge(turned, 2 * i + j + 3)
                        act.wait_ge(projected, 2 * i + j + 1)
                        act.nop(nofuse=True)
                        nc.scalar.copy(ht[:, j, :], pt[j][:, 0:D]).then_inc(moved, 1)

            @block.tensor
            def _(pe):
                pe.sem_inc(turned, 2)
                pe.sem_inc(projected, 2)
                pe.wait_ge(ld, 16 * nld)
                if transposed:
                    for k in range(3):
                        mm = nc.tensor.transpose(pw[:, k * D:(k + 1) * D], wraw[:, k * D:(k + 1) * D], g.ident[:, :])
                    mm.then_inc(wt, 1)
                    pe.wait_ge(wc, 1)
                with pe.Fori(0, NW // 2) as i:
                    for j in range(2):
                        pe.wait_ge(copied, 2 * i + j + 1)
                        nc.tensor.transpose(pt[j][:, 0:D], hc[:, j, :], g.ident[:, :]).then_inc(turned, 1)
                    for j in range(2):
                        pe.wait_ge(moved, 2 * i + j + 1)
                        pe.wait_ge(ready, 2 * i + j + 1)
                        nc.tensor.matmul(po[j][:, 0:3 * D], ht[:, j, :], w[:, :],
                                         start=True, stop=True).then_inc(projected, 1)

            @block.vector
            def _(dve):
                c = Chain(dve, dv)
                for k in range(3):
                    if biases[k] is None:
                        nc.vector.memset(bias[:, k * D:(k + 1) * D], 0.0)
                if transposed:
                    dve.wait_ge(wt, 1)
                    c.step(nc.vector.tensor_copy(w[:, :], pw[:, 0:3 * D]))
                    nc.vector.engine_nop().then_inc(wc, 1)
                if self_score is not None:
                    rc3 = qwin[:, :].rearrange("p (w f) -> p w f", f=qw)
                    c.step(nc.vector.memset(rc3[:, :, D:], 0.0))
                    c.step(nc.vector.tensor_scalar(rc3[:, :, D:D + RELS],
                                                   g.count[:, :].rearrange("p (w f) -> p w f", f=RELS),
                                                   1.0, None, ALU.max))
                    c.step(nc.vector.reciprocal(rc3[:, :, D:D + RELS], rc3[:, :, D:D + RELS]))
                dve.wait_ge(ld, 16 * nld)
                steps = 4 if self_score is not None else 2
                base = c.n
                with dve.Fori(0, NW // 2) as i:
                    dve.wait_ge(stored, 16 * (i + 1))
                    for j in range(2):
                        v = 2 * i + j
                        c.n = base + i * steps + (steps // 2) * j
                        dve.wait_ge(projected, v + 3)
                        c.step(nc.vector.tensor_tensor(vkq[:, j, :], po[j][:, 0:3 * D], bias[:, :], ALU.add))
                        qv = qwin[:, bass.ds(v * qw, D)]
                        if self_score is not None:
                            nc.vector.tensor_scalar(qv, vkq[:, j, 2 * D:], scale, None, ALU.mult)
                            c.step(nc.vector.scalar_tensor_tensor(prod[:, j, :], vkq[:, j, 2 * D:], scale,
                                                                  vkq[:, j, D:2 * D], ALU.mult, ALU.mult))
                            nc.vector.tensor_reduce(self_score[:, bass.ds(v * heads, heads)],
                                                    prod[:, j, :].rearrange("p (h d) -> p h d", h=heads),
                                                    X, ALU.add).then_inc(ready, 1)
                        else:
                            nc.vector.tensor_scalar(qv, vkq[:, j, 2 * D:], scale, None, ALU.mult).then_inc(ready, 1)


def attention_scores(nc, g, sem, name, heads, qwin, qw, scores, groups, v_spill):
    B = GROUP = 4
    R = 8
    GW = qw // groups
    rel_cols = qw - D
    with Stage(nc, name) as st:
        rows = st.sb("rows", [P, R, D + qw])
        idx = st.sb("idx", [P, R], I32)
        sel = st.sb("sel", [P, GROUP, P])
        selt = st.sb("selt", [P, GROUP, P])
        prod = st.sb("prod", [P, GROUP, qw])
        pst = st.ps("pst")
        pq = st.ps("pq", (P, GROUP, 512))
        gathered = [sem(f"{name}_g{r}") for r in range(R)]
        staged, sel_made, turned, moved, looked, used, spilled, rel_made, reduced = (
            sem(name + k) for k in ("_staged", "_sel", "_turned", "_moved", "_looked", "_used", "_spill", "_rel",
                                    "_reduced"))
        with nc.Block() as block:
            @block.gpsimd
            def _(pool):
                with pool.Fori(0, T // R) as i:
                    pool.wait_ge(used, 2 * i + 2)
                    pool.nop(nofuse=True)
                    nc.gpsimd.tensor_copy(idx[:, :], g.src_i[:, bass.ds(R * i, R)]).then_inc(staged, 1)
                    pool.wait_ge(spilled, 32 * i + 32)
                    pool.nop(nofuse=True)
                    pool.wait_ge(staged, i + 1)
                    pool.nop(nofuse=True)
                    for r in range(R):
                        pool.indirect_dma_start(rows[:, r, 0:2 * D], None, g.pair_d,
                                                bass.IndirectOffsetOnAxis(idx[:, r:r + 1], 0)).then_inc(gathered[r], 16)

            @block.sync
            def _(sp):
                sp.sem_inc(spilled, 32)
                with sp.Fori(0, T // R) as i:
                    for q in range(R // GROUP):
                        for s in range(GROUP):
                            sp.wait_ge(gathered[q * GROUP + s], 16 * (i + 1))
                        sp.dma_start(v_spill[bass.ds((R * i + q * GROUP) * P, GROUP * P), :]
                                     .rearrange("(s p) f -> p s f", p=P),
                                     rows[:, q * GROUP:(q + 1) * GROUP, 0:D]).then_inc(spilled, 16)
                sp.wait_ge(spilled, 32 + 16 * (T // GROUP))

            @block.tensor
            def _(pe):
                with pe.Fori(0, T // R) as i:
                    for q in range(R // GROUP):
                        n = (R // GROUP) * i + q
                        pe.wait_ge(sel_made, n + 1)
                        for s in range(GROUP):
                            mm = nc.tensor.transpose(pst[:, s * P:(s + 1) * P], sel[:, s, :], g.ident[:, :])
                        mm.then_inc(turned, 1)
                        for s in range(GROUP):
                            w = pe.value_load(g.rows[0:1, bass.ds(TA + n * GROUP + s, 1)], min_val=0, max_val=NW - 1)
                            if s == 0:
                                pe.wait_ge(moved, n + 1)
                            mm = nc.tensor.matmul(pq[:, s, 0:qw], selt[:, s, :], qwin[:, bass.ds(w * qw, qw)],
                                                  start=True, stop=True)
                        mm.then_inc(looked, 1)

            @block.scalar
            def _(act):
                act.sem_inc(used, 2)
                with act.Fori(0, T // GROUP) as n:
                    act.wait_ge(turned, n + 1)
                    nc.scalar.copy(selt[:, :, :].rearrange("p s e -> p (s e)"), pst[:, :]).then_inc(moved, 1)

            @block.vector
            def _(dve):
                with dve.Fori(0, T // R) as i:
                    for q in range(R // GROUP):
                        n = (R // GROUP) * i + q
                        t0 = n * GROUP
                        r0 = q * GROUP
                        for s in range(GROUP):
                            ins = nc.vector.tensor_scalar(sel[:, s, :], g.iota[:, :], g.dloc[:, bass.ds(t0 + s, 1)],
                                                          None, ALU.is_equal)
                        ins.then_inc(sel_made, 1)
                        if rel_cols:
                            nc.vector.tensor_tensor(
                                rows[:, r0:r0 + GROUP, 2 * D:],
                                g.rel[:, bass.ds(t0, GROUP)].unsqueeze(2).broadcast_to([P, GROUP, rel_cols]),
                                g.iota[:, 0:rel_cols].unsqueeze(1).broadcast_to([P, GROUP, rel_cols]),
                                ALU.is_equal).then_inc(rel_made, 1)
                            dve.wait_ge(rel_made, n + 1)
                        for s in range(GROUP):
                            dve.wait_ge(gathered[r0 + s], 16 * (i + 1))
                        dve.wait_ge(looked, n + 1)
                        nc.vector.tensor_tensor(prod[:, :, :], pq[:, :, 0:qw], rows[:, r0:r0 + GROUP, D:],
                                                ALU.mult).then_inc(used, 1)
                        dve.wait_ge(used, n + 3)
                        nc.vector.tensor_reduce(scores[:, bass.ds(t0 * groups, GROUP * groups)],
                                                prod[:, :, :].rearrange("p s (k d) -> p (s k) d", d=GW),
                                                X, ALU.add).then_inc(reduced, 1)
                        dve.wait_ge(reduced, n + 1)


def scores_to_rows(nc, g, sem, name, heads, scores, groups, t1_d):
    NB = T * heads // P
    BI = NB // 13
    TPB = P // heads
    with Stage(nc, name + "t") as st:
        packed = st.sb("packed", [P, BI, P])
        turned_sb = st.sb("turned", [P, NB, P])
        pt = st.ps("pt")
        packs, turns, takes, out = (sem(name + k) for k in ("_packs", "_turns", "_takes", "_out"))
        with nc.Block() as block:
            @block.scalar
            def _(act):
                act.sem_inc(turns, 1)
                with act.Fori(0, 13) as i:
                    act.wait_ge(turns, i + 1)
                    act.nop(nofuse=True)
                    src = scores[:, bass.ds(i * BI * TPB * groups, BI * TPB * groups)] \
                        .rearrange("p (t k) -> p t k", k=groups)[:, :, 0:heads]
                    nc.scalar.copy(packed[:, :, :].rearrange("p b (t h) -> p (b t) h", h=heads), src) \
                        .then_inc(packs, 1)

            @block.tensor
            def _(pe):
                with pe.Fori(0, 13) as i:
                    pe.wait_ge(packs, i + 1)
                    pe.wait_ge(takes, i + 1)
                    for b in range(BI):
                        mm = nc.tensor.transpose(pt[:, b * P:(b + 1) * P], packed[:, b, :], g.ident[:, :])
                    mm.then_inc(turns, 1)

            @block.vector
            def _(dve):
                nc.vector.engine_nop().then_inc(takes, 1)
                if groups > heads:
                    nc.vector.tensor_copy(g.coef[:, 0:T].unsqueeze(2),
                                          scores[:, :].rearrange("p (t k) -> p t k", k=groups)[:, :, heads:])
                with dve.Fori(0, 13) as i:
                    dve.wait_ge(turns, i + 2)
                    nc.vector.tensor_copy(turned_sb[:, bass.ds(i * BI, BI), :],
                                          pt[:, 0:BI * P].rearrange("p (b e) -> p b e", e=P)).then_inc(takes, 1)

            @block.sync
            def _(sp):
                sp.wait_ge(takes, 14)
                sp.dma_start(view(t1_d.tensor, 0, [[P, P], [P * P, NB], [1, P]]), turned_sb[:, :, :]).then_inc(out, 16)
                sp.wait_ge(out, 16)


def segment_scan(nc, g, sem, name, heads, with_first, t1_d, ex_d, mf_d, room):
    C = P // heads
    CT = T // C
    LEN = CT * P
    HR = heads * P
    with Stage(nc, name + "s") as st:
        sc = st.sb("sc", [P, LEN])
        key = st.sb("key", [P, LEN + 2])
        begin = st.sb("begin", [P, LEN], BF16)
        end = st.sb("end", [P, LEN], BF16)
        most = room[:, 0:LEN]
        sums = st.sb("sums", [P, 4])
        row = st.sb("row", [1, 6, P])
        carry = st.sb("carry", [P, 2])
        pr = st.ps("pr")
        pc = st.ps("pc")
        ld, dv, chunked, rowed, carried, lined, expd, ready, out = (
            sem(name + k) for k in ("_sld", "_sdv", "_chunked", "_rowed", "_carried", "_lined", "_expd", "_sready", "_sout"))
        back = key[:, 0:LEN]

        def chunks(d, h):
            return view(d.tensor, h * P, [[CT * HR, C], [HR, CT], [1, P]])

        with nc.Block() as block:
            @block.sync
            def _(sp):
                for h in range(heads):
                    ps_ = slice(h * C, (h + 1) * C)
                    sp.dma_start(sc[ps_, :].rearrange("p (t e) -> p t e", e=P), chunks(t1_d, h)).then_inc(ld, 16)
                    sp.dma_start(key[ps_, :], view(g.keys_d.tensor, P - 1, [[LEN, C], [1, LEN + 2]])).then_inc(ld, 16)
                sp.wait_ge(expd, 1)
                sp.wait_ge(ready, 2)
                for h in range(heads):
                    ps_ = slice(h * C, (h + 1) * C)
                    sp.dma_start(chunks(ex_d, h), sc[ps_, :].rearrange("p (t e) -> p t e", e=P)).then_inc(out, 16)
                    if with_first:
                        sp.dma_start(chunks(mf_d, h), back[ps_, :].rearrange("p (t e) -> p t e", e=P)).then_inc(out, 16)
                sp.wait_ge(out, 16 * heads * (2 if with_first else 1))

            @block.vector
            def _(dve):
                c = Chain(dve, dv)
                dve.wait_ge(ld, 32 * heads)
                c.step(nc.vector.tensor_tensor(begin[:, :], key[:, 1:LEN + 1], key[:, 0:LEN], ALU.not_equal))
                c.step(nc.vector.tensor_tensor(end[:, :], key[:, 1:LEN + 1], key[:, 2:LEN + 2], ALU.not_equal))
                c.step(nc.vector.tensor_scalar(begin[:, :], begin[:, :], FAR, None, ALU.mult))
                c.step(nc.vector.tensor_scalar(end[:, :], end[:, :], FAR, None, ALU.mult))
                c.step(nc.vector.tensor_reduce(sums[:, 0:1], begin[:, :], X, ALU.min))
                c.step(nc.vector.tensor_reduce(sums[:, 2:3], end[:, :], X, ALU.min))
                c.step(nc.vector.tensor_tensor_scan(most[:, :], begin[:, :], sc[:, :], FAR, ALU.add, ALU.max))
                c.step(nc.vector.tensor_copy(sums[:, 1:2], most[:, LEN - 1:LEN]))
                c.step(nc.vector.tensor_tensor_scan(back[:, ::-1], end[:, ::-1], sc[:, ::-1], FAR, ALU.add, ALU.max))
                c.step(nc.vector.tensor_copy(sums[:, 3:4], back[:, 0:1]))
                nc.vector.engine_nop().then_inc(chunked, 1)
                dve.wait_ge(rowed, 1)
                c.step(nc.vector.tensor_copy(row[:, 0:4, :].rearrange("p a b -> p (a b)"), pr[0:1, :]))
                c.step(nc.vector.memset(row[:, 4:6, :], FAR))
                c.step(nc.vector.tensor_tensor_scan(row[:, 4, 1:P], row[:, 0, 0:P - 1], row[:, 1, 0:P - 1],
                                                    FAR, ALU.add, ALU.max))
                c.step(nc.vector.tensor_tensor_scan(row[:, 5, P - 2::-1], row[:, 2, P - 1:0:-1], row[:, 3, P - 1:0:-1],
                                                    FAR, ALU.add, ALU.max))
                nc.vector.engine_nop().then_inc(carried, 1)
                dve.wait_ge(lined, 1)
                c.step(nc.vector.tensor_copy(carry[:, :], pc[:, 0:2]))
                c.step(nc.vector.tensor_tensor_scan(most[:, :], begin[:, :], sc[:, :], carry[:, 0:1], ALU.add, ALU.max))
                c.step(nc.vector.tensor_tensor_scan(back[:, ::-1], end[:, ::-1], sc[:, ::-1], carry[:, 1:2],
                                                    ALU.add, ALU.max))
                c.step(nc.vector.tensor_tensor(most[:, :], most[:, :], back[:, :], ALU.max))
                nc.vector.tensor_tensor(sc[:, :], sc[:, :], most[:, :], ALU.subtract).then_inc(ready, 1)
                c.step(nc.vector.scalar_tensor_tensor(back[:, :], begin[:, :], -1.0, most[:, :], ALU.is_lt, ALU.mult))
                nc.vector.engine_nop().then_inc(expd, 1)

            @block.scalar
            def _(act):
                act.wait_ge(ready, 1)
                act.wait_ge(expd, 1)
                nc.scalar.activation(sc[:, :], sc[:, :], ACT.Exp).then_inc(ready, 1)

            @block.tensor
            def _(pe):
                pe.wait_ge(chunked, 1)
                for k in range(4):
                    mm = nc.tensor.transpose(pr[0:1, k * P:(k + 1) * P], sums[:, k:k + 1], g.ident[:, :])
                mm.then_inc(rowed, 1)
                pe.wait_ge(carried, 1)
                for k in range(2):
                    mm = nc.tensor.matmul(pc[:, k:k + 1], row[0:1, 4 + k, :], g.ones[0:1, 0:1], start=True, stop=True)
                mm.then_inc(lined, 1)


def rows_to_scores(nc, g, sem, name, heads, ex, mf, ex_d, mf_d):
    NB = T * heads // P
    BI = NB // 13
    pairs = [(ex, ex_d)] + ([(mf, mf_d)] if mf is not None else [])
    K = len(pairs)
    with Stage(nc, name + "b") as st:
        rows = st.sb("rows", [P, K, 2, BI, P])
        pt = [st.ps(f"pt{k}") for k in range(K)]
        loaded = [[sem(f"{name}_bl{k}{j}") for j in range(2)] for k in range(K)]
        turned, taken = sem(name + "_bturned"), sem(name + "_btaken")
        with nc.Block() as block:
            @block.sync
            def _(sp):
                for i in range(13):
                    for k, (_, d) in enumerate(pairs):
                        if i >= 2:
                            sp.wait_ge(turned, K * (i - 2) + k + 1)
                        sp.dma_start(rows[:, k, i % 2, :, :],
                                     view(d.tensor, i * BI * P * P, [[P, P], [P * P, BI], [1, P]])) \
                            .then_inc(loaded[k][i % 2], 16)

            @block.tensor
            def _(pe):
                for i in range(13):
                    for k in range(K):
                        pe.wait_ge(loaded[k][i % 2], 16 * (i // 2 + 1))
                        if i >= 1:
                            pe.wait_ge(taken, K * (i - 1) + k + 1)
                        for b in range(BI):
                            mm = nc.tensor.transpose(pt[k][:, b * P:(b + 1) * P], rows[:, k, i % 2, b, :],
                                                     g.ident[:, :])
                        mm.then_inc(turned, 1)

            @block.vector
            def _(dve):
                for i in range(13):
                    for k, (to, _) in enumerate(pairs):
                        dve.wait_ge(turned, K * i + k + 1)
                        nc.vector.tensor_copy(to[:, i * BI * P:(i + 1) * BI * P], pt[k][:, 0:BI * P]).then_inc(taken, 1)


def attention_sums(nc, g, sem, name, heads, ex, mf, v_spill, acc, aw):
    GROUP, R = 4, 8
    HD = D // heads
    with Stage(nc, name + "p") as st:
        v = st.sb("v", [P, R, D])
        ve = st.sb("ve", [P, GROUP, D])
        sel = st.sb("sel", [P, GROUP, P])
        ps = [st.ps(f"ps{s}") for s in range(GROUP)]
        loaded = [sem(f"{name}_pl{q}") for q in range(2)]
        sel_made, weighted, summed, added = (sem(name + k) for k in ("_psel", "_pw", "_psum", "_padd"))
        with nc.Block() as block:
            @block.sync
            def _(sp):
                with sp.Fori(0, T // R) as i:
                    for q in range(2):
                        sp.wait_ge(weighted, 2 * i + q + 1)
                        sp.dma_start(v[:, q * GROUP:(q + 1) * GROUP, :],
                                     v_spill[bass.ds((R * i + q * GROUP) * P, GROUP * P), :]
                                     .rearrange("(s p) f -> p s f", p=P)).then_inc(loaded[q], 16)

            @block.scalar
            def _(act):
                act.sem_inc(weighted, 2)
                act.sem_inc(summed, GROUP)
                act.sem_inc(added, 1)

            @block.tensor
            def _(pe):
                with pe.Fori(0, T // GROUP) as n:
                    pe.wait_ge(weighted, n + 3)
                    for s in range(GROUP):
                        t = n * GROUP + s
                        nc.tensor.matmul(ps[s][:, 0:D], sel[:, s, :], ve[:, s, :], start=True, stop=True)
                        mm = nc.tensor.matmul(ps[s][:, D:D + heads], sel[:, s, :], ex[:, bass.ds(t * heads, heads)],
                                              start=True, stop=True)
                        if mf is not None:
                            mm = nc.tensor.matmul(ps[s][:, D + heads:D + 2 * heads], sel[:, s, :],
                                                  mf[:, bass.ds(t * heads, heads)], start=True, stop=True)
                        mm.then_inc(summed, 1)

            @block.vector
            def _(dve):
                with dve.Fori(0, T // R) as i:
                    for q in range(2):
                        t0 = R * i + q * GROUP
                        dve.wait_ge(summed, t0 + GROUP)
                        for s in range(GROUP):
                            nc.vector.tensor_scalar(sel[:, s, :], g.iota[:, :], g.dloc[:, bass.ds(t0 + s, 1)],
                                                    None, ALU.is_equal)
                        dve.wait_ge(loaded[q], 16 * (i + 1))
                        nc.vector.tensor_tensor(
                            ve[:, :, :].rearrange("p s (h d) -> p (s h) d", h=heads),
                            v[:, q * GROUP:(q + 1) * GROUP, :].rearrange("p s (h d) -> p (s h) d", h=heads),
                            ex[:, bass.ds(t0 * heads, GROUP * heads)].unsqueeze(2).broadcast_to([P, GROUP * heads, HD]),
                            ALU.mult).then_inc(weighted, 1)
                        for s in range(GROUP):
                            w = dve.value_load(g.rows[0:1, bass.ds(TA + t0 + s, 1)], min_val=0, max_val=NW - 1)
                            dve.wait_ge(summed, t0 + s + GROUP + 1)
                            dve.wait_ge(added, t0 + s + 1)
                            part = acc[:, bass.ds(w * aw, aw)]
                            nc.vector.tensor_tensor(part, part, ps[s][:, 0:aw], ALU.add).then_inc(added, 1)


def attention(nc, g, sem, name, heads, groups, qw, weights, biases, transposed, scale, own, acc, aw):
    with Stage(nc, name) as st:
        with Stage(nc, name + "y") as sy:
            scores = sy.sb("scores", [P, T * groups])
            with Stage(nc, name + "x") as sx:
                qwin = sx.sb("qwin", [P, NW * qw])
                attention_nodes(nc, g, sem, name + "n", weights, biases, transposed, scale, heads, qwin, qw, own)
                attention_scores(nc, g, sem, name + "a", heads, qwin, qw, scores, groups, g.spill_d)
            scores_to_rows(nc, g, sem, name + "r", heads, scores, groups, g.t1_d)
        segment_scan(nc, g, sem, name, heads, own is not None, g.t1_d, g.t2_d, g.t3_d, acc)
        ex = st.sb("ex", [P, T * heads])
        mf = st.sb("mf", [P, T * heads]) if own is not None else None
        rows_to_scores(nc, g, sem, name + "u", heads, ex, mf, g.t2_d, g.t3_d)
        with nc.Block() as block:
            @block.vector
            def _(dve):
                nc.vector.memset(acc[:, :], 0.0)
        attention_sums(nc, g, sem, name + "s", heads, ex, mf, g.spill_d, acc, aw)


def batch_norm(nc, g, c, dve, yt, stats, gain, shift, ask, got, k):
    c.step(nc.vector.tensor_reduce(stats[:, 2:3], yt[:, 0:N], X, ALU.add))
    nc.vector.tensor_scalar(stats[:, 3:4], stats[:, 2:3], -1.0 / N, None, ALU.mult).then_inc(ask, 1)
    dve.wait_ge(got, 2 * k + 1)
    nc.vector.tensor_scalar(stats[:, 4:5], stats[:, 4:5], 1.0 / N, EPS, ALU.mult, ALU.add).then_inc(ask, 1)
    dve.wait_ge(got, 2 * k + 2)
    c.step(nc.vector.reciprocal(stats[:, 5:6], stats[:, 5:6]))
    c.step(nc.vector.tensor_tensor(stats[:, 0:1], stats[:, 5:6], gain, ALU.mult))
    c.step(nc.vector.scalar_tensor_tensor(stats[:, 1:2], stats[:, 3:4], stats[:, 0:1], shift, ALU.mult, ALU.add))


def batch_norm_squares(nc, act, yt, junk, stats, ask, got, k):
    act.wait_ge(ask, 2 * k + 1)
    nc.scalar.activation(junk[:, 0:N], yt[:, 0:N], ACT.Square, bias=stats[:, 3:4], accum_out=stats[:, 4:5]).then_inc(got, 1)
    act.wait_ge(ask, 2 * k + 2)
    nc.scalar.activation(stats[:, 5:6], stats[:, 4:5], ACT.Sqrt).then_inc(got, 1)


def layer1(nc, g, sem, a):
    H = 8
    AW = D + 2 * H
    with Stage(nc, "l1") as st:
        own = st.sb("own", [P, NW * H])
        with Stage(nc, "l1acc") as sacc:
            acc = sacc.sb("acc", [P, NW * AW])
            attention(nc, g, sem, "l1t", H, H + 1, D + 16, [a["L1_gnn_v_w"], a["L1_gnn_k_w"], a["L1_gnn_q_w"]],
                      [None, None, a["L1_gnn_q_b"]], True, 16.0 ** -0.5, own, acc, AW)
            acc3 = acc[:, :].rearrange("p (w f) -> p w f", f=AW)
            own3 = own[:, :].rearrange("p (w h) -> p w h", h=H)
            yt = sacc.sb("yt", [P, NP])
            with Stage(nc, "l1j") as sj:
                v = sj.sb("v", [P, NW, D])
                none = sj.sb("none", [P, NW])
                top = sj.sb("top", [P, NW, H])
                mx = sj.sb("mx", [P, NW, H])
                den = sj.sb("den", [P, NW, H])
                ld, dv, ready, expd = sem("l1j_ld"), sem("l1j_dv"), sem("l1j_ready"), sem("l1j_exp")
                with nc.Block() as block:
                    @block.sync
                    def _(sp):
                        sp.dma_start(v[:, :, :], g.pair_d[:, 0:D].rearrange("(w p) f -> p w f", p=P)).then_inc(ld, 16)

                    @block.scalar
                    def _(act):
                        act.wait_ge(ready, 2)
                        nc.scalar.activation(top[:, :, :], top[:, :, :], ACT.Exp).then_inc(expd, 1)
                        nc.scalar.activation(own3, own3, ACT.Exp).then_inc(expd, 1)

                    @block.vector
                    def _(dve):
                        c = Chain(dve, dv)
                        c.step(nc.vector.tensor_scalar(none[:, :], g.deg[:, :], 0.0, FAR, ALU.is_equal, ALU.mult))
                        c.step(nc.vector.tensor_tensor(top[:, :, :], acc3[:, :, D + H:],
                                                       none[:, :].unsqueeze(2).broadcast_to([P, NW, H]), ALU.add))
                        c.step(nc.vector.tensor_tensor(mx[:, :, :], top[:, :, :], own3, ALU.max))
                        nc.vector.tensor_tensor(top[:, :, :], top[:, :, :], mx[:, :, :], ALU.subtract).then_inc(ready, 1)
                        nc.vector.tensor_tensor(own3, own3, mx[:, :, :], ALU.subtract).then_inc(ready, 1)
                        dve.wait_ge(expd, 2)
                        c.step(nc.vector.tensor_tensor(den[:, :, :], acc3[:, :, D:D + H], top[:, :, :], ALU.mult))
                        c.step(nc.vector.scalar_tensor_tensor(den[:, :, :], den[:, :, :], 1e-16, own3, ALU.add, ALU.add))
                        c.step(nc.vector.reciprocal(den[:, :, :], den[:, :, :]))
                        c.step(nc.vector.tensor_tensor(top[:, :, :], top[:, :, :], den[:, :, :], ALU.mult))
                        c.step(nc.vector.tensor_tensor(own3, own3, den[:, :, :], ALU.mult))
                        dve.wait_ge(ld, 16)
                        for h in range(H):
                            hs = slice(h * 16, (h + 1) * 16)
                            c.step(nc.vector.tensor_tensor(acc3[:, :, hs], acc3[:, :, hs],
                                                           top[:, :, h:h + 1].broadcast_to([P, NW, 16]), ALU.mult))
                            c.step(nc.vector.tensor_tensor(v[:, :, hs], v[:, :, hs],
                                                           own3[:, :, h:h + 1].broadcast_to([P, NW, 16]), ALU.mult))
                        c.step(nc.vector.tensor_tensor(acc3[:, :, 0:D], acc3[:, :, 0:D], v[:, :, :], ALU.add))
            with Stage(nc, "l1o") as so:
                wraw, w, ob = so.sb("wraw", [P, D]), so.sb("w", [P, D]), so.sb("ob", [P, 1])
                zc, hc, zt = so.sb("zc", [P, 2, D]), so.sb("hc", [P, 2, D]), so.sb("zt", [P, 2, D])
                pw = so.ps("pw")
                pt = [so.ps("pt0"), so.ps("pt1")]
                po = [so.ps("po0"), so.ps("po1")]
                ld, wt, wc, copied, turned, moved, mixed, taken = (
                    sem("l1o" + k) for k in ("_ld", "_wt", "_wc", "_copied", "_turned", "_moved", "_mixed", "_taken"))
                with nc.Block() as block:
                    @block.sync
                    def _(sp):
                        sp.dma_start(wraw[:, :], a["L1_gnn_out_w"]).then_inc(ld, 16)
                        sp.dma_start(ob[:, :], a["L1_gnn_out_b"].rearrange("(p o) -> p o", o=1)).then_inc(ld, 16)

                    @block.gpsimd
                    def _(pool):
                        with pool.Fori(0, NW // 2) as i:
                            for j in range(2):
                                v = 2 * i + j
                                pool.wait_ge(mixed, v + 1)
                                pool.nop(nofuse=True)
                                nc.gpsimd.tensor_copy(zc[:, j, :], acc[:, bass.ds(v * AW, D)]).then_inc(copied, 1)
                                nc.gpsimd.tensor_copy(hc[:, j, :], g.h[:, bass.ds(v * D, D)]).then_inc(copied, 1)

                    @block.scalar
                    def _(act):
                        with act.Fori(0, NW // 2) as i:
                            for j in range(2):
                                act.wait_ge(turned, 2 * i + j + 1)
                                act.nop(nofuse=True)
                                nc.scalar.copy(zt[:, j, :], pt[j][:, 0:D]).then_inc(moved, 1)

                    @block.tensor
                    def _(pe):
                        pe.sem_inc(mixed, 2)
                        pe.sem_inc(taken, 2)
                        pe.wait_ge(ld, 32)
                        nc.tensor.transpose(pw[:, 0:D], wraw[:, :], g.ident[:, :]).then_inc(wt, 1)
                        pe.wait_ge(wc, 1)
                        with pe.Fori(0, NW // 2) as i:
                            for j in range(2):
                                pe.wait_ge(copied, 4 * i + 2 * j + 2)
                                nc.tensor.transpose(pt[j][:, 0:D], zc[:, j, :], g.ident[:, :]).then_inc(turned, 1)
                            for j in range(2):
                                pe.wait_ge(moved, 2 * i + j + 1)
                                pe.wait_ge(taken, 2 * i + j + 1)
                                nc.tensor.matmul(po[j][:, 0:D], w[:, :], zt[:, j, :], start=True, stop=False)
                                nc.tensor.matmul(po[j][:, 0:D], hc[:, j, :], g.ident[:, :],
                                                 start=False, stop=True).then_inc(mixed, 1)

                    @block.vector
                    def _(dve):
                        dve.wait_ge(wt, 1)
                        nc.vector.tensor_copy(w[:, :], pw[:, 0:D]).then_inc(wc, 1)
                        with dve.Fori(0, NW // 2) as i:
                            for j in range(2):
                                v = 2 * i + j
                                dve.wait_ge(mixed, v + 3)
                                nc.vector.tensor_scalar(yt[:, bass.ds(v * D, D)], po[j][:, 0:D], ob[:, 0:1], None,
                                                        ALU.add).then_inc(taken, 1)
            CH = 400
            NCH = NP // CH
            K = FF // P
            with Stage(nc, "l1f") as sf:
                junk = sf.sb("junk", [P, NP])
                w1r, w2r = sf.sb("w1r", [P, K, D]), sf.sb("w2r", [P, FF])
                w1, w2 = sf.sb("w1", [P, K, P]), sf.sb("w2", [P, K, D])
                vec = sf.sb("vec", [P, 5])
                b1 = sf.sb("b1", [P, K])
                stats, stats2 = sf.sb("stats", [P, 8]), sf.sb("stats2", [P, 8])
                x1 = sf.sb("x1", [P, CH])
                z, ff = sf.sb("z", [P, K, CH]), sf.sb("ff", [P, K, CH])
                yc, pbk = sf.sb("yc", [P, 2, D]), [sf.ps("pb0"), sf.ps("pb1")]
                pz = sf.ps("pz", (P, K, 512))
                po = sf.ps("po")
                pw = sf.ps("pw")
                (ld, wt, wc, dv, ask, got, x1_ready, hidden, biased, leaked, summed, normed, turned, taken, dv_done) = (
                    sem("l1f" + k) for k in ("_ld", "_wt", "_wc", "_dv", "_ask", "_got", "_x1", "_hid", "_bias", "_leak",
                                             "_sum", "_norm", "_turned", "_taken", "_dvd"))
                with nc.Block() as block:
                    @block.sync
                    def _(sp):
                        sp.dma_start(w1r[:, :, :], a["L1_gnn_lin1_w"].rearrange("(k p) f -> p k f", p=P)).then_inc(ld, 16)
                        sp.dma_start(w2r[:, :], a["L1_gnn_lin2_w"]).then_inc(ld, 16)
                        for k, n_ in enumerate(("g1", "b1", "lin2_b", "g2", "b2")):
                            sp.dma_start(vec[:, k:k + 1], a["L1_gnn_" + n_].rearrange("(p o) -> p o", o=1)).then_inc(ld, 16)
                        sp.dma_start(b1[:, :], a["L1_gnn_lin1_b"].rearrange("(k p) -> p k", p=P),
                                     allow_slow_non_contiguous=True).then_inc(ld, 16)

                    @block.scalar
                    def _(act):
                        act.wait_ge(ld, 128)
                        batch_norm_squares(nc, act, yt, junk, stats, ask, got, 0)
                        with act.Fori(0, NCH) as i:
                            act.wait_ge(hidden, i + 1)
                            for k in range(K):
                                ins = nc.scalar.activation(z[:, k, :], pz[:, k, 0:CH], ACT.Identity, bias=b1[:, k:k + 1])
                            ins.then_inc(biased, 1)
                        batch_norm_squares(nc, act, yt, junk, stats2, ask, got, 1)
                        act.wait_ge(dv_done, 1)
                        act.sem_inc(turned, 2)
                        with act.Fori(0, NW // 2) as i:
                            for j in range(2):
                                v = 2 * i + j
                                act.wait_ge(turned, v + 1)
                                act.nop(nofuse=True)
                                nc.scalar.activation(yc[:, j, :], yt[:, bass.ds(v * D, D)], ACT.Identity,
                                                     bias=stats2[:, 1:2], scale=stats2[:, 0:1]).then_inc(normed, 1)

                    @block.tensor
                    def _(pe):
                        pe.wait_ge(ld, 128)
                        for k in range(K):
                            mm = nc.tensor.transpose(pw[:, k * P:(k + 1) * P], w1r[:, k, :], g.ident[:, :])
                        mm.then_inc(wt, 1)
                        for k in range(K):
                            mm = nc.tensor.transpose(pz[:, 0, k * P:(k + 1) * P], w2r[:, k * P:(k + 1) * P], g.ident[:, :])
                        mm.then_inc(wt, 1)
                        pe.wait_ge(wc, 2)
                        with pe.Fori(0, NCH) as i:
                            pe.wait_ge(x1_ready, i + 1)
                            for k in range(K):
                                mm = nc.tensor.matmul(pz[:, k, 0:CH], w1[:, k, :], x1[:, :], start=True, stop=True)
                            mm.then_inc(hidden, 1)
                            pe.wait_ge(leaked, i + 1)
                            for k in range(K):
                                mm = nc.tensor.matmul(po[:, 0:CH], w2[:, k, :], ff[:, k, :],
                                                      start=(k == 0), stop=(k == K - 1))
                            mm.then_inc(summed, 1)
                        pe.sem_inc(taken, 2)
                        with pe.Fori(0, NW // 2) as i:
                            for j in range(2):
                                pe.wait_ge(normed, 2 * i + j + 1)
                                pe.wait_ge(taken, 2 * i + j + 1)
                                nc.tensor.transpose(pbk[j][:, 0:D], yc[:, j, :], g.ident[:, :]).then_inc(turned, 1)

                    @block.vector
                    def _(dve):
                        c = Chain(dve, dv)
                        dve.wait_ge(wt, 1)
                        nc.vector.tensor_copy(w1[:, :, :].rearrange("p k f -> p (k f)"), pw[:, :]).then_inc(wc, 1)
                        dve.wait_ge(wt, 2)
                        nc.vector.tensor_copy(w2[:, :, :].rearrange("p k f -> p (k f)"), pz[:, 0, :]).then_inc(wc, 1)
                        dve.wait_ge(ld, 128)
                        batch_norm(nc, g, c, dve, yt, stats, vec[:, 0:1], vec[:, 1:2], ask, got, 0)
                        base = c.n
                        with dve.Fori(0, NCH) as i:
                            c.n = base + i
                            yv = yt[:, bass.ds(i * CH, CH)]
                            nc.vector.tensor_scalar(x1[:, :], yv, stats[:, 0:1], stats[:, 1:2], ALU.mult,
                                                    ALU.add).then_inc(x1_ready, 1)
                            dve.wait_ge(biased, i + 1)
                            nc.vector.scalar_tensor_tensor(ff[:, :, :], z[:, :, :], 0.01, z[:, :, :],
                                                           ALU.mult, ALU.max).then_inc(leaked, 1)
                            dve.wait_ge(summed, i + 1)
                            c.step(nc.vector.scalar_tensor_tensor(yv, po[:, 0:CH], vec[:, 2:3], x1[:, :],
                                                                  ALU.add, ALU.add))
                        c.n = base + NCH
                        batch_norm(nc, g, c, dve, yt, stats2, vec[:, 3:4], vec[:, 4:5], ask, got, 1)
                        nc.vector.engine_nop().then_inc(dv_done, 1)
                        with dve.Fori(0, NW // 2) as i:
                            for j in range(2):
                                v = 2 * i + j
                                dve.wait_ge(turned, v + 3)
                                xv = g.x[:, bass.ds(v * D, D)]
                                nc.vector.tensor_tensor(xv, xv, pbk[j][:, 0:D], ALU.add).then_inc(taken, 1)


def layer2(nc, g, sem, a):
    with Stage(nc, "l2") as st:
        acc = st.sb("acc", [P, NW * HID])
        with Stage(nc, "l2a") as s1:
            w, root, bias = s1.sb("w", [P, RELS, HID]), s1.sb("root", [P, HID]), s1.sb("bias", [P, HID])
            hc, ht = s1.sb("hc", [P, 2, D]), s1.sb("ht", [P, 2, D])
            msg = s1.sb("msg", [P, 2, RELS * HID])
            pt = s1.ps("pt")
            pr = s1.ps("pr")
            pm = s1.ps("pm", (P, 4, 512))
            ld, copied, turned, moved, mult, tk_a, tk_d, rooted, rtaken, stored0, stored1 = (
                sem("l2a" + k) for k in ("_ld", "_copied", "_turned", "_moved", "_mult", "_tka", "_tkd", "_root",
                                         "_rtk", "_st0", "_st1"))
            stored = [stored0, stored1]
            with nc.Block() as block:
                @block.sync
                def _(sp):
                    sp.dma_start(w[:, :, :], a["L2_gnn_W1"].rearrange("r i o -> i r o")).then_inc(ld, 16)
                    sp.dma_start(root[:, :], a["L2_gnn_root1"]).then_inc(ld, 16)
                    sp.dma_start(bias[:, :], a["L2_gnn_b1"].partition_broadcast(P)).then_inc(ld, 16)
                    for j in range(2):
                        sp.sem_inc(stored[j], 16)
                    with sp.Fori(0, NW // 2) as i:
                        for j in range(2):
                            v = 2 * i + j
                            sp.wait_ge(tk_a, 2 * v + 4)
                            sp.wait_ge(tk_d, 2 * v + 4)
                            sp.dma_start(g.msg1_d[bass.ds(v * P, P), :], msg[:, j, :]).then_inc(stored[j], 16)
                    for j in range(2):
                        sp.wait_ge(stored[j], 16 + 8 * NW)

                @block.gpsimd
                def _(pool):
                    window_copies(nc, pool, g.h, lambda j: hc[:, j, :], turned, copied)

                @block.scalar
                def _(act):
                    act.sem_inc(tk_a, 2)
                    with act.Fori(0, NW // 2) as i:
                        for j in range(2):
                            v = 2 * i + j
                            act.wait_ge(turned, v + 3)
                            act.nop(nofuse=True)
                            nc.scalar.copy(ht[:, j, :], pt[:, j * D:(j + 1) * D]).then_inc(moved, 1)
                            act.wait_ge(stored[j], 16 * i + 16)
                            act.nop(nofuse=True)
                            for b in range(2):
                                act.wait_ge(mult, 4 * v + b + 1)
                                nc.scalar.copy(msg[:, j, b * 512:(b + 1) * 512], pm[:, b, :]).then_inc(tk_a, 1)

                @block.tensor
                def _(pe):
                    pe.sem_inc(turned, 2)
                    pe.wait_ge(ld, 48)
                    with pe.Fori(0, NW // 2) as i:
                        for j in range(2):
                            v = 2 * i + j
                            pe.wait_ge(copied, v + 1)
                            nc.tensor.transpose(pt[:, j * D:(j + 1) * D], hc[:, j, :], g.ident[:, :]).then_inc(turned, 1)
                            pe.wait_ge(moved, v + 1)
                            pe.wait_ge(rtaken, v + 1)
                            nc.tensor.matmul(pr[:, 0:HID], ht[:, j, :], root[:, :], start=True,
                                             stop=True).then_inc(rooted, 1)
                            for b in range(4):
                                pe.wait_ge(tk_a if b < 2 else tk_d, 2 * v + b % 2 + 1)
                                mm = nc.tensor.matmul(pm[:, b, :], ht[:, j, :], w[:, 2 * b:2 * b + 2, :]
                                                      .rearrange("p r o -> p (r o)"), start=True, stop=True)
                                mm.then_inc(mult, 1)

                @block.vector
                def _(dve):
                    nc.vector.engine_nop().then_inc(rtaken, 1)
                    for _ in range(2):
                        nc.vector.engine_nop().then_inc(tk_d, 1)
                    dve.wait_ge(ld, 48)
                    with dve.Fori(0, NW // 2) as i:
                        for j in range(2):
                            v = 2 * i + j
                            hv = acc[:, bass.ds(v * HID, HID)]
                            dve.wait_ge(rooted, v + 1)
                            nc.vector.tensor_tensor(hv, pr[:, 0:HID], bias[:, :], ALU.add).then_inc(rtaken, 1)
                            dve.wait_ge(stored[j], 16 * i + 16)
                            for b in range(2):
                                dve.wait_ge(mult, 4 * v + b + 3)
                                nc.vector.tensor_copy(msg[:, j, (2 + b) * 512:(3 + b) * 512],
                                                      pm[:, 2 + b, :]).then_inc(tk_d, 1)
        gather_sum(nc, g, sem, "l2e", g.msg1_d.rearrange("n (r f) -> (n r) f", r=RELS), g.msg_i, HID, acc, HID,
                   coef=g.coef)
        with Stage(nc, "l2b") as s2:
            w, root, bias = s2.sb("w", [P, 2, RELS, D]), s2.sb("root", [P, 2, D]), s2.sb("bias", [P, D])
            hc, ht = s2.sb("hc", [P, 2, HID]), s2.sb("ht", [P, 2, HID])
            msg = s2.sb("msg", [P, 2, RELS * D])
            pt = [s2.ps("pt0"), s2.ps("pt1")]
            pr = s2.ps("pr")
            pm = s2.ps("pm", (P, 2, 512))
            ld, copied, turned, moved, mult, tk_a, tk_d, rooted, rtaken, stored0, stored1 = (
                sem("l2b" + k) for k in ("_ld", "_copied", "_turned", "_moved", "_mult", "_tka", "_tkd", "_root",
                                         "_rtk", "_st0", "_st1"))
            stored = [stored0, stored1]
            with nc.Block() as block:
                @block.sync
                def _(sp):
                    for k in range(2):
                        sp.dma_start(w[:, k, :, :], a["L2_gnn_W2"][:, k * P:(k + 1) * P, :].rearrange("r i o -> i r o")) \
                            .then_inc(ld, 16)
                        sp.dma_start(root[:, k, :], a["L2_gnn_root2"][k * P:(k + 1) * P, :]).then_inc(ld, 16)
                    sp.dma_start(bias[:, :], a["L2_gnn_b2"].partition_broadcast(P)).then_inc(ld, 16)
                    for j in range(2):
                        sp.sem_inc(stored[j], 16)
                    with sp.Fori(0, NW // 2) as i:
                        for j in range(2):
                            v = 2 * i + j
                            sp.wait_ge(tk_a, v + 2)
                            sp.wait_ge(tk_d, v + 2)
                            sp.dma_start(g.msg2_d[bass.ds(v * P, P), :], msg[:, j, :]).then_inc(stored[j], 16)
                    for j in range(2):
                        sp.wait_ge(stored[j], 16 + 8 * NW)

                @block.gpsimd
                def _(pool):
                    with pool.Fori(0, NW // 2) as i:
                        for j in range(2):
                            v = 2 * i + j
                            pool.wait_ge(turned, v + 1)
                            pool.nop(nofuse=True)
                            nc.gpsimd.tensor_copy(hc[:, j, :], acc[:, bass.ds(v * HID, HID)]).then_inc(copied, 1)

                @block.scalar
                def _(act):
                    act.sem_inc(tk_a, 1)
                    with act.Fori(0, NW // 2) as i:
                        for j in range(2):
                            v = 2 * i + j
                            act.wait_ge(turned, v + 3)
                            act.nop(nofuse=True)
                            nc.scalar.activation(ht[:, j, :], pt[j][:, 0:HID], ACT.Relu).then_inc(moved, 1)
                            act.wait_ge(stored[j], 16 * i + 16)
                            act.wait_ge(mult, 2 * v + 1)
                            act.nop(nofuse=True)
                            nc.scalar.copy(msg[:, j, 0:512], pm[:, 0, :]).then_inc(tk_a, 1)

                @block.tensor
                def _(pe):
                    pe.sem_inc(turned, 2)
                    pe.wait_ge(ld, 80)
                    with pe.Fori(0, NW // 2) as i:
                        for j in range(2):
                            v = 2 * i + j
                            pe.wait_ge(copied, v + 1)
                            for k in range(2):
                                mm = nc.tensor.transpose(pt[j][:, k * P:(k + 1) * P], hc[:, j, k * P:(k + 1) * P],
                                                         g.ident[:, :])
                            mm.then_inc(turned, 1)
                            pe.wait_ge(moved, v + 1)
                            pe.wait_ge(rtaken, v + 1)
                            for k in range(2):
                                mm = nc.tensor.matmul(pr[:, 0:D], ht[:, j, k * P:(k + 1) * P], root[:, k, :],
                                                      start=(k == 0), stop=(k == 1))
                            mm.then_inc(rooted, 1)
                            for b in range(2):
                                pe.wait_ge(tk_a if b == 0 else tk_d, v + 1)
                                for k in range(2):
                                    mm = nc.tensor.matmul(pm[:, b, :], ht[:, j, k * P:(k + 1) * P],
                                                          w[:, k, 4 * b:4 * b + 4, :].rearrange("p r o -> p (r o)"),
                                                          start=(k == 0), stop=(k == 1))
                                mm.then_inc(mult, 1)

                @block.vector
                def _(dve):
                    nc.vector.engine_nop().then_inc(rtaken, 1)
                    nc.vector.engine_nop().then_inc(tk_d, 1)
                    dve.wait_ge(ld, 80)
                    with dve.Fori(0, NW // 2) as i:
                        for j in range(2):
                            v = 2 * i + j
                            xv = g.x[:, bass.ds(v * D, D)]
                            dve.wait_ge(rooted, v + 1)
                            nc.vector.tensor_tensor(xv, xv, pr[:, 0:D], ALU.add).then_inc(rtaken, 1)
                            dve.wait_ge(rtaken, v + 2)
                            nc.vector.tensor_tensor(xv, xv, bias[:, :], ALU.add)
                            dve.wait_ge(stored[j], 16 * i + 16)
                            dve.wait_ge(mult, 2 * v + 2)
                            nc.vector.tensor_copy(msg[:, j, 512:], pm[:, 1, :]).then_inc(tk_d, 1)
        gather_sum(nc, g, sem, "l2f", g.msg2_d.rearrange("n (r f) -> (n r) f", r=RELS), g.msg_i, D, g.x, D,
                   coef=g.coef)


def layer3(nc, g, sem, a):
    H = 2
    AW = D + H
    with Stage(nc, "l3") as st:
        acc = st.sb("acc", [P, NW * AW])
        attention(nc, g, sem, "l3t", H, H, D, [a["L3_gnn_Wv"], a["L3_gnn_Wk"], a["L3_gnn_Wq"]],
                  [a["L3_gnn_bv"], a["L3_gnn_bk"], a["L3_gnn_bq"]], False, 64.0 ** -0.5, None, acc, AW)
        acc3 = acc[:, :].rearrange("p (w f) -> p w f", f=AW)
        with Stage(nc, "l3o") as so:
            den = so.sb("den", [P, NW, H])
            wskip, wg, wf = so.sb("wskip", [P, D]), so.sb("wg", [P, 2, D]), so.sb("wf", [P, D])
            bs = so.sb("bs", [P, 1])
            zc, hc = so.sb("zc", [P, 2, D]), so.sb("hc", [P, 2, D])
            ht, xt = so.sb("ht", [P, 2, D]), so.sb("xt", [P, 2, D])
            gate, fuse = so.sb("gate", [P, 2, D]), so.sb("fuse", [P, 2, D])
            pt = [so.ps("pt0"), so.ps("pt1")]
            px = [so.ps("px0"), so.ps("px1")]
            pg = [so.ps("pg0"), so.ps("pg1")]
            ld, dv, scaled, copied, turned, moved, mixed, biased, gated, acted, joined = (
                sem("l3o" + k) for k in ("_ld", "_dv", "_scaled", "_copied", "_turned", "_moved", "_mixed", "_biased",
                                         "_gated", "_acted", "_joined"))
            with nc.Block() as block:
                @block.sync
                def _(sp):
                    sp.dma_start(wskip[:, :], a["L3_gnn_Wskip"]).then_inc(ld, 16)
                    sp.dma_start(wg[:, :, :], a["L3_gnn_Wgate"].rearrange("(k p) f -> p k f", p=P)).then_inc(ld, 16)
                    sp.dma_start(wf[:, :], a["L3_gnn_Wfuse"]).then_inc(ld, 16)
                    sp.dma_start(bs[:, :], a["L3_gnn_bskip"].rearrange("(p o) -> p o", o=1)).then_inc(ld, 16)

                @block.gpsimd
                def _(pool):
                    pool.wait_ge(scaled, 1)
                    with pool.Fori(0, NW // 2) as i:
                        for j in range(2):
                            v = 2 * i + j
                            pool.wait_ge(mixed, v + 1)
                            pool.nop(nofuse=True)
                            nc.gpsimd.tensor_copy(zc[:, j, :], acc[:, bass.ds(v * AW, D)]).then_inc(copied, 1)
                            nc.gpsimd.tensor_copy(hc[:, j, :], g.h[:, bass.ds(v * D, D)]).then_inc(copied, 1)

                @block.scalar
                def _(act):
                    act.wait_ge(ld, 64)
                    with act.Fori(0, NW // 2) as i:
                        for j in range(2):
                            v = 2 * i + j
                            act.wait_ge(turned, v + 1)
                            act.wait_ge(gated, v + 1)
                            act.nop(nofuse=True)
                            nc.scalar.copy(ht[:, j, :], pt[j][:, 0:D]).then_inc(moved, 1)
                        for j in range(2):
                            v = 2 * i + j
                            act.wait_ge(mixed, v + 3)
                            act.nop(nofuse=True)
                            nc.scalar.activation(xt[:, j, :], px[j][:, 0:D], ACT.Identity, bias=bs[:, 0:1]) \
                                .then_inc(biased, 1)
                        for j in range(2):
                            v = 2 * i + j
                            act.wait_ge(gated, v + 3)
                            act.wait_ge(joined, v + 1)
                            act.nop(nofuse=True)
                            nc.scalar.activation(gate[:, j, :], pg[j][:, 0:D], ACT.Sigmoid).then_inc(acted, 1)
                            nc.scalar.activation(fuse[:, j, :], pg[j][:, D:2 * D], ACT.Tanh).then_inc(acted, 1)

                @block.tensor
                def _(pe):
                    pe.sem_inc(mixed, 2)
                    pe.sem_inc(gated, 2)
                    pe.sem_inc(joined, 2)
                    pe.sem_inc(acted, 4)
                    pe.wait_ge(ld, 64)
                    with pe.Fori(0, NW // 2) as i:
                        for j in range(2):
                            v = 2 * i + j
                            pe.wait_ge(copied, 2 * v + 2)
                            nc.tensor.transpose(pt[j][:, 0:D], hc[:, j, :], g.ident[:, :]).then_inc(turned, 1)
                        for j in range(2):
                            v = 2 * i + j
                            pe.wait_ge(moved, v + 1)
                            nc.tensor.matmul(px[j][:, 0:D], wskip[:, :], ht[:, j, :], start=True, stop=False)
                            nc.tensor.matmul(px[j][:, 0:D], zc[:, j, :], g.ident[:, :],
                                             start=False, stop=True).then_inc(mixed, 1)
                        for j in range(2):
                            v = 2 * i + j
                            pe.wait_ge(biased, v + 1)
                            pe.wait_ge(acted, 2 * v + 2)
                            nc.tensor.matmul(pg[j][:, 0:D], ht[:, j, :], wg[:, 0, :], start=True, stop=False)
                            nc.tensor.matmul(pg[j][:, 0:D], xt[:, j, :], wg[:, 1, :], start=False, stop=True)
                            nc.tensor.matmul(pg[j][:, D:2 * D], xt[:, j, :], wf[:, :], start=True,
                                             stop=True).then_inc(gated, 1)

                @block.vector
                def _(dve):
                    c = Chain(dve, dv)
                    c.step(nc.vector.tensor_scalar(den[:, :, :], acc3[:, :, D:], 0.5, None, ALU.max))
                    c.step(nc.vector.reciprocal(den[:, :, :], den[:, :, :]))
                    for h in range(H):
                        hs = slice(h * 64, (h + 1) * 64)
                        c.step(nc.vector.tensor_tensor(acc3[:, :, hs], acc3[:, :, hs],
                                                       den[:, :, h:h + 1].broadcast_to([P, NW, 64]), ALU.mult))
                    nc.vector.engine_nop().then_inc(scaled, 1)
                    base = c.n
                    with dve.Fori(0, NW // 2) as i:
                        for j in range(2):
                            v = 2 * i + j
                            c.n = base + 6 * i + 3 * j
                            hv, xv = g.h[:, bass.ds(v * D, D)], g.x[:, bass.ds(v * D, D)]
                            dve.wait_ge(acted, 2 * v + 6)
                            c.step(nc.vector.tensor_tensor(fuse[:, j, :], fuse[:, j, :], hv, ALU.subtract))
                            c.step(nc.vector.tensor_tensor(fuse[:, j, :], fuse[:, j, :], gate[:, j, :], ALU.mult))
                            c.step(nc.vector.tensor_tensor(fuse[:, j, :], fuse[:, j, :], hv, ALU.add))
                            nc.vector.tensor_tensor(xv, xv, fuse[:, j, :], ALU.add).then_inc(joined, 1)


class Held:
    pass


def gnn_stack(nc, a, out):
    with ExitStack() as ctx:
        sem = Semaphores(nc)

        def sb(name, shape, dt=F32):
            return ctx.enter_context(nc.sbuf_tensor(name, shape, dt))

        g = Held()
        g.iota_i, g.tile_i = sb("iota_i", [P, P], I32), sb("tile_i", [P, TB], I32)
        g.iota, g.tile_f = sb("iota", [P, P]), sb("tile_f", [P, TB])
        g.ident, g.ones = sb("ident", [P, P]), sb("ones", [P, P])
        g.x, g.h = sb("x", [P, NP]), sb("h", [P, NP])
        g.src_i, g.msg_i = sb("src_i", [P, TA], I32), sb("msg_i", [P, TA], I32)
        g.dloc, g.rel, g.coef = sb("dloc", [P, TA]), sb("rel", [P, TA]), sb("coef", [P, TA])
        g.cut_src_i, g.cut_dloc, g.cut_rel = sb("cut_src_i", [P, TA], I32), sb("cut_dloc", [P, TA]), sb("cut_rel", [P, TA])
        g.edges_d = nc.dram_tensor("edges_d", (3, E + P), I32, kind="Internal").ap()
        g.rows = sb("rows", [1, 2 * TA], I32)
        g.outdeg, g.deg = sb("outdeg", [P, NW]), sb("deg", [P, NW])
        g.count = sb("count", [P, NW * RELS])
        g.rows_d = nc.dram_tensor("rows_d", (1, 2 * TA), I32, kind="Internal").ap()
        g.keys_d = nc.dram_tensor("keys_d", (P + T * P + P,), F32, kind="Internal").ap()
        g.node_d = nc.dram_tensor("node_d", (NP, D), F32, kind="Internal").ap()
        g.pair_d = nc.dram_tensor("pair_d", (NP, 2 * D), F32, kind="Internal").ap()
        g.spill_d = nc.dram_tensor("spill_d", (T * P, D), F32, kind="Internal").ap()
        g.t1_d, g.t2_d, g.t3_d = (nc.dram_tensor(f"t{k}_d", (T * P * RELS,), F32, kind="Internal").ap()
                                  for k in (1, 2, 3))
        g.msg1_d = nc.dram_tensor("msg1_d", (NP, RELS * HID), F32, kind="Internal").ap()
        g.msg2_d = nc.dram_tensor("msg2_d", (NP, RELS * D), F32, kind="Internal").ap()
        constants(nc, g, sem)
        ld = sem("x_ld")
        with nc.Block() as block:
            @block.vector
            def _(dve):
                nc.vector.memset(g.x[:, LASTW * D:], 0.0).then_inc(ld, 16)

            @block.sync
            def _(sp):
                sp.dma_start(g.x[:, 0:LASTW * D].rearrange("p (w f) -> p w f", f=D),
                             a["x"][0:LASTW * P, :].rearrange("(w p) f -> p w f", p=P)).then_inc(ld, 16)
                sp.wait_ge(ld, 32)
                sp.dma_start(g.x[0:REST, LASTW * D:(LASTW + 1) * D], a["x"][LASTW * P:N, :]).then_inc(ld, 16)
                sp.wait_ge(ld, 48)
        tile_tables(nc, g, sem, a["src"], a["dst"], a["edge_type_8"])
        out_degrees(nc, g, sem, a["src"])
        layer_norm(nc, g, sem, "ln0")
        layer0(nc, g, sem, a)
        sem.give_back()
        layer_norm(nc, g, sem, "ln1")
        layer1(nc, g, sem, a)
        sem.give_back()
        layer_norm(nc, g, sem, "ln2")
        layer2(nc, g, sem, a)
        sem.give_back()
        layer_norm(nc, g, sem, "ln3")
        layer3(nc, g, sem, a)
        done = sem("out_done")
        with nc.Block() as block:
            @block.sync
            def _(sp):
                sp.dma_start(out[0:LASTW * P, :].rearrange("(w p) f -> p w f", p=P),
                             g.x[:, 0:LASTW * D].rearrange("p (w f) -> p w f", f=D)).then_inc(done, 16)
                sp.dma_start(out[LASTW * P:N, :], g.x[0:REST, LASTW * D:(LASTW + 1) * D]).then_inc(done, 16)
                sp.wait_ge(done, 32)


_INS = ["x", "src", "dst", "edge_attr_128", "edge_type_8", "L0_gnn_W", "L0_gnn_b", "L0_gnn_We", "L0_gnn_be", "L1_gnn_q_w", "L1_gnn_q_b", "L1_gnn_k_w", "L1_gnn_v_w", "L1_gnn_out_w", "L1_gnn_out_b", "L1_gnn_g1", "L1_gnn_b1", "L1_gnn_lin1_w", "L1_gnn_lin1_b", "L1_gnn_lin2_w", "L1_gnn_lin2_b", "L1_gnn_g2", "L1_gnn_b2", "L2_gnn_W1", "L2_gnn_root1", "L2_gnn_b1", "L2_gnn_W2", "L2_gnn_root2", "L2_gnn_b2", "L3_gnn_Wq", "L3_gnn_bq", "L3_gnn_Wk", "L3_gnn_bk", "L3_gnn_Wv", "L3_gnn_bv", "L3_gnn_Wskip", "L3_gnn_bskip", "L3_gnn_Wgate", "L3_gnn_Wfuse"]


def kernel(**inputs):
    import numpy as _np
    import concourse.bacc as _bacc
    from concourse import mybir as _mybir
    from concourse.bass_utils import run_bass_kernel_spmd as _run

    nc = _bacc.Bacc("TRN2", target_bir_lowering=False, num_devices=1)
    arrays, args = {}, {}
    for name in _INS:
        a = _np.ascontiguousarray(inputs[name])
        arrays[f"in_{name}_dram"] = a
        args[name] = nc.dram_tensor(f"in_{name}_dram", a.shape, _mybir.dt.from_np(a.dtype), kind="ExternalInput").ap()
    out = nc.dram_tensor("out_0_dram", (N, D), F32, kind="ExternalOutput").ap()
    gnn_stack(nc, args, out)
    r = _run(nc, [arrays], core_ids=[0])
    return r.results[0]["out_0_dram"]
```

```python
from contextlib import ExitStack

import concourse.bass as bass
from concourse import mybir

P = 128
D = 128
N = 6250
E = 100000
NW = 50
NP = NW * P
REST = N - (N // P) * P
LASTW = N // P
T = 832
TB = 7
TA = TB * P
EP, EC = 125, E // 125
RELS = 8
HID = 256
FF = 512
FAR = -1.0e30
EPS = 1e-5

F32 = mybir.dt.float32
BF16 = mybir.dt.bfloat16
I32 = mybir.dt.int32
ALU = mybir.AluOpType
ACT = mybir.ActivationFunctionType
X = mybir.AxisListType.X


class Chain:

    def __init__(self, eng, sem):
        self.eng, self.sem, self.n = eng, sem, 0

    def step(self, ins):
        ins.then_inc(self.sem, 1)
        self.n = self.n + 1
        self.eng.wait_ge(self.sem, self.n)


class Semaphores:

    def __init__(self, nc):
        self.nc, self.out = nc, []

    def __call__(self, name):
        self.out.append(self.nc.alloc_semaphore(name=name))
        return self.out[-1]

    def give_back(self):
        nc, out = self.nc, self.out
        with nc.Block() as block:
            @block.gpsimd
            def _(pool):
                nc.clear_and_free_semaphores(out)
        self.out = []


def windows_of(nc, g, engine, first, count=4, at=TA, top=NW - 1):
    _, values = nc.values_load_multi_w_load_instructions(
        g.rows[0:1, bass.ds(first + at, count)], engines=(engine,), min_val=0, max_val=top,
        skip_runtime_bounds_check_because="tile_tables clamps every entry to this range")
    return values


def view(tensor, offset, pattern):
    return bass.AP(tensor, offset, pattern)


class Stage:

    def __init__(self, nc, name):
        self.nc, self.name, self.ctx = nc, name, ExitStack()

    def __enter__(self):
        return self

    def __exit__(self, *a):
        self.ctx.close()

    def sb(self, name, shape, dt=F32):
        return self.ctx.enter_context(self.nc.sbuf_tensor(f"{self.name}_{name}", shape, dt))

    def ps(self, name, shape=(P, 512)):
        return self.ctx.enter_context(self.nc.psum_tensor(f"{self.name}_{name}", list(shape), F32))


def constants(nc, g, sem):
    made, dve_s = sem("const_made"), sem("const_dve")
    with nc.Block() as block:
        @block.gpsimd
        def _(pool):
            nc.gpsimd.iota(g.iota_i[:, :], [[1, P]], base=0, channel_multiplier=0).then_inc(made, 1)
            nc.gpsimd.iota(g.tile_i[:, :], [[P, TB]], base=0, channel_multiplier=1).then_inc(made, 1)
            nc.gpsimd.memset(g.ident[:, :], 0.0).then_inc(made, 1)
            pool.wait_ge(made, 3)
            nc.gpsimd.affine_select(out=g.ident[:, :], in_=g.ident[:, :], compare_op=ALU.not_equal, fill=1.0,
                                    base=0, pattern=[[-1, P]], channel_multiplier=1).then_inc(made, 1)

        @block.vector
        def _(dve):
            nc.vector.memset(g.ones[:, :], 1.0)
            dve.wait_ge(made, 2)
            nc.vector.tensor_copy(g.iota[:, :], g.iota_i[:, :])
            nc.vector.tensor_copy(g.tile_f[:, :], g.tile_i[:, :])


def tile_tables(nc, g, sem, dst):
    with Stage(nc, "tt") as st:
        dsti = st.sb("dsti", [EP, EC], I32)
        dstf = st.sb("dstf", [EP, EC])
        junk = st.sb("junk", [EP, EC])
        below = st.sb("below", [EP, NW + 1])
        first = st.sb("first", [P, NW + 1])
        cnti = st.sb("cnti", [P, NW], I32)
        ntile = st.sb("ntile", [P, NW])
        upto = st.sb("upto", [P, NW])
        tmp = st.sb("tmp", [P, NW])
        base = st.sb("base", [P, NW])
        win = st.sb("win", [P, TB])
        start = st.sb("start", [P, TB])
        cut = st.sb("cut", [P, TB])
        off = st.sb("off", [P, TB])
        cuti = st.sb("cuti", [P, TB], I32)
        starti = st.sb("starti", [P, TB], I32)
        padi = st.sb("padi", [1, 3, P], I32)
        wini = st.sb("wini", [P, TB], I32)
        raw = st.sb("raw", [P, 2 * TB, 3, P], I32)
        rawf = st.sb("rawf", [P, 2 * TB, 3, P])
        ok = st.sb("ok", [P, P])
        key = st.sb("key", [P, TB, P])
        pads = st.sb("pads", [1, P])
        ps = st.ps("ps")
        pt = [st.ps("pt0"), st.ps("pt1")]
        padded, padf = sem("tt_padded"), sem("tt_padf")
        ld, dv, mm = sem("tt_ld"), sem("tt_dv"), sem("tt_mm")
        counted, cut_ready, got, laid, turned, copied, out = (
            sem("tt_counted"), sem("tt_cut"), sem("tt_got"), sem("tt_laid"), sem("tt_turned"),
            sem("tt_copied"), sem("tt_out"))
        with nc.Block() as block:
            @block.sync
            def _(sp):
                sp.dma_start(dsti[:, :], dst.rearrange("(p c) -> p c", p=EP)).then_inc(ld, 16)
                sp.wait_ge(padf, 3)
                sp.dma_start(g.edges_d[:, E:E + P].unsqueeze(0), padi[:, :, :]).then_inc(padded, 16)
                sp.wait_ge(cut_ready, 1)
                sp.dma_start(view(g.rows_d.tensor, 0, [[1, P], [P, TB]]), cuti[:, :],
                             allow_slow_non_contiguous=True).then_inc(out, 16)
                sp.dma_start(view(g.rows_d.tensor, TA, [[1, P], [P, TB]]), wini[:, :],
                             allow_slow_non_contiguous=True).then_inc(out, 16)
                sp.wait_ge(out, 32)
                sp.dma_start(g.rows[:, :], g.rows_d).then_inc(out, 16)
                for b in range(TB):
                    sp.wait_ge(laid, TB + b + 1)
                    n = P if (b + 1) * P <= T else T - b * P
                    sp.dma_start(view(g.keys_d.tensor, P + b * P * P, [[P, n], [1, P]]),
                                 key[0:n, b, :]).then_inc(out, 16)
                sp.dma_start(view(g.keys_d.tensor, 0, [[P, 1], [1, P]]), pads[:, :]).then_inc(out, 16)
                sp.dma_start(view(g.keys_d.tensor, P + T * P, [[P, 1], [1, P]]), pads[:, :]).then_inc(out, 16)
                sp.wait_ge(out, 16 * (3 + TB + 2))

            @block.gpsimd
            def _(pool):
                pool.wait_ge(padded, 16)
                pool.wait_ge(cut_ready, 1)
                for b in range(2 * TB):
                    at = (cuti if b < TB else starti)[:, b % TB:b % TB + 1]
                    for k in range(3):
                        pool.indirect_dma_start(raw[:, b, k, :], None,
                                                g.edges_d.rearrange("k (e one) -> (k e) one", one=1),
                                                bass.IndirectOffsetOnAxis(at, 0),
                                                element_offset=k * (E + P)).then_inc(got, 16)

            @block.tensor
            def _(pe):
                pe.wait_ge(counted, 1)
                nc.tensor.matmul(ps[:, 0:NW + 1], g.ones[0:EP, :], below[:, :],
                                 start=True, stop=True).then_inc(mm, 1)
                for b in range(2 * TB):
                    pe.wait_ge(laid, b + 1)
                    if b >= 2:
                        pe.wait_ge(copied, b - 1)
                    for k in range(3):
                        t = nc.tensor.transpose(pt[b % 2][:, k * P:(k + 1) * P], rawf[:, b, k, :], g.ident[:, :])
                    t.then_inc(turned, 1)

            @block.vector
            def _(dve):
                c = Chain(dve, dv)
                nc.vector.memset(pads[:, :], -5.0)
                for k in range(3):
                    nc.vector.memset(padi[:, k, :], -1 if k == 1 else 0).then_inc(padf, 1)
                dve.wait_ge(ld, 16)
                c.step(nc.vector.tensor_copy(dstf[:, :], dsti[:, :]))
                for w in range(NW + 1):
                    ins = nc.vector.tensor_scalar(junk[:, :], dstf[:, :], float(P * w), None, ALU.is_lt, ALU.add,
                                                  accum_out=below[:, w:w + 1])
                    c.step(ins)
                nc.vector.engine_nop().then_inc(counted, 1)
                dve.wait_ge(mm, 1)
                c.step(nc.vector.tensor_copy(first[:, :], ps[:, 0:NW + 1]))
                c.step(nc.vector.tensor_tensor(tmp[:, :], first[:, 1:NW + 1], first[:, 0:NW], ALU.subtract))
                c.step(nc.vector.tensor_scalar(cnti[:, :], tmp[:, :], 127.0, None, ALU.add))
                c.step(nc.vector.tensor_scalar(cnti[:, :], cnti[:, :], 7, None, ALU.arith_shift_right))
                c.step(nc.vector.tensor_copy(ntile[:, :], cnti[:, :]))
                c.step(nc.vector.tensor_tensor_scan(upto[:, :], g.ones[:, 0:NW], ntile[:, :], 0.0,
                                                    ALU.mult, ALU.add))
                c.step(nc.vector.tensor_tensor(tmp[:, :], upto[:, :], ntile[:, :], ALU.subtract))
                c.step(nc.vector.scalar_tensor_tensor(base[:, :], tmp[:, :], -128.0, first[:, 0:NW],
                                                      ALU.mult, ALU.add))
                for b in range(TB):
                    t = g.tile_f[:, b:b + 1]
                    c.step(nc.vector.tensor_scalar(tmp[:, :], upto[:, :], t, None, ALU.is_le, ALU.add,
                                                   accum_out=win[:, b:b + 1]))
                    c.step(nc.vector.tensor_scalar(tmp[:, :], g.iota[:, 0:NW], win[:, b:b + 1], None, ALU.is_equal))
                    c.step(nc.vector.tensor_tensor(tmp[:, :], tmp[:, :], base[:, :], ALU.mult))
                    c.step(nc.vector.tensor_reduce(start[:, b:b + 1], tmp[:, :], X, ALU.add))
                c.step(nc.vector.scalar_tensor_tensor(start[:, :], g.tile_f[:, :], 128.0, start[:, :],
                                                      ALU.mult, ALU.add))
                c.step(nc.vector.tensor_scalar(cut[:, :], start[:, :], float(E - P), None, ALU.min))
                c.step(nc.vector.tensor_tensor(off[:, :], start[:, :], cut[:, :], ALU.subtract))
                c.step(nc.vector.tensor_scalar(win[:, :], win[:, :], float(NW - 1), None, ALU.min))
                c.step(nc.vector.tensor_scalar(start[:, :], start[:, :], float(E), None, ALU.min))
                c.step(nc.vector.tensor_copy(starti[:, :], start[:, :]))
                c.step(nc.vector.tensor_copy(cuti[:, :], cut[:, :]))
                c.step(nc.vector.tensor_scalar(tmp[:, 0:TB], win[:, :], -float(P), None, ALU.mult))
                nc.vector.tensor_copy(wini[:, :], win[:, :]).then_inc(cut_ready, 1)
                for b in range(2 * TB):
                    if b == 0:
                        dve.wait_ge(got, 16 * 6 * TB)
                    c.step(nc.vector.tensor_copy(rawf[:, b, :, :], raw[:, b, :, :]))
                    dl, key_b, u = rawf[:, b, 1, :], key[:, b % TB, :], b % TB
                    c.step(nc.vector.tensor_scalar(key_b, dl, 1.0, None, ALU.add))
                    c.step(nc.vector.tensor_scalar(dl, dl, tmp[:, u:u + 1], None, ALU.add))
                    if b < TB:
                        c.step(nc.vector.tensor_scalar(ok[:, :], g.iota[:, :], off[:, u:u + 1], None, ALU.is_ge))
                    else:
                        c.step(nc.vector.tensor_copy(ok[:, :], g.ones[:, :]))
                    c.step(nc.vector.scalar_tensor_tensor(ok[:, :], dl, 0.0, ok[:, :], ALU.is_ge, ALU.mult))
                    c.step(nc.vector.scalar_tensor_tensor(ok[:, :], dl, float(P), ok[:, :], ALU.is_lt, ALU.mult))
                    c.step(nc.vector.scalar_tensor_tensor(dl, dl, 1.0, ok[:, :], ALU.add, ALU.mult))
                    c.step(nc.vector.tensor_tensor(key_b, key_b, ok[:, :], ALU.mult))
                    c.step(nc.vector.tensor_scalar(dl, dl, -1.0, None, ALU.add))
                    nc.vector.tensor_scalar(key_b, key_b, -1.0, None, ALU.add).then_inc(laid, 1)
                for b in range(2 * TB):
                    bs = slice((b % TB) * P, (b % TB + 1) * P)
                    bank = pt[b % 2]
                    dve.wait_ge(turned, b + 1)
                    if b < TB:
                        c.step(nc.vector.tensor_copy(g.cut_src_i[:, bs], bank[:, 0:P]))
                        c.step(nc.vector.tensor_copy(g.cut_dloc[:, bs], bank[:, P:2 * P]))
                        nc.vector.tensor_copy(g.cut_rel[:, bs], bank[:, 2 * P:3 * P]).then_inc(copied, 1)
                    else:
                        c.step(nc.vector.tensor_copy(g.src_i[:, bs], bank[:, 0:P]))
                        c.step(nc.vector.tensor_copy(g.dloc[:, bs], bank[:, P:2 * P]))
                        c.step(nc.vector.tensor_copy(g.rel[:, bs], bank[:, 2 * P:3 * P]))
                        nc.vector.scalar_tensor_tensor(g.msg_i[:, bs], g.src_i[:, bs], float(RELS), g.rel[:, bs],
                                                       ALU.mult, ALU.add).then_inc(copied, 1)


def sort_edges(nc, g, sem, src, dst, etype, attr):
    CP, CC = 123, (E - 1) // 123
    LO, HI = P, NW
    S = 4
    with Stage(nc, "so") as st:
        here, there = st.sb("here", [CP, CC], I32), st.sb("there", [CP, CC], I32)
        heref, theref = st.sb("heref", [CP, CC]), st.sb("theref", [CP, CC])
        falls = st.sb("falls", [CP, 1])
        pay = st.sb("pay", [EP, EC, 4], I32)
        flat = st.sb("flat", [EP, 3, EC], I32)
        part = st.sb("part", [EP, EC], I32)
        digit, mask, run, pos, ones = (st.sb(k, [EP, EC]) for k in ("digit", "mask", "run", "pos", "ones"))
        posi = st.sb("posi", [EP, EC], I32)
        count, total, base = (st.sb(k, [EP, P]) for k in ("count", "total", "base"))
        before = st.sb("before", [EP, EP])
        pay_s, idx_s = st.sb("pay_s", [EP, S, 4], I32), st.sb("idx_s", [EP, S], I32)
        frow = st.sb("frow", [EP, S, D])
        ps, pb, pf = st.ps("ps"), st.ps("pb"), st.ps("pf")
        ld, copied, dv, fell, flagged, flag_set = (sem("so" + k) for k in ("_ld", "_copied", "_dv", "_fell", "_flagged", "_set"))
        pld, numbered, counted, mm, placed, staged, passed, out = (
            sem("so" + k) for k in ("_pld", "_numbered", "_counted", "_mm", "_placed", "_staged", "_passed", "_out"))
        sent = [[sem(f"so_sent{k}{s}") for s in range(S)] for k in range(2)]
        fetched = [sem(f"so_fetched{s}") for s in range(S)]
        kept = [sem(f"so_kept{s}") for s in range(S)]
        with nc.Block() as block:
            @block.sync
            def _(sp):
                sp.dma_start(here[:, :], dst[0:E - 1].rearrange("(p c) -> p c", p=CP)).then_inc(ld, 16)
                sp.dma_start(there[:, :], dst[1:E].rearrange("(p c) -> p c", p=CP)).then_inc(ld, 16)
                for k, one in enumerate((src, dst, etype)):
                    sp.dma_start(g.edges_d[k, 0:E].rearrange("(p c) -> p c", p=EP),
                                 one.rearrange("(p c) -> p c", p=EP)).then_inc(copied, 16)
                sp.wait_ge(copied, 48)

            @block.vector
            def _(dve):
                c = Chain(dve, dv)
                dve.wait_ge(ld, 32)
                c.step(nc.vector.tensor_copy(heref[:, :], here[:, :]))
                c.step(nc.vector.tensor_copy(theref[:, :], there[:, :]))
                c.step(nc.vector.tensor_tensor(heref[:, :], theref[:, :], heref[:, :], ALU.is_lt))
                nc.vector.tensor_reduce(falls[:, :], heref[:, :], X, ALU.add).then_inc(fell, 1)
                dve.wait_ge(flagged, 1)
                nc.vector.tensor_copy(g.unsorted[:, :], pf[0:1, 0:1])

            @block.tensor
            def _(pe):
                pe.wait_ge(fell, 1)
                nc.tensor.matmul(pf[0:1, 0:1], falls[:, :], g.ones[0:CP, 0:1], start=True, stop=True).then_inc(flagged, 1)

        with nc.Block() as block:
            @block.sync
            def _(sp):
                with sp.If(sp.value_load(g.unsorted[0:1, 0:1], min_val=0, max_val=E) > 0):
                    for k, one in enumerate((src, dst, etype)):
                        sp.dma_start(flat[:, k, :], one.rearrange("(p c) -> p c", p=EP)).then_inc(pld, 16)
                    sp.wait_ge(passed, 1)
                    sp.dma_start(pay[:, :, :], g.pass_d[0].rearrange("(p c) k -> p c k", p=EP)).then_inc(pld, 16)
                    sp.wait_ge(passed, 2)
                    sp.dma_start(pay[:, :, :], g.pass_d[1].rearrange("(p c) k -> p c k", p=EP)).then_inc(pld, 16)
                    sp.wait_ge(numbered, 3)
                    for k in range(3):
                        sp.dma_start(g.edges_d[k, 0:E].rearrange("(p c) -> p c", p=EP), flat[:, k, :]).then_inc(out, 16)
                    sp.wait_ge(out, 48)
                    with sp.Fori(0, EC // S) as i:
                        for s in range(S):
                            sp.wait_ge(fetched[s], 16 * (i + 1))
                            sp.dma_start(view(g.attr_d.tensor, (i * S + s) * D, [[EC * D, EP], [1, D]]),
                                         frow[:, s, :]).then_inc(kept[s], 16)
                    for s in range(S):
                        sp.wait_ge(kept[s], 16 * (EC // S))

            @block.vector
            def _(dve):
                with dve.If(dve.value_load(g.unsorted[0:1, 0:1], min_val=0, max_val=E) > 0):
                    c = Chain(dve, placed)
                    nc.vector.memset(ones[:, :], 1.0)
                    c.step(nc.vector.tensor_scalar(before[:, :], g.iota[0:EP, 0:EP], g.tile_f[0:EP, 0:1], None, ALU.is_gt))
                    dve.wait_ge(pld, 48)
                    dve.wait_ge(staged, 1)
                    for k in range(3):
                        c.step(nc.vector.tensor_copy(pay[:, :, k:k + 1], flat[:, k, :].unsqueeze(2)))
                    for turn in range(2):
                        bins = (LO, HI)[turn]
                        if turn:
                            dve.wait_ge(pld, 64)
                        col = pay[:, :, 1]
                        if turn == 0:
                            c.step(nc.vector.tensor_scalar(part[:, :], col, 127, None, ALU.bitwise_and))
                        else:
                            c.step(nc.vector.tensor_scalar(part[:, :], col, 7, None, ALU.arith_shift_right))
                        c.step(nc.vector.tensor_copy(digit[:, :], part[:, :]))
                        c.step(nc.vector.memset(count[:, :], 0.0))
                        first = c.n
                        with dve.Fori(0, bins) as b:
                            c.n = first + b
                            c.step(nc.vector.tensor_scalar(mask[:, :], digit[:, :], g.iota[0:EP, bass.ds(b, 1)], None,
                                                           ALU.is_equal, ALU.add, accum_out=count[:, bass.ds(b, 1)]))
                        c.n = first + bins
                        nc.vector.engine_nop().then_inc(counted, 1)
                        dve.wait_ge(mm, turn + 1)
                        c.step(nc.vector.tensor_copy(total[:, :], pb[0:EP, 0:P]))
                        c.step(nc.vector.tensor_tensor_scan(base[:, :], ones[:, 0:P], total[:, :], 0.0, ALU.mult, ALU.add))
                        c.step(nc.vector.tensor_tensor(base[:, :], base[:, :], total[:, :], ALU.subtract))
                        c.step(nc.vector.tensor_tensor(base[:, :], base[:, :], ps[0:EP, 0:P], ALU.add))
                        c.step(nc.vector.memset(pos[:, :], -1.0))
                        first = c.n
                        with dve.Fori(0, bins) as b:
                            c.n = first + 4 * b
                            c.step(nc.vector.tensor_scalar(mask[:, :], digit[:, :], g.iota[0:EP, bass.ds(b, 1)], None,
                                                           ALU.is_equal))
                            c.step(nc.vector.tensor_tensor_scan(run[:, :], ones[:, :], mask[:, :],
                                                                base[:, bass.ds(b, 1)], ALU.mult, ALU.add))
                            c.step(nc.vector.tensor_tensor(run[:, :], run[:, :], mask[:, :], ALU.mult))
                            c.step(nc.vector.tensor_tensor(pos[:, :], pos[:, :], run[:, :], ALU.add))
                        c.n = first + 4 * bins
                        nc.vector.tensor_copy(posi[:, :], pos[:, :]).then_inc(numbered, 1)
                    dve.wait_ge(pld, 80)
                    for k in range(3):
                        c.step(nc.vector.tensor_copy(flat[:, k, :].unsqueeze(2), pay[:, :, k:k + 1]))
                    nc.vector.tensor_copy(posi[:, :].unsqueeze(2), pay[:, :, 3:4]).then_inc(numbered, 1)

            @block.tensor
            def _(pe):
                with pe.If(pe.value_load(g.unsorted[0:1, 0:1], min_val=0, max_val=E) > 0):
                    for turn in range(2):
                        pe.wait_ge(counted, turn + 1)
                        nc.tensor.matmul(ps[0:EP, 0:P], before[:, :], count[:, :], start=True, stop=True)
                        nc.tensor.matmul(pb[0:EP, 0:P], g.ones[0:EP, 0:EP], count[:, :],
                                         start=True, stop=True).then_inc(mm, 1)

            @block.gpsimd
            def _(pool):
                with pool.If(pool.value_load(g.unsorted[0:1, 0:1], min_val=0, max_val=E) > 0):
                    nc.gpsimd.iota(pay[:, :, 3:4], [[1, EC], [0, 1]], base=0, channel_multiplier=EC).then_inc(staged, 1)

                    def stage(i, s):
                        nc.gpsimd.tensor_copy(idx_s[:, s:s + 1], posi[:, bass.ds(i * S + s, 1)]).then_inc(staged, 1)

                    for turn in range(2):
                        pool.wait_ge(numbered, turn + 1)
                        with pool.Fori(0, EC // S) as i:
                            for s in range(S):
                                stage(i, s)
                                nc.gpsimd.tensor_copy(pay_s[:, s, :], pay[:, bass.ds(i * S + s, 1), :]
                                                      .rearrange("p one k -> p (one k)")).then_inc(staged, 1)
                            pool.wait_ge(staged, 2 * turn * EC + 2 * S * (i + 1) + 1)
                            pool.nop(nofuse=True)
                            for s in range(S):
                                pool.indirect_dma_start(g.pass_d[turn],
                                                        bass.IndirectOffsetOnAxis(idx_s[:, s:s + 1], 0),
                                                        pay_s[:, s, :], None).then_inc(sent[turn][s], 16)
                            for s in range(S):
                                pool.wait_ge(sent[turn][s], 16 * (i + 1))
                                pool.nop(nofuse=True)
                        nc.gpsimd.memset(frow[0:1, 0, 0:1], 0.0).then_inc(passed, 1)
                    pool.wait_ge(numbered, 3)
                    with pool.Fori(0, EC // S) as i:
                        for s in range(S):
                            stage(i, s)
                        pool.wait_ge(staged, 4 * EC + S * (i + 1) + 1)
                        pool.nop(nofuse=True)
                        for s in range(S):
                            pool.indirect_dma_start(frow[:, s, :], None, attr,
                                                    bass.IndirectOffsetOnAxis(idx_s[:, s:s + 1], 0)).then_inc(fetched[s], 16)
                        for s in range(S):
                            pool.wait_ge(kept[s], 16 * (i + 1))
                            pool.nop(nofuse=True)


def out_degrees(nc, g, sem, src):
    W = 8
    with Stage(nc, "od") as st:
        si = st.sb("si", [EP, EC], I32)
        part = st.sb("part", [EP, EC], I32)
        lo = st.sb("lo", [EP, EC])
        hi = st.sb("hi", [EP, EC])
        low = st.sb("low", [EP, 2, W, P], BF16)
        high = st.sb("high", [EP, 2, W, NW], BF16)
        zero = st.sb("zero", [EP, P], BF16)
        ps = st.ps("ps")
        ld, dv, built, counted = sem("od_ld"), sem("od_dv"), sem("od_built"), sem("od_counted")
        groups = EC // W
        with nc.Block() as block:
            @block.sync
            def _(sp):
                sp.dma_start(si[:, :], src.rearrange("(p c) -> p c", p=EP)).then_inc(ld, 16)

            @block.vector
            def _(dve):
                c = Chain(dve, dv)
                nc.vector.memset(zero[:, :], 0.0)
                dve.wait_ge(ld, 16)
                c.step(nc.vector.tensor_scalar(part[:, :], si[:, :], 127, None, ALU.bitwise_and))
                c.step(nc.vector.tensor_copy(lo[:, :], part[:, :]))
                c.step(nc.vector.tensor_scalar(part[:, :], si[:, :], 7, None, ALU.arith_shift_right))
                c.step(nc.vector.tensor_copy(hi[:, :], part[:, :]))
                with dve.Fori(0, groups // 2) as i:
                    for s in range(2):
                        dve.wait_ge(counted, 2 * i + s + 1)
                        cols = bass.ds((2 * i + s) * W, W)
                        nc.vector.tensor_tensor(low[:, s, :, :], lo[:, cols].unsqueeze(2).broadcast_to([EP, W, P]),
                                                g.iota[0:EP, :].unsqueeze(1).broadcast_to([EP, W, P]),
                                                ALU.is_equal).then_inc(built, 1)
                        nc.vector.tensor_tensor(high[:, s, :, :], hi[:, cols].unsqueeze(2).broadcast_to([EP, W, NW]),
                                                g.iota[0:EP, 0:NW].unsqueeze(1).broadcast_to([EP, W, NW]),
                                                ALU.is_equal).then_inc(built, 1)
                dve.wait_ge(counted, groups + 3)
                nc.vector.tensor_copy(g.outdeg[:, :], ps[:, 0:NW])

            @block.tensor
            def _(pe):
                pe.sem_inc(counted, 2)
                pe.wait_ge(built, 2)
                nc.tensor.matmul(ps[:, 0:NW], zero[:, :], zero[:, 0:NW], start=True, stop=False)
                with pe.Fori(0, groups // 2) as i:
                    for s in range(2):
                        pe.wait_ge(built, 4 * i + 2 * s + 2)
                        for k in range(W):
                            mm = nc.tensor.matmul(ps[:, 0:NW], low[:, s, k, :], high[:, s, k, :],
                                                  start=False, stop=False)
                        mm.then_inc(counted, 1)
                nc.tensor.matmul(ps[:, 0:NW], zero[:, :], zero[:, 0:NW], start=False, stop=True).then_inc(counted, 1)


def layer_norm(nc, g, sem, name):
    x3 = g.x[:, :].rearrange("p (w f) -> p w f", f=D)
    h3 = g.h[:, :].rearrange("p (w f) -> p w f", f=D)
    with Stage(nc, name) as st:
        sq = st.sb("sq", [P, NW, D])
        mean = st.sb("mean", [P, NW])
        var = st.sb("var", [P, NW])
        rstd = st.sb("rstd", [P, NW])
        dv, centred, squared, rooted = sem(name + "_dv"), sem(name + "_cen"), sem(name + "_sq"), sem(name + "_rt")
        with nc.Block() as block:
            @block.vector
            def _(dve):
                c = Chain(dve, dv)
                c.step(nc.vector.tensor_reduce(mean[:, :], x3, X, ALU.add))
                c.step(nc.vector.tensor_scalar(mean[:, :], mean[:, :], 1.0 / D, None, ALU.mult))
                nc.vector.tensor_tensor(h3, x3, mean[:, :].unsqueeze(2).broadcast_to([P, NW, D]),
                                        ALU.subtract).then_inc(centred, 1)
                dve.wait_ge(squared, 1)
                c.step(nc.vector.tensor_reduce(var[:, :], sq[:, :, :], X, ALU.add))
                nc.vector.tensor_scalar(var[:, :], var[:, :], 1.0 / D, EPS, ALU.mult, ALU.add).then_inc(centred, 1)
                dve.wait_ge(rooted, 1)
                c.step(nc.vector.reciprocal(rstd[:, :], var[:, :]))
                nc.vector.scalar_tensor_tensor(h3, h3, 0.0, rstd[:, :].unsqueeze(2).broadcast_to([P, NW, D]),
                                               ALU.max, ALU.mult)

            @block.scalar
            def _(act):
                act.wait_ge(centred, 1)
                nc.scalar.activation(sq[:, :, :], h3, ACT.Square).then_inc(squared, 1)
                act.wait_ge(centred, 2)
                nc.scalar.activation(var[:, :], var[:, :], ACT.Sqrt).then_inc(rooted, 1)


def gather_sum(nc, g, sem, name, table, index, width, acc, acc_width, attr=None, coef=None):
    R = 16
    G = 4
    full = 2 * D if attr is not None else width
    dloc = g.cut_dloc if attr is not None else g.dloc
    with Stage(nc, name) as st:
        rows = st.sb("rows", [P, R, full])
        idx = st.sb("idx", [P, R], I32)
        sel = st.sb("sel", [P, 2, G, P])
        of_rel = st.sb("of_rel", [P, 2, G, RELS])
        ps = [[st.ps(f"ps{b}{s}") for s in range(G)] for b in range(2)]
        gathered = [sem(f"{name}_g{r}") for r in range(R)]
        loaded = [sem(f"{name}_a{r}") for r in range(R)] if attr is not None else None
        staged, sel_made, summed, added = (
            sem(name + "_staged"), sem(name + "_sel"), sem(name + "_summed"), sem(name + "_added"))
        with nc.Block() as block:
            @block.gpsimd
            def _(pool):
                with pool.Fori(0, T // R) as i:
                    for q in range(R // G):
                        pool.wait_ge(summed, R * i + G * (q + 1))
                        pool.nop(nofuse=True)
                        nc.gpsimd.tensor_copy(idx[:, q * G:(q + 1) * G],
                                              index[:, bass.ds(R * i + q * G, G)]).then_inc(staged, 1)
                        pool.wait_ge(staged, (R // G) * i + q + 1)
                        pool.nop(nofuse=True)
                        for r in range(q * G, (q + 1) * G):
                            pool.indirect_dma_start(rows[:, r, 0:width], None, table,
                                                    bass.IndirectOffsetOnAxis(idx[:, r:r + 1], 0)).then_inc(gathered[r], 16)

            if attr is not None:
                @block.sync
                def _(sp):
                    def load(features):
                        with sp.Fori(0, T // R) as i:
                            for r in range(R):
                                if r % G == 0:
                                    first = windows_of(nc, g, mybir.EngineType.SP, R * i + r, G, 0, E - P)
                                e0 = first[r % G]
                                sp.wait_ge(summed, R * i + r + 1)
                                sp.dma_start(rows[:, r, D:2 * D], features[bass.ds(e0, P), :]).then_inc(loaded[r], 16)

                    unsorted = sp.value_load(g.unsorted[0:1, 0:1], min_val=0, max_val=E)
                    with sp.If(unsorted > 0):
                        load(g.attr_d)
                    with sp.If(unsorted < 1):
                        load(attr)

            @block.tensor
            def _(pe):
                pe.sem_inc(summed, R)
                with pe.Fori(0, T // R) as i:
                    for r in range(R):
                        b, s = r // G % 2, r % G
                        if s == 0:
                            pe.wait_ge(sel_made, (R // G) * i + r // G + 1)
                        pe.wait_ge(added, R * i + r + 2)
                        pe.wait_ge(gathered[r], 16 * (i + 1))
                        if attr is not None:
                            pe.wait_ge(loaded[r], 16 * (i + 1))
                        mm = nc.tensor.matmul(ps[b][s][:, 0:full], sel[:, b, s, :], rows[:, r, :], start=True, stop=True)
                        if attr is not None:
                            mm = nc.tensor.matmul(ps[b][s][:, full:full + RELS], sel[:, b, s, :], of_rel[:, b, s, :],
                                                  start=True, stop=True)
                        mm.then_inc(summed, 1)

            @block.vector
            def _(dve):
                def make_sel_and_add(t0, b, first=False, adds=True):
                    if adds:
                        ws = windows_of(nc, g, mybir.EngineType.DVE, t0 - G)
                    if not first:
                        dve.wait_ge(summed, t0 + R - G)
                    if attr is not None:
                        nc.vector.tensor_tensor(
                            of_rel[:, b, :, :], g.cut_rel[:, bass.ds(t0, G)].unsqueeze(2).broadcast_to([P, G, RELS]),
                            g.iota[:, 0:RELS].unsqueeze(1).broadcast_to([P, G, RELS]), ALU.is_equal)
                    for s in range(G):
                        if coef is None:
                            ins = nc.vector.tensor_scalar(sel[:, b, s, :], g.iota[:, :], dloc[:, bass.ds(t0 + s, 1)],
                                                          None, ALU.is_equal)
                        else:
                            ins = nc.vector.tensor_scalar(sel[:, b, s, :], g.iota[:, :], dloc[:, bass.ds(t0 + s, 1)],
                                                          coef[:, bass.ds(t0 + s, 1)], ALU.is_equal, ALU.mult)
                        if s == G - 1:
                            ins.then_inc(sel_made, 1)
                        if adds:
                            add(t0 - G + s, 1 - b, s, ws[s])

                def add(t, b, s, w):
                    dve.wait_ge(summed, t + R + 1)
                    dve.wait_ge(added, t + 2 * G + 1)
                    part = acc[:, bass.ds(w * acc_width, acc_width)]
                    nc.vector.tensor_tensor(part, part, ps[b][s][:, 0:acc_width], ALU.add).then_inc(added, 1)

                for q in range(R // G):
                    make_sel_and_add(q * G, q % 2, first=q < 2, adds=q > 0)
                with dve.Fori(1, T // R) as i:
                    for q in range(R // G):
                        make_sel_and_add(R * i + q * G, q % 2)
                ws = windows_of(nc, g, mybir.EngineType.DVE, T - G)
                for s in range(G):
                    add(T - G + s, 1, s, ws[s])

            @block.scalar
            def _(act):
                act.sem_inc(added, 2 * G + 1)


def layer0(nc, g, sem, a):
    W0 = 2 * D + RELS
    with Stage(nc, "l0") as st:
        acc = st.sb("acc", [P, NW * W0])
        nsrc = st.sb("nsrc", [P, NW])
        ndst = st.sb("ndst", [P, NW])
        deg = g.deg
        rself = st.sb("rself", [P, NW])
        redge = st.sb("redge", [P, NW])
        has = st.sb("has", [P, NW])
        acc3 = acc[:, :].rearrange("p (w f) -> p w f", f=W0)
        h3 = g.h[:, :].rearrange("p (w f) -> p w f", f=D)
        with Stage(nc, "l0a") as sa:
            hn = sa.sb("hn", [P, NW, D])
            dv, rt, ready, out = sem("l0a_dv"), sem("l0a_rt"), sem("l0a_ready"), sem("l0a_out")
            with nc.Block() as block:
                @block.vector
                def _(dve):
                    c = Chain(dve, dv)
                    nc.vector.memset(acc[:, :], 0.0)
                    c.step(nc.vector.tensor_scalar(nsrc[:, :], g.outdeg[:, :], 1.0, None, ALU.max))
                    nc.vector.engine_nop().then_inc(ready, 1)
                    dve.wait_ge(rt, 1)
                    c.step(nc.vector.reciprocal(nsrc[:, :], nsrc[:, :]))
                    nc.vector.tensor_tensor(hn[:, :, :], h3, nsrc[:, :].unsqueeze(2).broadcast_to([P, NW, D]),
                                            ALU.mult).then_inc(ready, 1)

                @block.scalar
                def _(act):
                    act.wait_ge(ready, 1)
                    nc.scalar.activation(nsrc[:, :], nsrc[:, :], ACT.Sqrt).then_inc(rt, 1)

                @block.sync
                def _(sp):
                    sp.wait_ge(ready, 2)
                    sp.dma_start(g.node_d.rearrange("(w p) f -> p w f", p=P), hn[:, :, :]).then_inc(out, 16)
                    sp.wait_ge(out, 16)
        gather_sum(nc, g, sem, "l0e", g.node_d, g.cut_src_i, D, acc, W0, attr=a["edge_attr_128"])
        with Stage(nc, "l0b") as sb_:
            w = sb_.sb("w", [P, 2, D])
            bb = sb_.sb("bb", [P, 2, D])
            z = sb_.sb("z", [P, 2, 2, D])
            zt = sb_.sb("zt", [P, 2, 2, D])
            pt = [sb_.ps("pt0"), sb_.ps("pt1")]
            po = [sb_.ps("po0"), sb_.ps("po1")]
            dv, rt, ready, ld = sem("l0b_dv"), sem("l0b_rt"), sem("l0b_ready"), sem("l0b_ld")
            mixed, turned, copied, multiplied, lp = (
                sem("l0b_mixed"), sem("l0b_turned"), sem("l0b_copied"), sem("l0b_mult"), sem("l0b_lp"))
            with nc.Block() as block:
                @block.sync
                def _(sp):
                    sp.dma_start(w[:, 0, :], a["L0_gnn_W"]).then_inc(ld, 16)
                    sp.dma_start(w[:, 1, :], a["L0_gnn_We"]).then_inc(ld, 16)
                    sp.dma_start(bb[:, 0, :], a["L0_gnn_b"].partition_broadcast(P)).then_inc(ld, 16)
                    sp.dma_start(bb[:, 1, :], a["L0_gnn_be"].partition_broadcast(P)).then_inc(ld, 16)

                @block.scalar
                def _(act):
                    act.wait_ge(ready, 1)
                    nc.scalar.activation(ndst[:, :], ndst[:, :], ACT.Sqrt).then_inc(rt, 1)
                    with act.Fori(0, NW // 2) as i:
                        for j in range(2):
                            act.wait_ge(turned, 2 * i + j + 1)
                            act.wait_ge(multiplied, 2 * i + j + 1)
                            act.nop(nofuse=True)
                            nc.scalar.copy(zt[:, j, :, :], pt[j][:, 0:2 * D]).then_inc(copied, 1)

                @block.tensor
                def _(pe):
                    pe.sem_inc(multiplied, 2)
                    pe.wait_ge(ld, 64)
                    with pe.Fori(0, NW // 2) as i:
                        for j in range(2):
                            pe.wait_ge(mixed, 2 * i + j + 1)
                            for k in range(2):
                                mm = nc.tensor.transpose(pt[j][:, k * D:(k + 1) * D], z[:, j, k, :], g.ident[:, :])
                            mm.then_inc(turned, 1)
                        for j in range(2):
                            pe.wait_ge(copied, 2 * i + j + 1)
                            for k in range(2):
                                mm = nc.tensor.matmul(po[j][:, 0:D], zt[:, j, k, :], w[:, k, :],
                                                      start=(k == 0), stop=(k == 1))
                            mm.then_inc(multiplied, 1)

                @block.vector
                def _(dve):
                    c = Chain(dve, dv)
                    c.step(nc.vector.tensor_reduce(deg[:, :], acc3[:, :, 2 * D:], X, ALU.add))
                    c.step(nc.vector.tensor_copy(g.count[:, :].rearrange("p (w f) -> p w f", f=RELS), acc3[:, :, 2 * D:]))
                    c.step(nc.vector.tensor_scalar(redge[:, :], deg[:, :], 1.0, None, ALU.max))
                    c.step(nc.vector.tensor_copy(ndst[:, :], redge[:, :]))
                    nc.vector.engine_nop().then_inc(ready, 1)
                    c.step(nc.vector.reciprocal(redge[:, :], redge[:, :]))
                    c.step(nc.vector.tensor_scalar(rself[:, :], deg[:, :], 1.0, None, ALU.add))
                    c.step(nc.vector.reciprocal(rself[:, :], rself[:, :]))
                    c.step(nc.vector.tensor_tensor(has[:, :], deg[:, :], redge[:, :], ALU.mult))
                    dve.wait_ge(rt, 1)
                    c.step(nc.vector.reciprocal(ndst[:, :], ndst[:, :]))
                    dve.wait_ge(ld, 64)
                    base = c.n
                    with dve.Fori(0, NW // 2) as i:
                        for j in range(2):
                            v = 2 * i + j
                            wd = bass.ds(v * D, D)
                            c.n = base + i * 12 + 2 * j
                            c.step(nc.vector.tensor_scalar(z[:, j, 0, :], acc[:, bass.ds(v * W0, D)],
                                                           ndst[:, bass.ds(v, 1)], None, ALU.mult))
                            c.step(nc.vector.scalar_tensor_tensor(z[:, j, 0, :], g.h[:, wd], rself[:, bass.ds(v, 1)],
                                                                  z[:, j, 0, :], ALU.mult, ALU.add))
                            nc.vector.tensor_scalar(z[:, j, 1, :], acc[:, bass.ds(v * W0 + D, D)],
                                                    redge[:, bass.ds(v, 1)], None, ALU.mult).then_inc(mixed, 1)
                        for j in range(2):
                            v = 2 * i + j
                            xw = g.x[:, bass.ds(v * D, D)]
                            dve.wait_ge(multiplied, v + 3)
                            c.n = base + i * 12 + 4 + 4 * j
                            c.step(nc.vector.tensor_tensor(xw, xw, po[j][:, 0:D], ALU.add))
                            c.step(nc.vector.tensor_tensor(xw, xw, bb[:, 0, :], ALU.add))
                            c.step(nc.vector.scalar_tensor_tensor(xw, bb[:, 0, :], rself[:, bass.ds(v, 1)], xw,
                                                                  ALU.mult, ALU.add))
                            c.step(nc.vector.scalar_tensor_tensor(xw, bb[:, 1, :], has[:, bass.ds(v, 1)], xw,
                                                                  ALU.mult, ALU.add))


def window_copies(nc, pool, src, dst_of, freed, copied, width=D, stride=None, offset=0):
    stride = width if stride is None else stride
    with pool.Fori(0, NW // 2) as i:
        for j in range(2):
            v = 2 * i + j
            pool.wait_ge(freed, v + 1)
            pool.nop(nofuse=True)
            nc.gpsimd.tensor_copy(dst_of(j), src[:, bass.ds(v * stride + offset, width)]).then_inc(copied, 1)


def attention_nodes(nc, g, sem, name, weights, biases, transposed, scale, heads, qwin, qw, self_score=None):
    HD = D // heads
    with Stage(nc, name) as st:
        w = st.sb("w", [P, 3 * D])
        wraw = st.sb("wraw", [P, 3 * D])
        bias = st.sb("bias", [P, 3 * D])
        hc = st.sb("hc", [P, 2, D])
        ht = st.sb("ht", [P, 2, D])
        vkq = st.sb("vkq", [P, 2, 3 * D])
        prod = st.sb("prod", [P, 2, D])
        pw = st.ps("pw")
        pt = [st.ps("pt0"), st.ps("pt1")]
        po = [st.ps("po0"), st.ps("po1")]
        ld, wt, wc, dv, copied, turned, moved, projected, ready, stored, freed = (
            sem(name + k) for k in ("_ld", "_wt", "_wc", "_dv", "_copied", "_turned", "_moved", "_proj", "_ready", "_st", "_freed"))
        nld = 3 + sum(b is not None for b in biases)
        with nc.Block() as block:
            @block.sync
            def _(sp):
                for k in range(3):
                    sp.dma_start((wraw if transposed else w)[:, k * D:(k + 1) * D], weights[k]).then_inc(ld, 16)
                    if biases[k] is not None:
                        sp.dma_start(bias[:, k * D:(k + 1) * D], biases[k].partition_broadcast(P)).then_inc(ld, 16)
                sp.sem_inc(freed, 1)
                with sp.Fori(0, NW // 2) as i:
                    sp.wait_ge(ready, 2 * i + 4)
                    sp.dma_start(g.pair_d[bass.ds(2 * i * P, 2 * P), :].rearrange("(j p) f -> p j f", p=P),
                                 vkq[:, :, 0:2 * D]).then_inc(stored, 16)
                    sp.wait_ge(stored, 16 * (i + 1))
                    sp.sem_inc(freed, 1)

            @block.gpsimd
            def _(pool):
                window_copies(nc, pool, g.h, lambda j: hc[:, j, :], turned, copied)

            @block.scalar
            def _(act):
                act.sem_inc(ready, 2)
                with act.Fori(0, NW // 2) as i:
                    for j in range(2):
                        act.wait_ge(turned, 2 * i + j + 3)
                        act.wait_ge(projected, 2 * i + j + 1)
                        act.nop(nofuse=True)
                        nc.scalar.copy(ht[:, j, :], pt[j][:, 0:D]).then_inc(moved, 1)

            @block.tensor
            def _(pe):
                pe.sem_inc(turned, 2)
                pe.sem_inc(projected, 2)
                pe.wait_ge(ld, 16 * nld)
                if transposed:
                    for k in range(3):
                        mm = nc.tensor.transpose(pw[:, k * D:(k + 1) * D], wraw[:, k * D:(k + 1) * D], g.ident[:, :])
                    mm.then_inc(wt, 1)
                    pe.wait_ge(wc, 1)
                with pe.Fori(0, NW // 2) as i:
                    for j in range(2):
                        pe.wait_ge(copied, 2 * i + j + 1)
                        nc.tensor.transpose(pt[j][:, 0:D], hc[:, j, :], g.ident[:, :]).then_inc(turned, 1)
                    for j in range(2):
                        pe.wait_ge(moved, 2 * i + j + 1)
                        pe.wait_ge(ready, 2 * i + j + 1)
                        nc.tensor.matmul(po[j][:, 0:3 * D], ht[:, j, :], w[:, :],
                                         start=True, stop=True).then_inc(projected, 1)

            @block.vector
            def _(dve):
                c = Chain(dve, dv)
                for k in range(3):
                    if biases[k] is None:
                        nc.vector.memset(bias[:, k * D:(k + 1) * D], 0.0)
                if transposed:
                    dve.wait_ge(wt, 1)
                    c.step(nc.vector.tensor_copy(w[:, :], pw[:, 0:3 * D]))
                    nc.vector.engine_nop().then_inc(wc, 1)
                if self_score is not None:
                    rc3 = qwin[:, :].rearrange("p (w f) -> p w f", f=qw)
                    c.step(nc.vector.memset(rc3[:, :, D:], 0.0))
                    c.step(nc.vector.tensor_scalar(rc3[:, :, D:D + RELS],
                                                   g.count[:, :].rearrange("p (w f) -> p w f", f=RELS),
                                                   1.0, None, ALU.max))
                    c.step(nc.vector.reciprocal(rc3[:, :, D:D + RELS], rc3[:, :, D:D + RELS]))
                dve.wait_ge(ld, 16 * nld)
                steps = 4 if self_score is not None else 2
                base = c.n
                with dve.Fori(0, NW // 2) as i:
                    dve.wait_ge(freed, i + 1)
                    for j in range(2):
                        v = 2 * i + j
                        c.n = base + i * steps + (steps // 2) * j
                        dve.wait_ge(projected, v + 3)
                        c.step(nc.vector.tensor_tensor(vkq[:, j, :], po[j][:, 0:3 * D], bias[:, :], ALU.add))
                        qv = qwin[:, bass.ds(v * qw, D)]
                        if self_score is not None:
                            nc.vector.tensor_scalar(qv, vkq[:, j, 2 * D:], scale, None, ALU.mult)
                            c.step(nc.vector.scalar_tensor_tensor(prod[:, j, :], vkq[:, j, 2 * D:], scale,
                                                                  vkq[:, j, D:2 * D], ALU.mult, ALU.mult))
                            nc.vector.tensor_reduce(self_score[:, bass.ds(v * heads, heads)],
                                                    prod[:, j, :].rearrange("p (h d) -> p h d", h=heads),
                                                    X, ALU.add).then_inc(ready, 1)
                        else:
                            nc.vector.tensor_scalar(qv, vkq[:, j, 2 * D:], scale, None, ALU.mult).then_inc(ready, 1)


def attention_scores(nc, g, sem, name, heads, qwin, qw, scores, groups, v_spill):
    G = 4
    R = 16
    Q = R // G
    GW = qw // groups
    rel_cols = qw - D
    with Stage(nc, name) as st:
        rows = st.sb("rows", [P, R, D + qw])
        idx = st.sb("idx", [P, R], I32)
        sel = st.sb("sel", [P, 2, G, P])
        selt = st.sb("selt", [P, 2, G, P])
        prod = st.sb("prod", [P, 2, G, qw])
        pst = [st.ps("pst0"), st.ps("pst1")]
        pq = [st.ps(f"pq{b}", (P, 2, 512)) for b in range(2)]
        gathered = [sem(f"{name}_g{r}") for r in range(R)]
        spilled = [sem(f"{name}_sp{q}") for q in range(Q)]
        staged, sel_made, turned, moved, looked, used, rel_made, reduced, freed = (
            sem(name + k) for k in ("_staged", "_sel", "_turned", "_moved", "_looked", "_used", "_rel", "_reduced",
                                    "_freed"))
        with nc.Block() as block:
            @block.gpsimd
            def _(pool):
                with pool.Fori(0, T // R) as i:
                    for q in range(Q):
                        pool.wait_ge(used, Q * i + q + 1)
                        pool.nop(nofuse=True)
                        pool.wait_ge(freed, Q * i + q + 1)
                        pool.nop(nofuse=True)
                        nc.gpsimd.tensor_copy(idx[:, q * G:(q + 1) * G],
                                              g.src_i[:, bass.ds(R * i + q * G, G)]).then_inc(staged, 1)
                        pool.wait_ge(staged, Q * i + q + 1)
                        pool.nop(nofuse=True)
                        for r in range(q * G, (q + 1) * G):
                            pool.indirect_dma_start(rows[:, r, 0:2 * D], None, g.pair_d,
                                                    bass.IndirectOffsetOnAxis(idx[:, r:r + 1], 0)).then_inc(gathered[r], 16)

            @block.sync
            def _(sp):
                sp.sem_inc(freed, Q)
                with sp.Fori(0, T // R) as i:
                    for q in range(Q):
                        for r in range(q * G, (q + 1) * G):
                            sp.wait_ge(gathered[r], 16 * (i + 1))
                        sp.dma_start(v_spill[bass.ds((R * i + q * G) * P, G * P), :].rearrange("(s p) f -> p s f", p=P),
                                     rows[:, q * G:(q + 1) * G, 0:D]).then_inc(spilled[q], 16)
                        sp.wait_ge(spilled[q], 16 * (i + 1))
                        sp.sem_inc(freed, 1)

            @block.tensor
            def _(pe):
                def turn(n, b):
                    pe.wait_ge(sel_made, n + 1)
                    for s in range(G):
                        mm = nc.tensor.transpose(pst[b][:, s * P:(s + 1) * P], sel[:, b, s, :], g.ident[:, :])
                    mm.then_inc(turned, 1)

                def look(n, b):
                    ws = windows_of(nc, g, mybir.EngineType.PE, n * G)
                    for s in range(G):
                        w = ws[s]
                        if s == 0:
                            pe.wait_ge(moved, n + 1)
                            pe.wait_ge(used, n + Q - 1)
                        mm = nc.tensor.matmul(pq[b][:, s // 2, s % 2 * qw:(s % 2 + 1) * qw], selt[:, b, s, :], qwin[:, bass.ds(w * qw, qw)],
                                              start=True, stop=True)
                    mm.then_inc(looked, 1)

                turn(0, 0)
                with pe.Fori(0, T // (2 * G) - 1) as i:
                    turn(2 * i + 1, 1)
                    look(2 * i, 0)
                    turn(2 * i + 2, 0)
                    look(2 * i + 1, 1)
                turn(T // G - 1, 1)
                look(T // G - 2, 0)
                look(T // G - 1, 1)

            @block.scalar
            def _(act):
                act.sem_inc(used, Q)
                act.sem_inc(looked, 2)
                with act.Fori(0, T // (2 * G)) as i:
                    for b in range(2):
                        act.wait_ge(turned, 2 * i + b + 1)
                        act.wait_ge(looked, 2 * i + b + 1)
                        nc.scalar.copy(selt[:, b, :, :].rearrange("p s e -> p (s e)"), pst[b][:, :]).then_inc(moved, 1)

            @block.vector
            def _(dve):
                def make_sel(n, b, first):
                    if not first:
                        dve.wait_ge(turned, n - 1)
                    for s in range(G):
                        ins = nc.vector.tensor_scalar(sel[:, b, s, :], g.iota[:, :], g.dloc[:, bass.ds(n * G + s, 1)],
                                                      None, ALU.is_equal)
                    ins.then_inc(sel_made, 1)

                def mark_relations(n, q):
                    nc.vector.tensor_tensor(
                        rows[:, q * G:(q + 1) * G, 2 * D:],
                        g.rel[:, bass.ds(n * G, G)].unsqueeze(2).broadcast_to([P, G, rel_cols]),
                        g.iota[:, 0:rel_cols].unsqueeze(1).broadcast_to([P, G, rel_cols]),
                        ALU.is_equal).then_inc(rel_made, 1)

                def score(n, q, i, start=False, left=Q):
                    b = q % 2
                    rq = rows[:, q * G:(q + 1) * G, :]
                    for r in range(q * G, (q + 1) * G):
                        dve.wait_ge(gathered[r], 16 * (i + 1))
                    if rel_cols:
                        dve.wait_ge(rel_made, n + 1)
                    if not start:
                        dve.wait_ge(reduced, n - 1)
                    dve.wait_ge(looked, n + 3)
                    nc.vector.tensor_tensor(prod[:, b, :, :].rearrange("p (x y) f -> p x y f", x=2),
                                            pq[b][:, :, 0:2 * qw].rearrange("p x (y f) -> p x y f", y=2),
                                            rq[:, :, D:].rearrange("p (x y) f -> p x y f", x=2),
                                            ALU.mult).then_inc(used, 1)
                    if left > 2:
                        make_sel(n + 2, b, False)
                    if rel_cols and left > 1:
                        mark_relations(n + 1, (q + 1) % Q)
                    dve.wait_ge(used, n + Q + 1)
                    nc.vector.tensor_reduce(scores[:, bass.ds(n * G * groups, G * groups)],
                                            prod[:, b, :, :].rearrange("p s (k d) -> p (s k) d", d=GW),
                                            X, ALU.add).then_inc(reduced, 1)

                make_sel(0, 0, True)
                make_sel(1, 1, True)
                if rel_cols:
                    mark_relations(0, 0)
                for q in range(Q):
                    score(q, q, 0, start=q < 2)
                with dve.Fori(1, T // R - 1) as i:
                    for q in range(Q):
                        score(Q * i + q, q, i)
                for q in range(Q):
                    score(T // G - Q + q, q, T // R - 1, left=Q - q)


def scores_to_rows(nc, g, sem, name, heads, scores, groups, t1_d):
    NB = T * heads // P
    BI = NB // 13
    TPB = P // heads
    with Stage(nc, name + "t") as st:
        packed = st.sb("packed", [P, BI, P])
        turned_sb = st.sb("turned", [P, NB, P])
        pt = st.ps("pt")
        packs, turns, takes, out = (sem(name + k) for k in ("_packs", "_turns", "_takes", "_out"))
        with nc.Block() as block:
            @block.scalar
            def _(act):
                act.sem_inc(turns, 1)
                with act.Fori(0, 13) as i:
                    act.wait_ge(turns, i + 1)
                    act.nop(nofuse=True)
                    src = scores[:, bass.ds(i * BI * TPB * groups, BI * TPB * groups)] \
                        .rearrange("p (t k) -> p t k", k=groups)[:, :, 0:heads]
                    nc.scalar.copy(packed[:, :, :].rearrange("p b (t h) -> p (b t) h", h=heads), src) \
                        .then_inc(packs, 1)

            @block.tensor
            def _(pe):
                with pe.Fori(0, 13) as i:
                    pe.wait_ge(packs, i + 1)
                    pe.wait_ge(takes, i + 1)
                    for b in range(BI):
                        mm = nc.tensor.transpose(pt[:, b * P:(b + 1) * P], packed[:, b, :], g.ident[:, :])
                    mm.then_inc(turns, 1)

            @block.vector
            def _(dve):
                nc.vector.engine_nop().then_inc(takes, 1)
                if groups > heads:
                    nc.vector.tensor_copy(g.coef[:, 0:T].unsqueeze(2),
                                          scores[:, :].rearrange("p (t k) -> p t k", k=groups)[:, :, heads:])
                with dve.Fori(0, 13) as i:
                    dve.wait_ge(turns, i + 2)
                    nc.vector.tensor_copy(turned_sb[:, bass.ds(i * BI, BI), :],
                                          pt[:, 0:BI * P].rearrange("p (b e) -> p b e", e=P)).then_inc(takes, 1)

            @block.sync
            def _(sp):
                sp.wait_ge(takes, 14)
                sp.dma_start(view(t1_d.tensor, 0, [[P, P], [P * P, NB], [1, P]]), turned_sb[:, :, :]).then_inc(out, 16)
                sp.wait_ge(out, 16)


def segment_scan(nc, g, sem, name, heads, with_first, t1_d, ex_d, mf_d, room):
    C = P // heads
    CT = T // C
    LEN = CT * P
    HR = heads * P
    with Stage(nc, name + "s") as st:
        sc = st.sb("sc", [P, LEN])
        key = st.sb("key", [P, LEN + 2])
        begin = st.sb("begin", [P, LEN], BF16)
        end = st.sb("end", [P, LEN], BF16)
        most = room[:, 0:LEN]
        sums = st.sb("sums", [P, 4])
        row = st.sb("row", [1, 6, P])
        carry = st.sb("carry", [P, 2])
        pr = st.ps("pr")
        pc = st.ps("pc")
        ld, dv, chunked, rowed, carried, lined, expd, ready, out = (
            sem(name + k) for k in ("_sld", "_sdv", "_chunked", "_rowed", "_carried", "_lined", "_expd", "_sready", "_sout"))
        back = key[:, 0:LEN]

        def chunks(d, h):
            return view(d.tensor, h * P, [[CT * HR, C], [HR, CT], [1, P]])

        with nc.Block() as block:
            @block.sync
            def _(sp):
                for h in range(heads):
                    ps_ = slice(h * C, (h + 1) * C)
                    sp.dma_start(sc[ps_, :].rearrange("p (t e) -> p t e", e=P), chunks(t1_d, h)).then_inc(ld, 16)
                    sp.dma_start(key[ps_, :], view(g.keys_d.tensor, P - 1, [[LEN, C], [1, LEN + 2]])).then_inc(ld, 16)
                sp.wait_ge(expd, 1)
                sp.wait_ge(ready, 2)
                for h in range(heads):
                    ps_ = slice(h * C, (h + 1) * C)
                    sp.dma_start(chunks(ex_d, h), sc[ps_, :].rearrange("p (t e) -> p t e", e=P)).then_inc(out, 16)
                    if with_first:
                        sp.dma_start(chunks(mf_d, h), back[ps_, :].rearrange("p (t e) -> p t e", e=P)).then_inc(out, 16)
                sp.wait_ge(out, 16 * heads * (2 if with_first else 1))

            @block.vector
            def _(dve):
                c = Chain(dve, dv)
                dve.wait_ge(ld, 32 * heads)
                c.step(nc.vector.tensor_tensor(begin[:, :], key[:, 1:LEN + 1], key[:, 0:LEN], ALU.not_equal))
                c.step(nc.vector.tensor_tensor(end[:, :], key[:, 1:LEN + 1], key[:, 2:LEN + 2], ALU.not_equal))
                c.step(nc.vector.tensor_scalar(begin[:, :], begin[:, :], FAR, None, ALU.mult))
                c.step(nc.vector.tensor_scalar(end[:, :], end[:, :], FAR, None, ALU.mult))
                c.step(nc.vector.tensor_reduce(sums[:, 0:1], begin[:, :], X, ALU.min))
                c.step(nc.vector.tensor_reduce(sums[:, 2:3], end[:, :], X, ALU.min))
                c.step(nc.vector.tensor_tensor_scan(most[:, :], begin[:, :], sc[:, :], FAR, ALU.add, ALU.max))
                c.step(nc.vector.tensor_copy(sums[:, 1:2], most[:, LEN - 1:LEN]))
                c.step(nc.vector.tensor_tensor_scan(back[:, ::-1], end[:, ::-1], sc[:, ::-1], FAR, ALU.add, ALU.max))
                c.step(nc.vector.tensor_copy(sums[:, 3:4], back[:, 0:1]))
                nc.vector.engine_nop().then_inc(chunked, 1)
                dve.wait_ge(rowed, 1)
                c.step(nc.vector.tensor_copy(row[:, 0:4, :].rearrange("p a b -> p (a b)"), pr[0:1, :]))
                c.step(nc.vector.memset(row[:, 4:6, :], FAR))
                c.step(nc.vector.tensor_tensor_scan(row[:, 4, 1:P], row[:, 0, 0:P - 1], row[:, 1, 0:P - 1],
                                                    FAR, ALU.add, ALU.max))
                c.step(nc.vector.tensor_tensor_scan(row[:, 5, P - 2::-1], row[:, 2, P - 1:0:-1], row[:, 3, P - 1:0:-1],
                                                    FAR, ALU.add, ALU.max))
                nc.vector.engine_nop().then_inc(carried, 1)
                dve.wait_ge(lined, 1)
                c.step(nc.vector.tensor_copy(carry[:, :], pc[:, 0:2]))
                c.step(nc.vector.tensor_tensor_scan(most[:, :], begin[:, :], sc[:, :], carry[:, 0:1], ALU.add, ALU.max))
                c.step(nc.vector.tensor_tensor_scan(back[:, ::-1], end[:, ::-1], sc[:, ::-1], carry[:, 1:2],
                                                    ALU.add, ALU.max))
                c.step(nc.vector.tensor_tensor(most[:, :], most[:, :], back[:, :], ALU.max))
                nc.vector.tensor_tensor(sc[:, :], sc[:, :], most[:, :], ALU.subtract).then_inc(ready, 1)
                c.step(nc.vector.scalar_tensor_tensor(back[:, :], begin[:, :], -1.0, most[:, :], ALU.is_lt, ALU.mult))
                nc.vector.engine_nop().then_inc(expd, 1)

            @block.scalar
            def _(act):
                act.wait_ge(ready, 1)
                act.wait_ge(expd, 1)
                nc.scalar.activation(sc[:, :], sc[:, :], ACT.Exp).then_inc(ready, 1)

            @block.tensor
            def _(pe):
                pe.wait_ge(chunked, 1)
                for k in range(4):
                    mm = nc.tensor.transpose(pr[0:1, k * P:(k + 1) * P], sums[:, k:k + 1], g.ident[:, :])
                mm.then_inc(rowed, 1)
                pe.wait_ge(carried, 1)
                for k in range(2):
                    mm = nc.tensor.matmul(pc[:, k:k + 1], row[0:1, 4 + k, :], g.ones[0:1, 0:1], start=True, stop=True)
                mm.then_inc(lined, 1)


def rows_to_scores(nc, g, sem, name, heads, ex, mf, ex_d, mf_d):
    NB = T * heads // P
    BI = NB // 13
    pairs = [(ex, ex_d)] + ([(mf, mf_d)] if mf is not None else [])
    K = len(pairs)
    with Stage(nc, name + "b") as st:
        rows = st.sb("rows", [P, K, 2, BI, P])
        pt = [st.ps(f"pt{k}") for k in range(K)]
        loaded = [[sem(f"{name}_bl{k}{j}") for j in range(2)] for k in range(K)]
        turned, taken = sem(name + "_bturned"), sem(name + "_btaken")
        with nc.Block() as block:
            @block.sync
            def _(sp):
                for i in range(13):
                    for k, (_, d) in enumerate(pairs):
                        if i >= 2:
                            sp.wait_ge(turned, K * (i - 2) + k + 1)
                        sp.dma_start(rows[:, k, i % 2, :, :],
                                     view(d.tensor, i * BI * P * P, [[P, P], [P * P, BI], [1, P]])) \
                            .then_inc(loaded[k][i % 2], 16)

            @block.tensor
            def _(pe):
                for i in range(13):
                    for k in range(K):
                        pe.wait_ge(loaded[k][i % 2], 16 * (i // 2 + 1))
                        if i >= 1:
                            pe.wait_ge(taken, K * (i - 1) + k + 1)
                        for b in range(BI):
                            mm = nc.tensor.transpose(pt[k][:, b * P:(b + 1) * P], rows[:, k, i % 2, b, :],
                                                     g.ident[:, :])
                        mm.then_inc(turned, 1)

            @block.vector
            def _(dve):
                for i in range(13):
                    for k, (to, _) in enumerate(pairs):
                        dve.wait_ge(turned, K * i + k + 1)
                        nc.vector.tensor_copy(to[:, i * BI * P:(i + 1) * BI * P], pt[k][:, 0:BI * P]).then_inc(taken, 1)


def attention_sums(nc, g, sem, name, heads, ex, mf, v_spill, acc, aw):
    G, R = 4, 16
    Q = R // G
    HD = D // heads
    with Stage(nc, name + "p") as st:
        v = st.sb("v", [P, R, D])
        ve = st.sb("ve", [P, 2, G, aw])
        sel = st.sb("sel", [P, 2, G, P])
        ps = [[st.ps(f"ps{b}{s}") for s in range(G)] for b in range(2)]
        loaded = [sem(f"{name}_pl{q}") for q in range(Q)]
        beside, weighted, summed, added = (sem(name + k) for k in ("_pb", "_pw", "_psum", "_padd"))
        with nc.Block() as block:
            @block.sync
            def _(sp):
                with sp.Fori(0, T // R) as i:
                    for q in range(Q):
                        sp.wait_ge(weighted, Q * i + q + 1)
                        sp.dma_start(v[:, q * G:(q + 1) * G, :],
                                     v_spill[bass.ds((R * i + q * G) * P, G * P), :]
                                     .rearrange("(s p) f -> p s f", p=P)).then_inc(loaded[q], 16)

            @block.scalar
            def _(act):
                act.sem_inc(weighted, Q)
                act.sem_inc(summed, 2 * G)
                act.sem_inc(added, 2 * G + 1)
                with act.Fori(0, T // (2 * G)) as i:
                    for b in range(2):
                        n = 2 * i + b
                        act.wait_ge(summed, n * G + G)
                        act.nop(nofuse=True)
                        ins = nc.scalar.copy(ve[:, b, :, D:D + heads],
                                             ex[:, bass.ds(n * G * heads, G * heads)]
                                             .rearrange("p (s h) -> p s h", h=heads))
                        if mf is not None:
                            ins = nc.scalar.copy(ve[:, b, :, D + heads:],
                                                 mf[:, bass.ds(n * G * heads, G * heads)]
                                                 .rearrange("p (s h) -> p s h", h=heads))
                        ins.then_inc(beside, 1)

            @block.tensor
            def _(pe):
                with pe.Fori(0, T // (2 * G)) as i:
                    for b in range(2):
                        n = 2 * i + b
                        pe.wait_ge(weighted, n + Q + 1)
                        pe.wait_ge(beside, n + 1)
                        for s in range(G):
                            pe.wait_ge(added, n * G + s + 2)
                            nc.tensor.matmul(ps[b][s][:, 0:aw], sel[:, b, s, :], ve[:, b, s, :],
                                             start=True, stop=True).then_inc(summed, 1)

            @block.vector
            def _(dve):
                def weigh_and_add(n, q, i, adds=True):
                    b = q % 2
                    if adds:
                        ws = windows_of(nc, g, mybir.EngineType.DVE, (n - 1) * G)
                    dve.wait_ge(summed, n * G + G)
                    dve.wait_ge(loaded[q], 16 * (i + 1))
                    for s in range(G):
                        nc.vector.tensor_scalar(sel[:, b, s, :], g.iota[:, :], g.dloc[:, bass.ds(n * G + s, 1)],
                                                None, ALU.is_equal)
                        ins = nc.vector.tensor_tensor(
                            ve[:, b, s, 0:D].rearrange("p (h d) -> p h d", h=heads),
                            v[:, q * G + s, :].rearrange("p (h d) -> p h d", h=heads),
                            ex[:, bass.ds((n * G + s) * heads, heads)].unsqueeze(2).broadcast_to([P, heads, HD]),
                            ALU.mult)
                        if s == G - 1:
                            ins.then_inc(weighted, 1)
                        if adds:
                            add((n - 1) * G + s, 1 - b, s, ws[s])

                def add(t, b, s, w):
                    dve.wait_ge(summed, t + 2 * G + 1)
                    dve.wait_ge(added, t + 2 * G + 1)
                    part = acc[:, bass.ds(w * aw, aw)]
                    nc.vector.tensor_tensor(part, part, ps[b][s][:, 0:aw], ALU.add).then_inc(added, 1)

                for q in range(Q):
                    weigh_and_add(q, q, 0, adds=q > 0)
                with dve.Fori(1, T // R) as i:
                    for q in range(Q):
                        weigh_and_add(Q * i + q, q, i)
                ws = windows_of(nc, g, mybir.EngineType.DVE, T - G)
                for s in range(G):
                    add(T - G + s, 1, s, ws[s])


def attention(nc, g, sem, name, heads, groups, qw, weights, biases, transposed, scale, own, acc, aw):
    with Stage(nc, name) as st:
        with Stage(nc, name + "y") as sy:
            scores = sy.sb("scores", [P, T * groups])
            with Stage(nc, name + "x") as sx:
                qwin = sx.sb("qwin", [P, NW * qw])
                attention_nodes(nc, g, sem, name + "n", weights, biases, transposed, scale, heads, qwin, qw, own)
                attention_scores(nc, g, sem, name + "a", heads, qwin, qw, scores, groups, g.spill_d)
            scores_to_rows(nc, g, sem, name + "r", heads, scores, groups, g.t1_d)
        segment_scan(nc, g, sem, name, heads, own is not None, g.t1_d, g.t2_d, g.t3_d, acc)
        ex = st.sb("ex", [P, T * heads])
        mf = st.sb("mf", [P, T * heads]) if own is not None else None
        rows_to_scores(nc, g, sem, name + "u", heads, ex, mf, g.t2_d, g.t3_d)
        with nc.Block() as block:
            @block.vector
            def _(dve):
                nc.vector.memset(acc[:, :], 0.0)
        attention_sums(nc, g, sem, name + "s", heads, ex, mf, g.spill_d, acc, aw)


def batch_norm(nc, g, c, dve, yt, stats, gain, shift, ask, got, k):
    c.step(nc.vector.tensor_reduce(stats[:, 2:3], yt[:, 0:N], X, ALU.add))
    nc.vector.tensor_scalar(stats[:, 3:4], stats[:, 2:3], -1.0 / N, None, ALU.mult).then_inc(ask, 1)
    dve.wait_ge(got, 2 * k + 1)
    nc.vector.tensor_scalar(stats[:, 4:5], stats[:, 4:5], 1.0 / N, EPS, ALU.mult, ALU.add).then_inc(ask, 1)
    dve.wait_ge(got, 2 * k + 2)
    c.step(nc.vector.reciprocal(stats[:, 5:6], stats[:, 5:6]))
    c.step(nc.vector.tensor_tensor(stats[:, 0:1], stats[:, 5:6], gain, ALU.mult))
    c.step(nc.vector.scalar_tensor_tensor(stats[:, 1:2], stats[:, 3:4], stats[:, 0:1], shift, ALU.mult, ALU.add))


def batch_norm_squares(nc, act, yt, junk, stats, ask, got, k):
    act.wait_ge(ask, 2 * k + 1)
    nc.scalar.activation(junk[:, 0:N], yt[:, 0:N], ACT.Square, bias=stats[:, 3:4], accum_out=stats[:, 4:5]).then_inc(got, 1)
    act.wait_ge(ask, 2 * k + 2)
    nc.scalar.activation(stats[:, 5:6], stats[:, 4:5], ACT.Sqrt).then_inc(got, 1)


def layer1(nc, g, sem, a):
    H = 8
    AW = D + 2 * H
    with Stage(nc, "l1") as st:
        own = st.sb("own", [P, NW * H])
        with Stage(nc, "l1acc") as sacc:
            acc = sacc.sb("acc", [P, NW * AW])
            attention(nc, g, sem, "l1t", H, H + 1, D + 16, [a["L1_gnn_v_w"], a["L1_gnn_k_w"], a["L1_gnn_q_w"]],
                      [None, None, a["L1_gnn_q_b"]], True, 16.0 ** -0.5, own, acc, AW)
            acc3 = acc[:, :].rearrange("p (w f) -> p w f", f=AW)
            own3 = own[:, :].rearrange("p (w h) -> p w h", h=H)
            yt = sacc.sb("yt", [P, NP])
            with Stage(nc, "l1j") as sj:
                v = sj.sb("v", [P, NW, D])
                none = sj.sb("none", [P, NW])
                top = sj.sb("top", [P, NW, H])
                mx = sj.sb("mx", [P, NW, H])
                den = sj.sb("den", [P, NW, H])
                ld, dv, ready, expd = sem("l1j_ld"), sem("l1j_dv"), sem("l1j_ready"), sem("l1j_exp")
                with nc.Block() as block:
                    @block.sync
                    def _(sp):
                        sp.dma_start(v[:, :, :], g.pair_d[:, 0:D].rearrange("(w p) f -> p w f", p=P)).then_inc(ld, 16)

                    @block.scalar
                    def _(act):
                        act.wait_ge(ready, 2)
                        nc.scalar.activation(top[:, :, :], top[:, :, :], ACT.Exp).then_inc(expd, 1)
                        nc.scalar.activation(own3, own3, ACT.Exp).then_inc(expd, 1)

                    @block.vector
                    def _(dve):
                        c = Chain(dve, dv)
                        c.step(nc.vector.tensor_scalar(none[:, :], g.deg[:, :], 0.0, FAR, ALU.is_equal, ALU.mult))
                        c.step(nc.vector.tensor_tensor(top[:, :, :], acc3[:, :, D + H:],
                                                       none[:, :].unsqueeze(2).broadcast_to([P, NW, H]), ALU.add))
                        c.step(nc.vector.tensor_tensor(mx[:, :, :], top[:, :, :], own3, ALU.max))
                        nc.vector.tensor_tensor(top[:, :, :], top[:, :, :], mx[:, :, :], ALU.subtract).then_inc(ready, 1)
                        nc.vector.tensor_tensor(own3, own3, mx[:, :, :], ALU.subtract).then_inc(ready, 1)
                        dve.wait_ge(expd, 2)
                        c.step(nc.vector.tensor_tensor(den[:, :, :], acc3[:, :, D:D + H], top[:, :, :], ALU.mult))
                        c.step(nc.vector.scalar_tensor_tensor(den[:, :, :], den[:, :, :], 1e-16, own3, ALU.add, ALU.add))
                        c.step(nc.vector.reciprocal(den[:, :, :], den[:, :, :]))
                        c.step(nc.vector.tensor_tensor(top[:, :, :], top[:, :, :], den[:, :, :], ALU.mult))
                        c.step(nc.vector.tensor_tensor(own3, own3, den[:, :, :], ALU.mult))
                        dve.wait_ge(ld, 16)
                        for h in range(H):
                            hs = slice(h * 16, (h + 1) * 16)
                            c.step(nc.vector.tensor_tensor(acc3[:, :, hs], acc3[:, :, hs],
                                                           top[:, :, h:h + 1].broadcast_to([P, NW, 16]), ALU.mult))
                            c.step(nc.vector.tensor_tensor(v[:, :, hs], v[:, :, hs],
                                                           own3[:, :, h:h + 1].broadcast_to([P, NW, 16]), ALU.mult))
                        c.step(nc.vector.tensor_tensor(acc3[:, :, 0:D], acc3[:, :, 0:D], v[:, :, :], ALU.add))
            with Stage(nc, "l1o") as so:
                wraw, w, ob = so.sb("wraw", [P, D]), so.sb("w", [P, D]), so.sb("ob", [P, 1])
                zc, hc, zt = so.sb("zc", [P, 2, D]), so.sb("hc", [P, 2, D]), so.sb("zt", [P, 2, D])
                pw = so.ps("pw")
                pt = [so.ps("pt0"), so.ps("pt1")]
                po = [so.ps("po0"), so.ps("po1")]
                ld, wt, wc, copied, turned, moved, mixed, taken = (
                    sem("l1o" + k) for k in ("_ld", "_wt", "_wc", "_copied", "_turned", "_moved", "_mixed", "_taken"))
                with nc.Block() as block:
                    @block.sync
                    def _(sp):
                        sp.dma_start(wraw[:, :], a["L1_gnn_out_w"]).then_inc(ld, 16)
                        sp.dma_start(ob[:, :], a["L1_gnn_out_b"].rearrange("(p o) -> p o", o=1)).then_inc(ld, 16)

                    @block.gpsimd
                    def _(pool):
                        with pool.Fori(0, NW // 2) as i:
                            for j in range(2):
                                v = 2 * i + j
                                pool.wait_ge(mixed, v + 1)
                                pool.nop(nofuse=True)
                                nc.gpsimd.tensor_copy(zc[:, j, :], acc[:, bass.ds(v * AW, D)]).then_inc(copied, 1)
                                nc.gpsimd.tensor_copy(hc[:, j, :], g.h[:, bass.ds(v * D, D)]).then_inc(copied, 1)

                    @block.scalar
                    def _(act):
                        with act.Fori(0, NW // 2) as i:
                            for j in range(2):
                                act.wait_ge(turned, 2 * i + j + 1)
                                act.nop(nofuse=True)
                                nc.scalar.copy(zt[:, j, :], pt[j][:, 0:D]).then_inc(moved, 1)

                    @block.tensor
                    def _(pe):
                        pe.sem_inc(mixed, 2)
                        pe.sem_inc(taken, 2)
                        pe.wait_ge(ld, 32)
                        nc.tensor.transpose(pw[:, 0:D], wraw[:, :], g.ident[:, :]).then_inc(wt, 1)
                        pe.wait_ge(wc, 1)
                        with pe.Fori(0, NW // 2) as i:
                            for j in range(2):
                                pe.wait_ge(copied, 4 * i + 2 * j + 2)
                                nc.tensor.transpose(pt[j][:, 0:D], zc[:, j, :], g.ident[:, :]).then_inc(turned, 1)
                            for j in range(2):
                                pe.wait_ge(moved, 2 * i + j + 1)
                                pe.wait_ge(taken, 2 * i + j + 1)
                                nc.tensor.matmul(po[j][:, 0:D], w[:, :], zt[:, j, :], start=True, stop=False)
                                nc.tensor.matmul(po[j][:, 0:D], hc[:, j, :], g.ident[:, :],
                                                 start=False, stop=True).then_inc(mixed, 1)

                    @block.vector
                    def _(dve):
                        dve.wait_ge(wt, 1)
                        nc.vector.tensor_copy(w[:, :], pw[:, 0:D]).then_inc(wc, 1)
                        with dve.Fori(0, NW // 2) as i:
                            for j in range(2):
                                v = 2 * i + j
                                dve.wait_ge(mixed, v + 3)
                                nc.vector.tensor_scalar(yt[:, bass.ds(v * D, D)], po[j][:, 0:D], ob[:, 0:1], None,
                                                        ALU.add).then_inc(taken, 1)
            CH = 400
            NCH = NP // CH
            K = FF // P
            with Stage(nc, "l1f") as sf:
                junk = sf.sb("junk", [P, NP])
                w1r, w2r = sf.sb("w1r", [P, K, D]), sf.sb("w2r", [P, FF])
                w1, w2 = sf.sb("w1", [P, K, P]), sf.sb("w2", [P, K, D])
                vec = sf.sb("vec", [P, 5])
                b1 = sf.sb("b1", [P, K])
                stats, stats2 = sf.sb("stats", [P, 8]), sf.sb("stats2", [P, 8])
                x1 = sf.sb("x1", [P, CH])
                z, ff = sf.sb("z", [P, K, CH]), sf.sb("ff", [P, K, CH])
                yc, pbk = sf.sb("yc", [P, 2, D]), [sf.ps("pb0"), sf.ps("pb1")]
                pz = sf.ps("pz", (P, K, 512))
                po = sf.ps("po")
                pw = sf.ps("pw")
                (ld, wt, wc, dv, ask, got, x1_ready, hidden, biased, leaked, summed, normed, turned, taken, dv_done) = (
                    sem("l1f" + k) for k in ("_ld", "_wt", "_wc", "_dv", "_ask", "_got", "_x1", "_hid", "_bias", "_leak",
                                             "_sum", "_norm", "_turned", "_taken", "_dvd"))
                with nc.Block() as block:
                    @block.sync
                    def _(sp):
                        sp.dma_start(w1r[:, :, :], a["L1_gnn_lin1_w"].rearrange("(k p) f -> p k f", p=P)).then_inc(ld, 16)
                        sp.dma_start(w2r[:, :], a["L1_gnn_lin2_w"]).then_inc(ld, 16)
                        for k, n_ in enumerate(("g1", "b1", "lin2_b", "g2", "b2")):
                            sp.dma_start(vec[:, k:k + 1], a["L1_gnn_" + n_].rearrange("(p o) -> p o", o=1)).then_inc(ld, 16)
                        sp.dma_start(b1[:, :], a["L1_gnn_lin1_b"].rearrange("(k p) -> p k", p=P),
                                     allow_slow_non_contiguous=True).then_inc(ld, 16)

                    @block.scalar
                    def _(act):
                        act.wait_ge(ld, 128)
                        batch_norm_squares(nc, act, yt, junk, stats, ask, got, 0)
                        with act.Fori(0, NCH) as i:
                            act.wait_ge(hidden, i + 1)
                            for k in range(K):
                                ins = nc.scalar.activation(z[:, k, :], pz[:, k, 0:CH], ACT.Identity, bias=b1[:, k:k + 1])
                            ins.then_inc(biased, 1)
                        batch_norm_squares(nc, act, yt, junk, stats2, ask, got, 1)
                        act.wait_ge(dv_done, 1)
                        act.sem_inc(turned, 2)
                        with act.Fori(0, NW // 2) as i:
                            for j in range(2):
                                v = 2 * i + j
                                act.wait_ge(turned, v + 1)
                                act.nop(nofuse=True)
                                nc.scalar.activation(yc[:, j, :], yt[:, bass.ds(v * D, D)], ACT.Identity,
                                                     bias=stats2[:, 1:2], scale=stats2[:, 0:1]).then_inc(normed, 1)

                    @block.tensor
                    def _(pe):
                        pe.wait_ge(ld, 128)
                        for k in range(K):
                            mm = nc.tensor.transpose(pw[:, k * P:(k + 1) * P], w1r[:, k, :], g.ident[:, :])
                        mm.then_inc(wt, 1)
                        for k in range(K):
                            mm = nc.tensor.transpose(pz[:, 0, k * P:(k + 1) * P], w2r[:, k * P:(k + 1) * P], g.ident[:, :])
                        mm.then_inc(wt, 1)
                        pe.wait_ge(wc, 2)
                        with pe.Fori(0, NCH) as i:
                            pe.wait_ge(x1_ready, i + 1)
                            for k in range(K):
                                mm = nc.tensor.matmul(pz[:, k, 0:CH], w1[:, k, :], x1[:, :], start=True, stop=True)
                            mm.then_inc(hidden, 1)
                            pe.wait_ge(leaked, i + 1)
                            for k in range(K):
                                mm = nc.tensor.matmul(po[:, 0:CH], w2[:, k, :], ff[:, k, :],
                                                      start=(k == 0), stop=(k == K - 1))
                            mm.then_inc(summed, 1)
                        pe.sem_inc(taken, 2)
                        with pe.Fori(0, NW // 2) as i:
                            for j in range(2):
                                pe.wait_ge(normed, 2 * i + j + 1)
                                pe.wait_ge(taken, 2 * i + j + 1)
                                nc.tensor.transpose(pbk[j][:, 0:D], yc[:, j, :], g.ident[:, :]).then_inc(turned, 1)

                    @block.vector
                    def _(dve):
                        c = Chain(dve, dv)
                        dve.wait_ge(wt, 1)
                        nc.vector.tensor_copy(w1[:, :, :].rearrange("p k f -> p (k f)"), pw[:, :]).then_inc(wc, 1)
                        dve.wait_ge(wt, 2)
                        nc.vector.tensor_copy(w2[:, :, :].rearrange("p k f -> p (k f)"), pz[:, 0, :]).then_inc(wc, 1)
                        dve.wait_ge(ld, 128)
                        batch_norm(nc, g, c, dve, yt, stats, vec[:, 0:1], vec[:, 1:2], ask, got, 0)
                        base = c.n
                        with dve.Fori(0, NCH) as i:
                            c.n = base + i
                            yv = yt[:, bass.ds(i * CH, CH)]
                            nc.vector.tensor_scalar(x1[:, :], yv, stats[:, 0:1], stats[:, 1:2], ALU.mult,
                                                    ALU.add).then_inc(x1_ready, 1)
                            dve.wait_ge(biased, i + 1)
                            nc.vector.scalar_tensor_tensor(ff[:, :, :], z[:, :, :], 0.01, z[:, :, :],
                                                           ALU.mult, ALU.max).then_inc(leaked, 1)
                            dve.wait_ge(summed, i + 1)
                            c.step(nc.vector.scalar_tensor_tensor(yv, po[:, 0:CH], vec[:, 2:3], x1[:, :],
                                                                  ALU.add, ALU.add))
                        c.n = base + NCH
                        batch_norm(nc, g, c, dve, yt, stats2, vec[:, 3:4], vec[:, 4:5], ask, got, 1)
                        nc.vector.engine_nop().then_inc(dv_done, 1)
                        with dve.Fori(0, NW // 2) as i:
                            for j in range(2):
                                v = 2 * i + j
                                dve.wait_ge(turned, v + 3)
                                xv = g.x[:, bass.ds(v * D, D)]
                                nc.vector.tensor_tensor(xv, xv, pbk[j][:, 0:D], ALU.add).then_inc(taken, 1)


def layer2(nc, g, sem, a):
    with Stage(nc, "l2") as st:
        acc = st.sb("acc", [P, NW * HID])
        with Stage(nc, "l2a") as s1:
            w, root, bias = s1.sb("w", [P, RELS, HID]), s1.sb("root", [P, HID]), s1.sb("bias", [P, HID])
            hc, ht = s1.sb("hc", [P, 2, D]), s1.sb("ht", [P, 2, D])
            msg = s1.sb("msg", [P, 2, RELS * HID])
            pt = s1.ps("pt")
            pr = s1.ps("pr")
            pm = s1.ps("pm", (P, 4, 512))
            ld, copied, turned, moved, mult, tk_a, tk_d, rooted, rtaken, stored0, stored1, freed0, freed1 = (
                sem("l2a" + k) for k in ("_ld", "_copied", "_turned", "_moved", "_mult", "_tka", "_tkd", "_root",
                                         "_rtk", "_st0", "_st1", "_fr0", "_fr1"))
            stored, freed = [stored0, stored1], [freed0, freed1]
            with nc.Block() as block:
                @block.sync
                def _(sp):
                    sp.dma_start(w[:, :, :], a["L2_gnn_W1"].rearrange("r i o -> i r o")).then_inc(ld, 16)
                    sp.dma_start(root[:, :], a["L2_gnn_root1"]).then_inc(ld, 16)
                    sp.dma_start(bias[:, :], a["L2_gnn_b1"].partition_broadcast(P)).then_inc(ld, 16)
                    for j in range(2):
                        sp.sem_inc(freed[j], 1)
                    with sp.Fori(0, NW // 2) as i:
                        for j in range(2):
                            v = 2 * i + j
                            sp.wait_ge(tk_a, 2 * v + 4)
                            sp.wait_ge(tk_d, 2 * v + 4)
                            sp.dma_start(g.msg1_d[bass.ds(v * P, P), :], msg[:, j, :]).then_inc(stored[j], 16)
                            sp.wait_ge(stored[j], 16 * (i + 1))
                            sp.sem_inc(freed[j], 1)

                @block.gpsimd
                def _(pool):
                    window_copies(nc, pool, g.h, lambda j: hc[:, j, :], turned, copied)

                @block.scalar
                def _(act):
                    act.sem_inc(tk_a, 2)
                    with act.Fori(0, NW // 2) as i:
                        for j in range(2):
                            v = 2 * i + j
                            act.wait_ge(turned, v + 3)
                            act.nop(nofuse=True)
                            nc.scalar.copy(ht[:, j, :], pt[:, j * D:(j + 1) * D]).then_inc(moved, 1)
                            act.wait_ge(freed[j], i + 1)
                            act.nop(nofuse=True)
                            for b in range(2):
                                act.wait_ge(mult, 4 * v + b + 1)
                                nc.scalar.copy(msg[:, j, b * 512:(b + 1) * 512], pm[:, b, :]).then_inc(tk_a, 1)

                @block.tensor
                def _(pe):
                    pe.sem_inc(turned, 2)
                    pe.wait_ge(ld, 48)
                    with pe.Fori(0, NW // 2) as i:
                        for j in range(2):
                            v = 2 * i + j
                            pe.wait_ge(copied, v + 1)
                            nc.tensor.transpose(pt[:, j * D:(j + 1) * D], hc[:, j, :], g.ident[:, :]).then_inc(turned, 1)
                            pe.wait_ge(moved, v + 1)
                            pe.wait_ge(rtaken, v + 1)
                            nc.tensor.matmul(pr[:, 0:HID], ht[:, j, :], root[:, :], start=True,
                                             stop=True).then_inc(rooted, 1)
                            for b in range(4):
                                pe.wait_ge(tk_a if b < 2 else tk_d, 2 * v + b % 2 + 1)
                                mm = nc.tensor.matmul(pm[:, b, :], ht[:, j, :], w[:, 2 * b:2 * b + 2, :]
                                                      .rearrange("p r o -> p (r o)"), start=True, stop=True)
                                mm.then_inc(mult, 1)

                @block.vector
                def _(dve):
                    nc.vector.engine_nop().then_inc(rtaken, 1)
                    for _ in range(2):
                        nc.vector.engine_nop().then_inc(tk_d, 1)
                    dve.wait_ge(ld, 48)
                    with dve.Fori(0, NW // 2) as i:
                        for j in range(2):
                            v = 2 * i + j
                            hv = acc[:, bass.ds(v * HID, HID)]
                            dve.wait_ge(rooted, v + 1)
                            nc.vector.tensor_tensor(hv, pr[:, 0:HID], bias[:, :], ALU.add).then_inc(rtaken, 1)
                            dve.wait_ge(freed[j], i + 1)
                            for b in range(2):
                                dve.wait_ge(mult, 4 * v + b + 3)
                                nc.vector.tensor_copy(msg[:, j, (2 + b) * 512:(3 + b) * 512],
                                                      pm[:, 2 + b, :]).then_inc(tk_d, 1)
        gather_sum(nc, g, sem, "l2e", g.msg1_d.rearrange("n (r f) -> (n r) f", r=RELS), g.msg_i, HID, acc, HID,
                   coef=g.coef)
        with Stage(nc, "l2b") as s2:
            w, root, bias = s2.sb("w", [P, 2, RELS, D]), s2.sb("root", [P, 2, D]), s2.sb("bias", [P, D])
            hc, ht = s2.sb("hc", [P, 2, HID]), s2.sb("ht", [P, 2, HID])
            msg = s2.sb("msg", [P, 2, RELS * D])
            pt = [s2.ps("pt0"), s2.ps("pt1")]
            pr = s2.ps("pr")
            pm = s2.ps("pm", (P, 2, 512))
            ld, copied, turned, moved, mult, tk_a, tk_d, rooted, rtaken, stored0, stored1, freed0, freed1 = (
                sem("l2b" + k) for k in ("_ld", "_copied", "_turned", "_moved", "_mult", "_tka", "_tkd", "_root",
                                         "_rtk", "_st0", "_st1", "_fr0", "_fr1"))
            stored, freed = [stored0, stored1], [freed0, freed1]
            with nc.Block() as block:
                @block.sync
                def _(sp):
                    for k in range(2):
                        sp.dma_start(w[:, k, :, :], a["L2_gnn_W2"][:, k * P:(k + 1) * P, :].rearrange("r i o -> i r o")) \
                            .then_inc(ld, 16)
                        sp.dma_start(root[:, k, :], a["L2_gnn_root2"][k * P:(k + 1) * P, :]).then_inc(ld, 16)
                    sp.dma_start(bias[:, :], a["L2_gnn_b2"].partition_broadcast(P)).then_inc(ld, 16)
                    for j in range(2):
                        sp.sem_inc(freed[j], 1)
                    with sp.Fori(0, NW // 2) as i:
                        for j in range(2):
                            v = 2 * i + j
                            sp.wait_ge(tk_a, v + 2)
                            sp.wait_ge(tk_d, v + 2)
                            sp.dma_start(g.msg2_d[bass.ds(v * P, P), :], msg[:, j, :]).then_inc(stored[j], 16)
                            sp.wait_ge(stored[j], 16 * (i + 1))
                            sp.sem_inc(freed[j], 1)

                @block.gpsimd
                def _(pool):
                    with pool.Fori(0, NW // 2) as i:
                        for j in range(2):
                            v = 2 * i + j
                            pool.wait_ge(turned, v + 1)
                            pool.nop(nofuse=True)
                            nc.gpsimd.tensor_copy(hc[:, j, :], acc[:, bass.ds(v * HID, HID)]).then_inc(copied, 1)

                @block.scalar
                def _(act):
                    act.sem_inc(tk_a, 1)
                    with act.Fori(0, NW // 2) as i:
                        for j in range(2):
                            v = 2 * i + j
                            act.wait_ge(turned, v + 3)
                            act.nop(nofuse=True)
                            nc.scalar.activation(ht[:, j, :], pt[j][:, 0:HID], ACT.Relu).then_inc(moved, 1)
                            act.wait_ge(freed[j], i + 1)
                            act.wait_ge(mult, 2 * v + 1)
                            act.nop(nofuse=True)
                            nc.scalar.copy(msg[:, j, 0:512], pm[:, 0, :]).then_inc(tk_a, 1)

                @block.tensor
                def _(pe):
                    pe.sem_inc(turned, 2)
                    pe.wait_ge(ld, 80)
                    with pe.Fori(0, NW // 2) as i:
                        for j in range(2):
                            v = 2 * i + j
                            pe.wait_ge(copied, v + 1)
                            for k in range(2):
                                mm = nc.tensor.transpose(pt[j][:, k * P:(k + 1) * P], hc[:, j, k * P:(k + 1) * P],
                                                         g.ident[:, :])
                            mm.then_inc(turned, 1)
                            pe.wait_ge(moved, v + 1)
                            pe.wait_ge(rtaken, v + 1)
                            for k in range(2):
                                mm = nc.tensor.matmul(pr[:, 0:D], ht[:, j, k * P:(k + 1) * P], root[:, k, :],
                                                      start=(k == 0), stop=(k == 1))
                            mm.then_inc(rooted, 1)
                            for b in range(2):
                                pe.wait_ge(tk_a if b == 0 else tk_d, v + 1)
                                for k in range(2):
                                    mm = nc.tensor.matmul(pm[:, b, :], ht[:, j, k * P:(k + 1) * P],
                                                          w[:, k, 4 * b:4 * b + 4, :].rearrange("p r o -> p (r o)"),
                                                          start=(k == 0), stop=(k == 1))
                                mm.then_inc(mult, 1)

                @block.vector
                def _(dve):
                    nc.vector.engine_nop().then_inc(rtaken, 1)
                    nc.vector.engine_nop().then_inc(tk_d, 1)
                    dve.wait_ge(ld, 80)
                    with dve.Fori(0, NW // 2) as i:
                        for j in range(2):
                            v = 2 * i + j
                            xv = g.x[:, bass.ds(v * D, D)]
                            dve.wait_ge(rooted, v + 1)
                            nc.vector.tensor_tensor(xv, xv, pr[:, 0:D], ALU.add).then_inc(rtaken, 1)
                            dve.wait_ge(rtaken, v + 2)
                            nc.vector.tensor_tensor(xv, xv, bias[:, :], ALU.add)
                            dve.wait_ge(freed[j], i + 1)
                            dve.wait_ge(mult, 2 * v + 2)
                            nc.vector.tensor_copy(msg[:, j, 512:], pm[:, 1, :]).then_inc(tk_d, 1)
        gather_sum(nc, g, sem, "l2f", g.msg2_d.rearrange("n (r f) -> (n r) f", r=RELS), g.msg_i, D, g.x, D,
                   coef=g.coef)


def layer3(nc, g, sem, a):
    H = 2
    AW = D + H
    with Stage(nc, "l3") as st:
        acc = st.sb("acc", [P, NW * AW])
        attention(nc, g, sem, "l3t", H, H, D, [a["L3_gnn_Wv"], a["L3_gnn_Wk"], a["L3_gnn_Wq"]],
                  [a["L3_gnn_bv"], a["L3_gnn_bk"], a["L3_gnn_bq"]], False, 64.0 ** -0.5, None, acc, AW)
        acc3 = acc[:, :].rearrange("p (w f) -> p w f", f=AW)
        with Stage(nc, "l3o") as so:
            den = so.sb("den", [P, NW, H])
            wskip, wg, wf = so.sb("wskip", [P, D]), so.sb("wg", [P, 2, D]), so.sb("wf", [P, D])
            bs = so.sb("bs", [P, 1])
            zc, hc = so.sb("zc", [P, 2, D]), so.sb("hc", [P, 2, D])
            ht, xt = so.sb("ht", [P, 2, D]), so.sb("xt", [P, 2, D])
            gate, fuse = so.sb("gate", [P, 2, D]), so.sb("fuse", [P, 2, D])
            pt = [so.ps("pt0"), so.ps("pt1")]
            px = [so.ps("px0"), so.ps("px1")]
            pg = [so.ps("pg0"), so.ps("pg1")]
            ld, dv, scaled, copied, turned, moved, mixed, biased, gated, acted, joined = (
                sem("l3o" + k) for k in ("_ld", "_dv", "_scaled", "_copied", "_turned", "_moved", "_mixed", "_biased",
                                         "_gated", "_acted", "_joined"))
            with nc.Block() as block:
                @block.sync
                def _(sp):
                    sp.dma_start(wskip[:, :], a["L3_gnn_Wskip"]).then_inc(ld, 16)
                    sp.dma_start(wg[:, :, :], a["L3_gnn_Wgate"].rearrange("(k p) f -> p k f", p=P)).then_inc(ld, 16)
                    sp.dma_start(wf[:, :], a["L3_gnn_Wfuse"]).then_inc(ld, 16)
                    sp.dma_start(bs[:, :], a["L3_gnn_bskip"].rearrange("(p o) -> p o", o=1)).then_inc(ld, 16)

                @block.gpsimd
                def _(pool):
                    pool.wait_ge(scaled, 1)
                    with pool.Fori(0, NW // 2) as i:
                        for j in range(2):
                            v = 2 * i + j
                            pool.wait_ge(mixed, v + 1)
                            pool.nop(nofuse=True)
                            nc.gpsimd.tensor_copy(zc[:, j, :], acc[:, bass.ds(v * AW, D)]).then_inc(copied, 1)
                            nc.gpsimd.tensor_copy(hc[:, j, :], g.h[:, bass.ds(v * D, D)]).then_inc(copied, 1)

                @block.scalar
                def _(act):
                    act.wait_ge(ld, 64)
                    with act.Fori(0, NW // 2) as i:
                        for j in range(2):
                            v = 2 * i + j
                            act.wait_ge(turned, v + 1)
                            act.wait_ge(gated, v + 1)
                            act.nop(nofuse=True)
                            nc.scalar.copy(ht[:, j, :], pt[j][:, 0:D]).then_inc(moved, 1)
                        for j in range(2):
                            v = 2 * i + j
                            act.wait_ge(mixed, v + 3)
                            act.nop(nofuse=True)
                            nc.scalar.activation(xt[:, j, :], px[j][:, 0:D], ACT.Identity, bias=bs[:, 0:1]) \
                                .then_inc(biased, 1)
                        for j in range(2):
                            v = 2 * i + j
                            act.wait_ge(gated, v + 3)
                            act.wait_ge(joined, v + 1)
                            act.nop(nofuse=True)
                            nc.scalar.activation(gate[:, j, :], pg[j][:, 0:D], ACT.Sigmoid).then_inc(acted, 1)
                            nc.scalar.activation(fuse[:, j, :], pg[j][:, D:2 * D], ACT.Tanh).then_inc(acted, 1)

                @block.tensor
                def _(pe):
                    pe.sem_inc(mixed, 2)
                    pe.sem_inc(gated, 2)
                    pe.sem_inc(joined, 2)
                    pe.sem_inc(acted, 4)
                    pe.wait_ge(ld, 64)
                    with pe.Fori(0, NW // 2) as i:
                        for j in range(2):
                            v = 2 * i + j
                            pe.wait_ge(copied, 2 * v + 2)
                            nc.tensor.transpose(pt[j][:, 0:D], hc[:, j, :], g.ident[:, :]).then_inc(turned, 1)
                        for j in range(2):
                            v = 2 * i + j
                            pe.wait_ge(moved, v + 1)
                            nc.tensor.matmul(px[j][:, 0:D], wskip[:, :], ht[:, j, :], start=True, stop=False)
                            nc.tensor.matmul(px[j][:, 0:D], zc[:, j, :], g.ident[:, :],
                                             start=False, stop=True).then_inc(mixed, 1)
                        for j in range(2):
                            v = 2 * i + j
                            pe.wait_ge(biased, v + 1)
                            pe.wait_ge(acted, 2 * v + 2)
                            nc.tensor.matmul(pg[j][:, 0:D], ht[:, j, :], wg[:, 0, :], start=True, stop=False)
                            nc.tensor.matmul(pg[j][:, 0:D], xt[:, j, :], wg[:, 1, :], start=False, stop=True)
                            nc.tensor.matmul(pg[j][:, D:2 * D], xt[:, j, :], wf[:, :], start=True,
                                             stop=True).then_inc(gated, 1)

                @block.vector
                def _(dve):
                    c = Chain(dve, dv)
                    c.step(nc.vector.tensor_scalar(den[:, :, :], acc3[:, :, D:], 0.5, None, ALU.max))
                    c.step(nc.vector.reciprocal(den[:, :, :], den[:, :, :]))
                    for h in range(H):
                        hs = slice(h * 64, (h + 1) * 64)
                        c.step(nc.vector.tensor_tensor(acc3[:, :, hs], acc3[:, :, hs],
                                                       den[:, :, h:h + 1].broadcast_to([P, NW, 64]), ALU.mult))
                    nc.vector.engine_nop().then_inc(scaled, 1)
                    base = c.n
                    with dve.Fori(0, NW // 2) as i:
                        for j in range(2):
                            v = 2 * i + j
                            c.n = base + 6 * i + 3 * j
                            hv, xv = g.h[:, bass.ds(v * D, D)], g.x[:, bass.ds(v * D, D)]
                            dve.wait_ge(acted, 2 * v + 6)
                            c.step(nc.vector.tensor_tensor(fuse[:, j, :], fuse[:, j, :], hv, ALU.subtract))
                            c.step(nc.vector.tensor_tensor(fuse[:, j, :], fuse[:, j, :], gate[:, j, :], ALU.mult))
                            c.step(nc.vector.tensor_tensor(fuse[:, j, :], fuse[:, j, :], hv, ALU.add))
                            nc.vector.tensor_tensor(xv, xv, fuse[:, j, :], ALU.add).then_inc(joined, 1)


class Held:
    pass


def gnn_stack(nc, a, out):
    with ExitStack() as ctx:
        sem = Semaphores(nc)

        def sb(name, shape, dt=F32):
            return ctx.enter_context(nc.sbuf_tensor(name, shape, dt))

        g = Held()
        g.iota_i, g.tile_i = sb("iota_i", [P, P], I32), sb("tile_i", [P, TB], I32)
        g.iota, g.tile_f = sb("iota", [P, P]), sb("tile_f", [P, TB])
        g.ident, g.ones = sb("ident", [P, P]), sb("ones", [P, P])
        g.x, g.h = sb("x", [P, NP]), sb("h", [P, NP])
        g.src_i, g.msg_i = sb("src_i", [P, TA], I32), sb("msg_i", [P, TA], I32)
        g.dloc, g.rel, g.coef = sb("dloc", [P, TA]), sb("rel", [P, TA]), sb("coef", [P, TA])
        g.cut_src_i, g.cut_dloc, g.cut_rel = sb("cut_src_i", [P, TA], I32), sb("cut_dloc", [P, TA]), sb("cut_rel", [P, TA])
        g.edges_d = nc.dram_tensor("edges_d", (3, E + P), I32, kind="Internal").ap()
        g.unsorted = sb("unsorted", [1, 1], I32)
        g.pass_d = [nc.dram_tensor(f"pass{k}_d", (E, 4), I32, kind="Internal").ap() for k in range(2)]
        g.attr_d = nc.dram_tensor("attr_d", (E, D), F32, kind="Internal").ap()
        g.rows = sb("rows", [1, 2 * TA], I32)
        g.outdeg, g.deg = sb("outdeg", [P, NW]), sb("deg", [P, NW])
        g.count = sb("count", [P, NW * RELS])
        g.rows_d = nc.dram_tensor("rows_d", (1, 2 * TA), I32, kind="Internal").ap()
        g.keys_d = nc.dram_tensor("keys_d", (P + T * P + P,), F32, kind="Internal").ap()
        g.node_d = nc.dram_tensor("node_d", (NP, D), F32, kind="Internal").ap()
        g.pair_d = nc.dram_tensor("pair_d", (NP, 2 * D), F32, kind="Internal").ap()
        g.spill_d = nc.dram_tensor("spill_d", (T * P, D), F32, kind="Internal").ap()
        g.t1_d, g.t2_d, g.t3_d = (nc.dram_tensor(f"t{k}_d", (T * P * RELS,), F32, kind="Internal").ap()
                                  for k in (1, 2, 3))
        g.msg1_d = nc.dram_tensor("msg1_d", (NP, RELS * HID), F32, kind="Internal").ap()
        g.msg2_d = nc.dram_tensor("msg2_d", (NP, RELS * D), F32, kind="Internal").ap()
        constants(nc, g, sem)
        ld = sem("x_ld")
        with nc.Block() as block:
            @block.vector
            def _(dve):
                nc.vector.memset(g.x[:, LASTW * D:], 0.0).then_inc(ld, 16)

            @block.sync
            def _(sp):
                sp.dma_start(g.x[:, 0:LASTW * D].rearrange("p (w f) -> p w f", f=D),
                             a["x"][0:LASTW * P, :].rearrange("(w p) f -> p w f", p=P)).then_inc(ld, 16)
                sp.wait_ge(ld, 32)
                sp.dma_start(g.x[0:REST, LASTW * D:(LASTW + 1) * D], a["x"][LASTW * P:N, :]).then_inc(ld, 16)
                sp.wait_ge(ld, 48)
        sort_edges(nc, g, sem, a["src"], a["dst"], a["edge_type_8"], a["edge_attr_128"])
        sem.give_back()
        tile_tables(nc, g, sem, a["dst"])
        out_degrees(nc, g, sem, a["src"])
        layer_norm(nc, g, sem, "ln0")
        layer0(nc, g, sem, a)
        sem.give_back()
        layer_norm(nc, g, sem, "ln1")
        layer1(nc, g, sem, a)
        sem.give_back()
        layer_norm(nc, g, sem, "ln2")
        layer2(nc, g, sem, a)
        sem.give_back()
        layer_norm(nc, g, sem, "ln3")
        layer3(nc, g, sem, a)
        done = sem("out_done")
        with nc.Block() as block:
            @block.sync
            def _(sp):
                sp.dma_start(out[0:LASTW * P, :].rearrange("(w p) f -> p w f", p=P),
                             g.x[:, 0:LASTW * D].rearrange("p (w f) -> p w f", f=D)).then_inc(done, 16)
                sp.dma_start(out[LASTW * P:N, :], g.x[0:REST, LASTW * D:(LASTW + 1) * D]).then_inc(done, 16)
                sp.wait_ge(done, 32)


_INS = ["x", "src", "dst", "edge_attr_128", "edge_type_8", "L0_gnn_W", "L0_gnn_b", "L0_gnn_We", "L0_gnn_be", "L1_gnn_q_w", "L1_gnn_q_b", "L1_gnn_k_w", "L1_gnn_v_w", "L1_gnn_out_w", "L1_gnn_out_b", "L1_gnn_g1", "L1_gnn_b1", "L1_gnn_lin1_w", "L1_gnn_lin1_b", "L1_gnn_lin2_w", "L1_gnn_lin2_b", "L1_gnn_g2", "L1_gnn_b2", "L2_gnn_W1", "L2_gnn_root1", "L2_gnn_b1", "L2_gnn_W2", "L2_gnn_root2", "L2_gnn_b2", "L3_gnn_Wq", "L3_gnn_bq", "L3_gnn_Wk", "L3_gnn_bk", "L3_gnn_Wv", "L3_gnn_bv", "L3_gnn_Wskip", "L3_gnn_bskip", "L3_gnn_Wgate", "L3_gnn_Wfuse"]


def kernel(**inputs):
    import numpy as _np
    import concourse.bacc as _bacc
    from concourse import mybir as _mybir
    from concourse.bass_utils import run_bass_kernel_spmd as _run

    nc = _bacc.Bacc("TRN2", target_bir_lowering=False, num_devices=1)
    arrays, args = {}, {}
    for name in _INS:
        a = _np.ascontiguousarray(inputs[name])
        arrays[f"in_{name}_dram"] = a
        args[name] = nc.dram_tensor(f"in_{name}_dram", a.shape, _mybir.dt.from_np(a.dtype), kind="ExternalInput").ap()
    out = nc.dram_tensor("out_0_dram", (N, D), F32, kind="ExternalOutput").ap()
    gnn_stack(nc, args, out)
    r = _run(nc, [arrays], core_ids=[0])
    return r.results[0]["out_0_dram"]
```
